# Optimizing a Trainium2 kernel written in Bass

```python
import numpy as np
import jax
import jax.numpy as jnp

def _softmax(x, axis=-1):
    return jax.nn.softmax(x, axis=axis)

def _gelu(x):
    return jax.nn.gelu(x, approximate=True)

def _silu(x):
    return jax.nn.silu(x)

def _sigmoid(x):
    return jax.nn.sigmoid(x)

def _layernorm(x, axis=-1, eps=1e-05):
    m = jnp.mean(x, axis=axis, keepdims=True)
    v = jnp.var(x, axis=axis, keepdims=True)
    return (x - m) / jnp.sqrt(v + eps)

def _scatter_add(tgt, idx, src, axis=0):
    return tgt.at[idx].add(src)

def _segment_sum(src, seg, n):
    return jax.ops.segment_sum(src, seg, n)
kernel_name = 'mk_gnn_ffn_d1_gnn_r8_aea9fb'

def setup_inputs(seed: int=0):
    np.random.seed(seed)
    _w = jnp.asarray

    def _rec_inputs():
        import jax
        import jax.numpy as jnp
        _gk = jax.random.key(seed)
        x = -0.0003713 + 1 * jax.random.normal(jax.random.fold_in(_gk, 1), (6250, 256), jnp.float32)
        _s = jax.random.randint(jax.random.fold_in(_gk, 2), (50000,), 0, 6250, jnp.int32)
        _d = jax.random.randint(jax.random.fold_in(_gk, 3), (50000,), 0, 6250, jnp.int32)
        _loop = jnp.arange(6250, dtype=jnp.int32)
        src = jnp.concatenate([_s, _d, _loop])
        dst = jnp.concatenate([_d, _s, _loop])
        _o = jnp.argsort(dst, stable=True)
        src = src[_o]
        dst = dst[_o]
        edge_type_8 = jax.random.randint(jax.random.fold_in(_gk, 12), (106250,), 0, 8, jnp.int32)
        edge_weight1 = jax.random.uniform(jax.random.fold_in(_gk, 13), (106250, 1), jnp.float32, 0.0, 1)
        return (x, src, dst, edge_type_8, edge_weight1)
    x, src, dst, edge_type_8, edge_weight1 = _rec_inputs()

    def _L0_gnn_setup():
        import jax, jax.numpy as jnp
        import numpy as np
        N_NODES = 6250
        N_EDGES = 100000
        IN_FEAT = 256
        OUT_FEAT = 256
        NUM_RELS = 8
        NUM_BASES = 4
        key = jax.random.key(seed)
        ks = jax.random.split(key, 8)
        feat = jax.random.normal(ks[0], (N_NODES, IN_FEAT), dtype=jnp.float32)
        norm = jax.random.uniform(ks[1], (N_EDGES, 1), dtype=jnp.float32)
        src = jax.random.randint(ks[2], (N_EDGES,), 0, N_NODES)
        dst = jax.random.randint(ks[3], (N_EDGES,), 0, N_NODES)
        etypes = jax.random.randint(ks[4], (N_EDGES,), 0, NUM_RELS)
        weight = jax.random.normal(ks[5], (NUM_BASES, IN_FEAT, OUT_FEAT), dtype=jnp.float32) * (2.0 / np.sqrt(IN_FEAT + OUT_FEAT))
        w_comp = jax.random.normal(ks[6], (NUM_RELS, NUM_BASES), dtype=jnp.float32) * (2.0 / np.sqrt(NUM_RELS + NUM_BASES))
        loop_weight = jax.random.normal(ks[7], (IN_FEAT, OUT_FEAT), dtype=jnp.float32) * (2.0 / np.sqrt(IN_FEAT + OUT_FEAT))
        h_bias = jnp.zeros((OUT_FEAT,), dtype=jnp.float32)
        return {'feat': feat, 'weight': weight, 'w_comp': w_comp, 'loop_weight': loop_weight, 'h_bias': h_bias, 'norm': norm, 'src': src, 'dst': dst, 'etypes': etypes}
    _L0_gnn_all = _L0_gnn_setup()
    _L0_gnn_in = {k: v for k, v in _L0_gnn_all.items() if k in ('weight', 'w_comp', 'loop_weight', 'h_bias')}
    del _L0_gnn_all

    def _L0_ffn_setup():
        import jax, jax.numpy as jnp
        import numpy as np
        B, S, H, F, E, K = (8, 512, 256, 512, 16, 2)
        EPS = 1e-05
        key = jax.random.key(seed)
        ks = jax.random.split(key, 9)
        sc = 0.02
        return {'x': jax.random.normal(ks[0], (B, S, H), dtype=jnp.float32), 'gate_w': jax.random.normal(ks[1], (H, E), dtype=jnp.float32) * sc, 'gate_b': jnp.zeros((E,), dtype=jnp.float32), 'w1': jax.random.normal(ks[2], (E, H, F), dtype=jnp.float32) * sc, 'b1': jnp.zeros((E, F), dtype=jnp.float32), 'w2': jax.random.normal(ks[3], (E, F, H), dtype=jnp.float32) * sc, 'b2': jnp.zeros((E, H), dtype=jnp.float32), 'gamma': jnp.ones((H,), dtype=jnp.float32), 'beta': jnp.zeros((H,), dtype=jnp.float32)}
    _L0_ffn_all = _L0_ffn_setup()
    _L0_ffn_in = {k: v for k, v in _L0_ffn_all.items() if k in ('gate_w', 'gate_b', 'w1', 'b1', 'w2', 'b2', 'gamma', 'beta')}
    del _L0_ffn_all
    return {'x': x, 'src': src, 'dst': dst, 'edge_type_8': edge_type_8, 'edge_weight1': edge_weight1, 'L0_gnn_weight': _L0_gnn_in['weight'], 'L0_gnn_w_comp': _L0_gnn_in['w_comp'], 'L0_gnn_loop_weight': _L0_gnn_in['loop_weight'], 'L0_gnn_h_bias': _L0_gnn_in['h_bias'], 'L0_ffn_gate_w': _L0_ffn_in['gate_w'], 'L0_ffn_gate_b': _L0_ffn_in['gate_b'], 'L0_ffn_w1': _L0_ffn_in['w1'], 'L0_ffn_b1': _L0_ffn_in['b1'], 'L0_ffn_w2': _L0_ffn_in['w2'], 'L0_ffn_b2': _L0_ffn_in['b2'], 'L0_ffn_gamma': _L0_ffn_in['gamma'], 'L0_ffn_beta': _L0_ffn_in['beta']}

def reference(x, src, dst, edge_type_8, edge_weight1, L0_gnn_weight, L0_gnn_w_comp, L0_gnn_loop_weight, L0_gnn_h_bias, L0_ffn_gate_w, L0_ffn_gate_b, L0_ffn_w1, L0_ffn_b1, L0_ffn_w2, L0_ffn_b2, L0_ffn_gamma, L0_ffn_beta):
    import jax
    import jax.numpy as jnp

    def _L0_gnn_ref(feat, weight, w_comp, loop_weight, h_bias, norm, src, dst, etypes):
        import jax, jax.numpy as jnp
        import numpy as np
        N_NODES = 6250
        N_EDGES = 100000
        IN_FEAT = 256
        OUT_FEAT = 256
        NUM_RELS = 8
        NUM_BASES = 4
        W = jnp.einsum('rb,bio->rio', w_comp, weight)
        Hr = jnp.einsum('ni,rio->nro', feat, W)
        msg = Hr[src, etypes] * norm
        agg = jax.ops.segment_sum(msg, dst, num_segments=N_NODES)
        out = agg + feat @ loop_weight + h_bias
        return jax.nn.relu(out)

    def _L0_ffn_ref(x, gate_w, gate_b, w1, b1, w2, b2, gamma, beta):
        import jax, jax.numpy as jnp
        import numpy as np
        B, S, H, F, E, K = (8, 512, 256, 512, 16, 2)
        EPS = 1e-05
        gate_logits = x @ gate_w + gate_b
        topk_vals, topk_idx = jax.lax.top_k(gate_logits, K)
        topk_w = jax.nn.softmax(topk_vals, axis=-1)
        h = jax.nn.relu(jnp.einsum('bsh,ehf->bsef', x, w1) + b1)
        expert_out = jnp.einsum('bsef,efh->bseh', h, w2) + b2
        sel = jnp.take_along_axis(expert_out, topk_idx[:, :, :, None], axis=2)
        moe = jnp.sum(topk_w[..., None] * sel, axis=2)
        y = x + moe
        mu = jnp.mean(y, axis=-1, keepdims=True)
        var = jnp.var(y, axis=-1, keepdims=True)
        return (y - mu) / jnp.sqrt(var + EPS) * gamma + beta
    x = x + _L0_gnn_ref(_layernorm(x, axis=-1), L0_gnn_weight, L0_gnn_w_comp, L0_gnn_loop_weight, L0_gnn_h_bias, edge_weight1, src, dst, edge_type_8)
    x = x + _L0_ffn_ref(_layernorm(x, axis=-1)[None], L0_ffn_gate_w, L0_ffn_gate_b, L0_ffn_w1, L0_ffn_b1, L0_ffn_w2, L0_ffn_b2, L0_ffn_gamma, L0_ffn_beta)[0]
    return x

_drawn_inputs = setup_inputs


def setup_inputs(seed=0):
    import zlib

    import numpy as np

    out = dict(_drawn_inputs(seed))
    spreads = {'L0_gnn_h_bias': (0.0, 0.333),
     'L0_ffn_gate_b': (0.0, 0.479),
     'L0_ffn_b1': (0.0, 0.8),
     'L0_ffn_b2': (0.0, 0.452),
     'L0_ffn_gamma': (1.0, 0.2),
     'L0_ffn_beta': (0.0, 0.336)}
    factors = {'L0_ffn_w1': 3.799, 'L0_ffn_w2': 3.033}
    for name, (base, spread) in spreads.items():
        noise = np.random.default_rng([zlib.crc32(name.encode()), seed]).standard_normal(out[name].shape)
        drawn = base * np.exp(spread * noise) if base else spread * noise
        out[name] = jnp.asarray(drawn.astype(out[name].dtype))
    for name, factor in factors.items():
        out[name] = (out[name] * factor).astype(out[name].dtype)
    return out
```

```python
from contextlib import ExitStack

import concourse.bass as bass
from concourse import mybir

F32 = mybir.dt.float32
I32 = mybir.dt.int32
U32 = mybir.dt.uint32
ALU = mybir.AluOpType
ACT = mybir.ActivationFunctionType
AX = mybir.AxisListType

N_NODES = 6250
N_EDGES = 106250
D = 256
RELS = 8
BASES = 4
EXPERTS = 16
FF = 512
EPS = 1e-5
P = 128

TILE = 125
TILES = N_NODES // TILE
assert TILE * TILES == N_NODES

EDGE_COLS = 832
EDGES_PAD = P * EDGE_COLS
LAST_COLS = N_EDGES - (P - 1) * EDGE_COLS
BLOCK = 32
BLOCKS = EDGE_COLS // BLOCK
CHUNKS = 2
ROUND = CHUNKS * P
META_ROWS = EDGES_PAD + ROUND * 8
NO_NODE = N_NODES + TILE - 1
BIG = float(P * BLOCKS)
PHASES = 4
SEGMENTS = [2, 1, 1, 1, 1]
MIN_ROUNDS = sum(SEGMENTS) + 1
MAX_ROUNDS = EDGES_PAD // ROUND + MIN_ROUNDS

CAP = (-(-N_NODES // P) + 1) * P
REGIONS = EXPERTS * CAP
RING = 3
MOE_TILES = -(-((2 * N_NODES + EXPERTS * (P - 1)) // P) // RING) * RING
W_COLS = 2 * FF + 4 * D + 4


def build(nc, x, src, dst, etype, eweight, basis, comp, loop_w, h_bias, gate_w, gate_b, w_cat, b2,
          gamma, beta, out):
    ctx = ExitStack()
    with ctx:
        def sb(name, shape, dt=F32):
            return ctx.enter_context(nc.sbuf_tensor(name, shape, dt))

        def sem(name):
            return ctx.enter_context(nc.semaphore(name))

        def dram(name, shape, dt=F32):
            return nc.dram_tensor(name, shape, dt).ap()

        meta_d = dram("meta_d", (META_ROWS, 3), I32)
        h_d = dram("h_d", (N_NODES * RELS, D))
        xnT_d = dram("xnT_d", (TILES * P, 2 * TILE))
        pair_d = dram("pair_d", (N_NODES, 2 * D))
        disp_d = dram("disp_d", (REGIONS + P, D))
        moe_d = dram("moe_d", (MOE_TILES * P, D))

        ident = sb("ident", [P, P])
        ones = sb("ones", [P, P])
        row0 = sb("row0", [P, P])
        before = sb("before", [P, P])
        zeros = sb("zeros", [P, D])
        iota_n = sb("iota_n", [P, TILE])
        iota_e = sb("iota_e", [P, EXPERTS])
        region = sb("region", [P, EXPERTS])
        hb = sb("hb", [P, D])
        gb = sb("gb", [P, EXPERTS])
        gw = sb("gw", [P, 2, EXPERTS])
        lw = sb("lw", [P, 2, D])
        eps = sb("eps", [P, 1])
        gam = sb("gam", [P, D])
        bet = sb("bet", [P, D])

        src_i = sb("src_i", [P, EDGE_COLS], I32)
        dst_i = sb("dst_i", [P, EDGE_COLS], I32)
        et_i = sb("et_i", [P, EDGE_COLS], I32)
        nrm = sb("nrm", [P, EDGE_COLS])
        meta = sb("meta", [P, EDGE_COLS, 3], I32)
        tail_meta = sb("tail_meta", [P, (META_ROWS - EDGES_PAD) // P, 3], I32)
        meta_f = meta[:, :, :].bitcast(F32)
        bmin = sb("bmin", [P, BLOCKS])
        bmax = sb("bmax", [P, BLOCKS])
        bid = sb("bid", [P, BLOCKS])
        bidr = sb("bidr", [P, BLOCKS])
        tlo = sb("tlo", [P, TILES])
        candA = sb("candA", [P, TILES, BLOCKS])
        candB = sb("candB", [P, TILES, BLOCKS])
        ends = sb("ends", [P, 2 * TILES])
        ends1 = sb("ends1", [2 * TILES, 1])
        er = sb("er", [1, 2 * TILES])
        has = sb("has", [1, TILES])
        fst = sb("fst", [1, TILES])
        rnf = sb("rnf", [1, TILES])
        rni = sb("rni", [1, TILES], I32)
        start_t = sb("start_t", [1, TILES], I32)
        rounds_t = sb("rounds_t", [1, TILES], I32)

        comp_s = sb("comp_s", [P, RELS * BASES])
        bas = sb("bas", [P, BASES, 2, D])
        w_rel = sb("w_rel", [P, 2, RELS, D])
        xin = [sb(f"xin{i}", [TILE, D]) for i in range(2)]
        st = [sb(f"st{i}", [TILE, 6]) for i in range(2)]
        mv = [sb(f"mv{i}", [TILE, 2]) for i in range(2)]
        sd = [sb(f"sd{i}", [TILE, 1]) for i in range(2)]
        rs = [sb(f"rs{i}", [TILE, 1]) for i in range(2)]
        xn = [sb(f"xn{i}", [TILE, D]) for i in range(2)]
        xnT = [sb(f"xnT{i}", [P, 2, TILE]) for i in range(2)]
        hr = [sb(f"hr{i}", [TILE, RELS * D]) for i in range(2)]

        m_s = [sb(f"m_s{q}", [P, CHUNKS * 3], I32) for q in range(PHASES)]
        m_f = [t[:, :].bitcast(F32) for t in m_s]
        rows = [[sb(f"rows{q}_{c}", [P, D]) for c in range(CHUNKS)] for q in range(PHASES)]
        hot = [sb(f"hot{q}", [P, CHUNKS, TILE]) for q in range(PHASES)]
        x_c = sb("x_c", [TILE, D])
        xT_c = sb("xT_c", [P, 2 * TILE])
        pair = sb("pair", [TILE, 2, D])
        st_c = sb("st_c", [TILE, 6])
        mv_c = sb("mv_c", [TILE, 2])
        sd_c = sb("sd_c", [TILE, 1])
        rs_c = sb("rs_c", [TILE, 1])
        send = sb("send", [TILE, D])
        xn2T = sb("xn2T", [P, 2, TILE])
        lg = sb("lg", [TILE, EXPERTS])
        top = sb("top", [TILE, 8])
        topi = sb("topi", [TILE, 8], U32)
        topf = sb("topf", [TILE, 2])
        oh = sb("oh", [TILE, 2, EXPERTS])
        both = sb("both", [P, EXPERTS])
        seen = sb("seen", [P, EXPERTS])
        slf = sb("slf", [TILE, EXPERTS])
        slx = sb("slx", [TILE, 2, EXPERTS])
        slot_f = sb("slot_f", [TILE, 2])
        slots = sb("slots", [TILE, 2], I32)
        slot_all = sb("slot_all", [TILE, 2 * TILES])
        expert_all = sb("expert_all", [TILE, 2 * TILES])
        moe_row = sb("moe_row", [TILE, 2 * TILES], I32)
        shifted = [sb(f"shifted{i}", [TILE, 2 * TILES]) for i in range(2)]
        shift = sb("shift", [TILE, EXPERTS])
        shift0 = sb("shift0", [TILE, EXPERTS])
        gap = sb("gap", [TILE, TILES])

        cnt = sb("cnt", [TILE, EXPERTS])
        cnt_i = sb("cnt_i", [TILE, EXPERTS], I32)
        padr_i = sb("padr_i", [TILE, EXPERTS], I32)
        nt_i = sb("nt_i", [TILE, EXPERTS], I32)
        nt_f = sb("nt_f", [TILE, EXPERTS])
        cum = sb("cum", [TILE, EXPERTS])
        step = sb("step", [TILE, EXPERTS])
        iota_m = sb("iota_m", [1, MOE_TILES])
        past = sb("past", [1, MOE_TILES, EXPERTS])
        past2 = sb("past2", [1, MOE_TILES, EXPERTS])
        e_f = sb("e_f", [1, MOE_TILES])
        r_f = sb("r_f", [1, MOE_TILES])
        new_f = sb("new_f", [1, MOE_TILES])
        e_t = sb("e_t", [1, MOE_TILES], I32)
        row_t = sb("row_t", [1, MOE_TILES], I32)
        new_t = sb("new_t", [1, MOE_TILES], I32)
        xd = [sb(f"xd{i}", [P, D]) for i in range(RING)]
        xdT = [sb(f"xdT{i}", [P, 2, P]) for i in range(RING)]
        w_s = [sb(f"w_s{i}", [P, W_COLS]) for i in range(RING)]
        b2_s = [sb(f"b2_s{i}", [P, D]) for i in range(RING)]
        hT = [sb(f"hT{i}", [P, 4, P]) for i in range(RING)]
        yo = [sb(f"yo{i}", [P, D]) for i in range(RING)]

        wt = sb("wt", [TILE, 2, TILES])
        wden = sb("wden", [TILE, TILES])
        sl_e = [sb(f"sl_e{i}", [TILE, 2], I32) for i in range(2)]
        y_e = [[sb(f"y_e{i}_{k}", [TILE, D]) for k in range(2)] for i in range(2)]
        pr_e = [sb(f"pr_e{i}", [TILE, 2, D]) for i in range(2)]
        acc_e = [sb(f"acc_e{i}", [TILE, D]) for i in range(2)]
        o_e = [sb(f"o_e{i}", [TILE, D]) for i in range(2)]
        st_e = [sb(f"st_e{i}", [TILE, 6]) for i in range(2)]
        mv_e = [sb(f"mv_e{i}", [TILE, 2]) for i in range(2)]
        sd_e = [sb(f"sd_e{i}", [TILE, 1]) for i in range(2)]
        rs_e = [sb(f"rs_e{i}", [TILE, 1]) for i in range(2)]

        bank = [ctx.enter_context(nc.psum_tensor(f"bank{i}", [P, 512], F32)) for i in range(8)]
        agg = bank[0]
        x2T_p, lg_p, rank_p, y_p, xdT_p = bank[1], bank[2], bank[2], bank[3], bank[4]
        h_p = bank[5:8]

        const_loaded = sem("const_loaded")
        edges_loaded = sem("edges_loaded")
        basis_loaded = sem("basis_loaded")
        pool_const = sem("pool_const")
        pads_set = sem("pads_set")
        zeros_set = sem("zeros_set")
        meta_built = sem("meta_built")
        nrm_copied = sem("nrm_copied")
        meta_stored = sem("meta_stored")
        zero_rows = sem("zero_rows")
        ends_ready = sem("ends_ready")
        ends_turned = sem("ends_turned")
        ends_max = sem("ends_max")
        ends_back = sem("ends_back")
        ranges_ready = sem("ranges_ready")
        w_ready = sem("w_ready")
        x_loaded = [sem(f"x_loaded{i}") for i in range(2)]
        var_ready = sem("var_ready")
        std_ready = sem("std_ready")
        xn_ready = sem("xn_ready")
        xnT_done = sem("xnT_done")
        xnT_ready = sem("xnT_ready")
        h_done = sem("h_done")
        h_out_act = sem("h_out_act")
        h_out_dve = sem("h_out_dve")
        h_stored = [sem(f"h_stored{i}") for i in range(2)]
        xnT_stored = [sem(f"xnT_stored{i}") for i in range(2)]
        table_ready = sem("table_ready")

        meta_loaded = [sem(f"meta_loaded{q}") for q in range(PHASES)]
        gathered = [[sem(f"gathered{q}_{c}") for c in range(CHUNKS)] for q in range(PHASES)]
        hot_ready = [sem(f"hot_ready{q}") for q in range(PHASES)]
        phase_free = [sem(f"phase_free{q}") for q in range(PHASES)]
        xc_loaded = sem("xc_loaded")
        xTc_loaded = sem("xTc_loaded")
        agg_open = sem("agg_open")
        agg_done = sem("agg_done")
        agg_read = sem("agg_read")
        var2_ready = sem("var2_ready")
        std2_ready = sem("std2_ready")
        xn2_ready = sem("xn2_ready")
        x2T_done = sem("x2T_done")
        send_ready = sem("send_ready")
        x2T_ready = sem("x2T_ready")
        pair_stored = sem("pair_stored")
        logits_done = sem("logits_done")
        both_ready = sem("both_ready")
        rank_done = sem("rank_done")
        slots_ready = sem("slots_ready")
        sent = [sem(f"sent{k}") for k in range(2)]

        count_done = sem("count_done")
        moe_table = sem("moe_table")
        gaps_zeroed = sem("gaps_zeroed")
        xd_loaded = [sem(f"xd_loaded{i}") for i in range(RING)]
        w_loaded = [sem(f"w_loaded{i}") for i in range(RING)]
        xdT_done = sem("xdT_done")
        xdT_ready = sem("xdT_ready")
        mm1_done = sem("mm1_done")
        hT_ready = sem("hT_ready")
        mm2_done = sem("mm2_done")
        yo_ready = sem("yo_ready")
        yo_stored = [sem(f"yo_stored{i}") for i in range(RING)]
        moe_stored = sem("moe_stored")

        exp_done = sem("exp_done")
        gap_ready = sem("gap_ready")
        sl_ready = sem("sl_ready")
        y_loaded = [[sem(f"y_loaded{i}_{k}") for k in range(2)] for i in range(2)]
        pr_loaded = [sem(f"pr_loaded{i}") for i in range(2)]
        acc_used = sem("acc_used")
        var3_ready = sem("var3_ready")
        std3_ready = sem("std3_ready")
        o_ready = sem("o_ready")
        o_stored = [sem(f"o_stored{i}") for i in range(2)]

        block = ctx.enter_context(nc.Block())

        def by_phase(eng, counter, body):
            r = eng.snap(counter, min_val=0, max_val=TILES * MAX_ROUNDS)
            u1 = eng.snap((r >> 2) + 1, min_val=1, max_val=TILES * MAX_ROUNDS)
            q = r & 3
            with eng.If(q < 2):
                with eng.If(q == 0):
                    body(0, u1)
                with eng.Else():
                    body(1, u1)
                eng.nop()
            with eng.Else():
                with eng.If(q == 2):
                    body(2, u1)
                with eng.Else():
                    body(3, u1)
                eng.nop()
            eng.reg_add(counter, counter, 1)

        def tile_rounds(eng, counter, t, body, between, before_round=None):
            n = eng.value_load(rounds_t[0:1, bass.ds(t, 1)], min_val=MIN_ROUNDS, max_val=MAX_ROUNDS)
            for s, k in enumerate(SEGMENTS):
                with eng.Fori(0, k):
                    by_phase(eng, counter, body)
                between(s)
            with eng.Fori(sum(SEGMENTS), n):
                by_phase(eng, counter, body)

        @block.sync
        def _(sp):
            for dst_t, src_t in ((src_i, src), (dst_i, dst), (et_i, etype), (nrm, eweight)):
                if dst_t is src_i:
                    sp.wait_ge(pads_set, 4)
                sp.dma_start(dst_t[0:P - 1, :], src_t[0:(P - 1) * EDGE_COLS].rearrange("(p c) -> p c", p=P - 1)
                             ).then_inc(edges_loaded, 16)
                sp.dma_start(dst_t[P - 1:P, 0:LAST_COLS],
                             src_t[(P - 1) * EDGE_COLS:N_EDGES].rearrange("(p c) -> p c", p=1)
                             ).then_inc(edges_loaded, 16)
            sp.dma_start(bas[:, :, :, :].rearrange("p b k o -> p (b k) o"),
                         basis.rearrange("b (k p) o -> p (b k) o", p=P)).then_inc(basis_loaded, 16)
            sp.dma_start(comp_s[:, :], comp.rearrange("(a r) b -> a (r b)", a=1).to_broadcast([P, RELS * BASES])
                         ).then_inc(basis_loaded, 16)
            sp.wait_ge(zeros_set, 1)
            sp.dma_start(hb[0:1, :], h_bias.rearrange("(a o) -> a o", a=1)).then_inc(const_loaded, 16)
            sp.dma_start(gb[0:1, :], gate_b.rearrange("(a o) -> a o", a=1)).then_inc(const_loaded, 16)
            sp.dma_start(gw[:, :, :], gate_w.rearrange("(k p) e -> p k e", p=P)).then_inc(const_loaded, 16)
            sp.dma_start(lw[:, :, :], loop_w.rearrange("(k p) o -> p k o", p=P)).then_inc(const_loaded, 16)
            sp.dma_start(gam[:, :], gamma.rearrange("(a o) -> a o", a=1).to_broadcast([P, D])).then_inc(const_loaded, 16)
            sp.dma_start(bet[:, :], beta.rearrange("(a o) -> a o", a=1).to_broadcast([P, D])).then_inc(const_loaded, 16)

            def load_x(t, i):
                sp.dma_start(xin[i][:, :], x[bass.ds(t * TILE, TILE), :]).then_inc(x_loaded[i], 16)

            def store_h(t, i):
                sp.wait_ge(xnT_ready, t + 1)
                sp.dma_start(xnT_d[bass.ds(t * P, P), :], xnT[i][:, :, :].rearrange("p k n -> p (k n)")
                             ).then_inc(xnT_stored[i], 16)
                sp.wait_ge(h_out_act, 2 * t + 2)
                sp.wait_ge(h_out_dve, 2 * t + 2)
                sp.dma_start(h_d[bass.ds(t * TILE * RELS, TILE * RELS), :].rearrange("(n r) o -> n (r o)", r=RELS),
                             hr[i][:, :]).then_inc(h_stored[i], 16)

            load_x(0, 0)
            load_x(1, 1)
            sp.wait_ge(meta_built, 1)
            sp.wait_ge(nrm_copied, 1)
            sp.dma_start(meta_d[0:EDGES_PAD, :].rearrange("(p c) f -> p (c f)", p=P),
                         meta[:, :, :].rearrange("p c f -> p (c f)")).then_inc(meta_stored, 16)
            sp.dma_start(meta_d[EDGES_PAD:META_ROWS, :].rearrange("(p c) f -> p (c f)", p=P),
                         tail_meta[:, :, :].rearrange("p c f -> p (c f)")).then_inc(meta_stored, 16)
            sp.dma_start(disp_d[REGIONS:REGIONS + P, :], zeros[:, :]).then_inc(zero_rows, 16)
            with sp.Fori(0, TILES // 2 - 1) as m:
                for i in range(2):
                    t = 2 * m + i
                    store_h(t, i)
                    sp.wait_ge(xn_ready, t + 1)
                    load_x(t + 2, i)
            for i in range(2):
                store_h(TILES - 2 + i, i)

            for i in range(2):
                sp.wait_ge(xnT_stored[i], 16 * (TILES // 2))
                sp.wait_ge(h_stored[i], 16 * (TILES // 2))
            sp.wait_ge(meta_stored, 32)
            sp.wait_ge(zero_rows, 16)
            sp.nop(nofuse=True).then_inc(table_ready, 1)
            sp.wait_ge(ranges_ready, 1)
            rnd = sp.alloc_register("rnd_sp")
            edge = sp.alloc_register("edge_sp")
            sp.reg_mov(rnd, 0)

            def load_meta(q, u1):
                e0 = sp.snap(edge, min_val=0, max_val=META_ROWS - ROUND)
                sp.wait_ge(phase_free[q], u1)
                sp.dma_start(m_s[q][:, :], meta_d[bass.ds(e0, ROUND), :].rearrange("(p c) f -> p (c f)", p=P)
                             ).then_inc(meta_loaded[q], 16)
                sp.reg_add(edge, edge, ROUND)

            def store_pair(t):
                sp.wait_ge(xn2_ready, t + 1)
                sp.dma_start(pair_d[bass.ds(t * TILE, TILE), :], pair[:, :, :].rearrange("n a o -> n (a o)")
                             ).then_inc(pair_stored, 16)

            def load_tile(t):
                sp.dma_start(x_c[:, :], x[bass.ds(t * TILE, TILE), :]).then_inc(xc_loaded, 16)
                sp.dma_start(xT_c[:, :], xnT_d[bass.ds(t * P, P), :]).then_inc(xTc_loaded, 16)

            def sp_tile(t, first):
                e = sp.value_load(start_t[0:1, bass.ds(t, 1)], min_val=0, max_val=EDGES_PAD)
                sp.reg_mov(edge, e)

                def between(s):
                    if s == 2 and not first:
                        store_pair(t - 1)
                        sp.dma_start(x_c[:, :], x[bass.ds(t * TILE, TILE), :]).then_inc(xc_loaded, 16)
                    if s == 3 and not first:
                        pass

                tile_rounds(sp, rnd, t, load_meta, between)

            sp.dma_start(x_c[:, :], x[0:TILE, :]).then_inc(xc_loaded, 16)
            sp.dma_start(xT_c[:, :], xnT_d[0:P, :]).then_inc(xTc_loaded, 16)
            sp_tile(0, True)
            with sp.Fori(1, TILES) as t:
                sp.wait_ge(agg_open, t)
                sp.dma_start(xT_c[:, :], xnT_d[bass.ds(t * P, P), :]).then_inc(xTc_loaded, 16)
                sp_tile(t, False)
            store_pair(TILES - 1)

            sp.wait_ge(moe_table, 1)
            for k in range(2):
                sp.wait_ge(sent[k], 16 * TILES)
            with sp.Fori(0, EXPERTS) as e:
                r = sp.value_load(padr_i[0:1, bass.ds(e, 1)], min_val=0, max_val=REGIONS - P)
                sp.dma_start(disp_d[bass.ds(r, P), :], zeros[:, :]).then_inc(gaps_zeroed, 16)
            sp.wait_ge(gaps_zeroed, 16 * EXPERTS)

            def load_expert(i, k, warm):
                r = sp.value_load(row_t[0:1, bass.ds(i, 1)], min_val=0, max_val=REGIONS)
                e = sp.value_load(e_t[0:1, bass.ds(i, 1)], min_val=0, max_val=EXPERTS - 1)
                new = sp.value_load(new_t[0:1, bass.ds(i, 1)], min_val=0, max_val=1)
                if warm:
                    sp.wait_ge(xdT_done, i - RING + 1)
                sp.dma_start(xd[k][:, :], disp_d[bass.ds(r, P), :]).then_inc(xd_loaded[k], 16)
                if warm:
                    sp.wait_ge(yo_ready, i - RING + 1)
                sp.dma_start(w_s[k][:, :], w_cat[bass.ds(e * P, P), :], cond=new == 1
                             ).then_inc(w_loaded[k], 16)
                sp.dma_start(b2_s[k][:, :], b2[bass.ds(e, 1), :].to_broadcast([P, D]), cond=new == 1
                             ).then_inc(w_loaded[k], 16)

            def store_expert(i, k):
                sp.wait_ge(yo_ready, i + 1)
                sp.dma_start(moe_d[bass.ds(i * P, P), :], yo[k][:, :]).then_inc(yo_stored[k], 16)

            for i in range(RING):
                load_expert(i, i, False)
            with sp.Fori(0, MOE_TILES // RING - 1) as m:
                for k in range(RING):
                    load_expert(RING * m + RING + k, k, True)
                    store_expert(RING * m + k, k)
            for k in range(RING):
                store_expert(MOE_TILES - RING + k, k)
            for k in range(RING):
                sp.wait_ge(yo_stored[k], 16 * (MOE_TILES // RING))
            sp.wait_ge(pair_stored, 16 * TILES)
            sp.nop(nofuse=True).then_inc(moe_stored, 1)

            def load_pair(t, i):
                sp.dma_start(pr_e[i][:, :, :].rearrange("n a o -> n (a o)"), pair_d[bass.ds(t * TILE, TILE), :]
                             ).then_inc(pr_loaded[i], 16)

            def store_out(t, i):
                sp.wait_ge(o_ready, t + 1)
                sp.dma_start(out[bass.ds(t * TILE, TILE), :], o_e[i][:, :]).then_inc(o_stored[i], 16)

            load_pair(0, 0)
            load_pair(1, 1)
            with sp.Fori(0, TILES // 2 - 1) as m:
                for i in range(2):
                    t = 2 * m + i
                    store_out(t, i)
                    load_pair(t + 2, i)
            for i in range(2):
                store_out(TILES - 2 + i, i)
            for i in range(2):
                sp.wait_ge(o_stored[i], 16 * (TILES // 2))

        @block.gpsimd
        def _(pool):
            nc.gpsimd.memset(ident[:, :], 0.0)
            nc.gpsimd.memset(row0[:, :], 0.0)
            nc.gpsimd.memset(before[:, :], 0.0)
            nc.gpsimd.iota(iota_n[:, :], pattern=[[1, TILE]], base=-TILE, channel_multiplier=0,
                           allow_small_or_imprecise_dtypes=True)
            nc.gpsimd.iota(iota_e[:, :], pattern=[[1, EXPERTS]], base=0, channel_multiplier=0,
                           allow_small_or_imprecise_dtypes=True)
            nc.gpsimd.iota(region[:, :], pattern=[[CAP, EXPERTS]], base=0, channel_multiplier=0,
                           allow_small_or_imprecise_dtypes=True)
            nc.gpsimd.iota(tlo[:, :], pattern=[[TILE, TILES]], base=0, channel_multiplier=0,
                           allow_small_or_imprecise_dtypes=True)
            nc.gpsimd.iota(bid[:, :], pattern=[[1, BLOCKS]], base=1, channel_multiplier=BLOCKS,
                           allow_small_or_imprecise_dtypes=True)
            nc.gpsimd.iota(bidr[:, :], pattern=[[-1, BLOCKS]], base=int(BIG), channel_multiplier=-BLOCKS,
                           allow_small_or_imprecise_dtypes=True)
            nc.gpsimd.iota(iota_m[:, :], pattern=[[1, MOE_TILES]], base=0, channel_multiplier=0,
                           allow_small_or_imprecise_dtypes=True)
            pool.drain()
            nc.gpsimd.affine_select(out=ident[:, :], in_=ident[:, :], compare_op=ALU.not_equal, fill=1.0, base=0,
                                    pattern=[[-1, P]], channel_multiplier=1)
            nc.gpsimd.affine_select(out=before[:, :], in_=before[:, :], compare_op=ALU.is_ge, fill=1.0, base=0,
                                    pattern=[[-1, P]], channel_multiplier=1)
            nc.gpsimd.affine_select(out=row0[:, :], in_=row0[:, :], compare_op=ALU.not_equal, fill=1.0, base=0,
                                    pattern=[[0, P]], channel_multiplier=1)
            pool.drain().then_inc(pool_const, 1)

            pool.wait_ge(table_ready, 1)
            pool.wait_ge(ranges_ready, 1)
            rnd = pool.alloc_register("rnd_pool")
            pool.reg_mov(rnd, 0)

            def gather(q, u1):
                pool.wait_ge(meta_loaded[q], u1 * 16)
                pool.nop(nofuse=True)
                for c in range(CHUNKS):
                    nc.gpsimd.indirect_dma_start(
                        out=rows[q][c][:, :], out_offset=None, in_=h_d,
                        in_offset=bass.IndirectOffsetOnAxis(ap=m_s[q][:, 3 * c:3 * c + 1], axis=0),
                    ).then_inc(gathered[q][c], 16)

            def scatter(t):
                pool.wait_ge(slots_ready, t + 1)
                pool.wait_ge(send_ready, t + 1)
                pool.nop(nofuse=True)
                for k in range(2):
                    nc.gpsimd.indirect_dma_start(
                        out=disp_d, out_offset=bass.IndirectOffsetOnAxis(ap=slots[:, k:k + 1], axis=0),
                        in_=send[:, :], in_offset=None).then_inc(sent[k], 16)

            def pool_tile(t, lag):
                def between(s):
                    if s == 2 and lag:
                        scatter(t - 2)

                tile_rounds(pool, rnd, t, gather, between)

            pool_tile(0, False)
            pool_tile(1, False)
            with pool.Fori(2, TILES) as t:
                pool_tile(t, True)
            scatter(TILES - 2)
            scatter(TILES - 1)

            pool.wait_ge(moe_stored, 1)

            def gather_y(t, i):
                pool.wait_ge(sl_ready, t + 1)
                pool.nop(nofuse=True)
                for k in range(2):
                    nc.gpsimd.indirect_dma_start(
                        out=y_e[i][k][:, :], out_offset=None, in_=moe_d,
                        in_offset=bass.IndirectOffsetOnAxis(ap=sl_e[i][:, k:k + 1], axis=0),
                    ).then_inc(y_loaded[i][k], 16)

            with pool.Fori(0, TILES // 2) as m:
                for i in range(2):
                    gather_y(2 * m + i, i)

        @block.scalar
        def _(act):
            act.wait_ge(edges_loaded, 128)
            nc.scalar.copy(meta_f[:, :, 2], nrm[:, :])
            act.drain().then_inc(nrm_copied, 1)
            act.wait_ge(zeros_set, 1)

            def act_std(t, i):
                act.wait_ge(var_ready, t + 1)
                nc.scalar.activation(sd[i][:, :], mv[i][:, 1:2], ACT.Sqrt, bias=eps[0:TILE, :]).then_inc(std_ready, 1)

            def act_h(t, i, warm):
                act.wait_ge(xnT_done, t + 1)
                if warm:
                    act.wait_ge(xnT_stored[i], (t // 2) * 16)
                nc.scalar.copy(xnT[i][:, :, :].rearrange("p k n -> p (k n)"), bank[4 + i][:, 0:2 * TILE]
                               ).then_inc(xnT_ready, 1)

            def act_out(t, i, warm):
                if warm:
                    act.wait_ge(h_stored[i], (t // 2) * 16)
                for j in (0, 2):
                    act.wait_ge(h_done, 4 * t + j + 1)
                    nc.scalar.copy(hr[i][:, j * 512:(j + 1) * 512], bank[j][0:TILE, :]).then_inc(h_out_act, 1)

            act_std(0, 0)
            act_h(0, 0, False)
            act_std(1, 1)
            act_h(1, 1, False)
            act_out(0, 0, False)
            act_std(2, 0)
            act_h(2, 0, True)
            act_out(1, 1, False)
            with act.Fori(1, TILES // 2 - 1) as m:
                for i in range(2):
                    t = 2 * m + i
                    act_std(t + 1, 1 - i)
                    act_h(t + 1, 1 - i, True)
                    act_out(t, i, True)
            act_std(TILES - 1, 1)
            act_h(TILES - 1, 1, True)
            act_out(TILES - 2, 0, True)
            act_out(TILES - 1, 1, True)

            def act_finish(t, warm):
                act.wait_ge(var2_ready, t + 1)
                nc.scalar.activation(sd_c[:, :], mv_c[:, 1:2], ACT.Sqrt, bias=eps[0:TILE, :]).then_inc(std2_ready, 1)
                act.wait_ge(xn2_ready, t + 1)
                if warm:
                    for k in range(2):
                        act.wait_ge(sent[k], t * 16)
                nc.scalar.copy(send[:, :], pair[:, 1, :]).then_inc(send_ready, 1)
                act.wait_ge(x2T_done, t + 1)
                nc.scalar.copy(xn2T[:, :, :].rearrange("p k n -> p (k n)"), x2T_p[:, 0:2 * TILE]).then_inc(x2T_ready, 1)

            act_finish(0, False)
            with act.Fori(1, TILES) as t:
                act_finish(t, True)

            def act_turn(i, k):
                act.wait_ge(xdT_done, i + 1)
                nc.scalar.copy(xdT[k][:, :, :].rearrange("p k n -> p (k n)"), xdT_p[:, 0:2 * P]).then_inc(xdT_ready, 1)

            def act_relu(i, k):
                act.wait_ge(mm1_done, i + 1)
                for f in range(4):
                    b0 = 2 * FF + 4 * D + f
                    last = nc.scalar.activation(hT[k][:, f, :], h_p[k][:, f * P:(f + 1) * P], ACT.Relu,
                                                bias=w_s[k][:, b0:b0 + 1])
                last.then_inc(hT_ready, 1)

            act_turn(0, 0)
            act_turn(1, 1)
            act_relu(0, 0)
            act_turn(2, 2)
            act_relu(1, 1)
            with act.Fori(1, MOE_TILES // RING) as m:
                for k in range(RING):
                    act_turn(RING * m + k, k)
                    act_relu(RING * m + k - 1, (k - 1) % RING)
            act_relu(MOE_TILES - 1, RING - 1)

            act.wait_ge(gap_ready, 1)
            nc.scalar.activation(wt[:, 1, :], gap[:, :], ACT.Exp).then_inc(exp_done, 1)
            with act.Fori(0, TILES // 2) as m:
                for i in range(2):
                    act.wait_ge(var3_ready, 2 * m + i + 1)
                    nc.scalar.activation(sd_e[i][:, :], mv_e[i][:, 1:2], ACT.Sqrt, bias=eps[0:TILE, :]
                                         ).then_inc(std3_ready, 1)

        @block.vector
        def _(dve):
            v = nc.vector
            v.memset(src_i[96:P, :], 0).then_inc(pads_set, 1)
            v.memset(dst_i[96:P, :], NO_NODE).then_inc(pads_set, 1)
            v.memset(et_i[96:P, :], 0).then_inc(pads_set, 1)
            v.memset(nrm[96:P, :], 0.0).then_inc(pads_set, 1)
            v.memset(ones[:, :], 1.0)
            v.memset(zeros[:, :], 0.0)
            v.memset(hb[:, :], 0.0)
            v.memset(gb[:, :], 0.0)
            v.memset(eps[:, :], EPS)
            v.memset(both[:, :], 0.0)
            v.memset(seen[:, :], 0.0)
            v.memset(tail_meta[:, :, :], 0)
            dve.drain().then_inc(zeros_set, 1)
            v.memset(tail_meta[:, :, :].bitcast(F32)[:, :, 1], float(NO_NODE))

            dve.wait_ge(basis_loaded, 32)
            for b in range(BASES):
                for r in range(RELS):
                    c = comp_s[:, r * BASES + b:r * BASES + b + 1]
                    if b == 0:
                        v.tensor_scalar(w_rel[:, :, r, :], bas[:, b, :, :], c, None, ALU.mult)
                    else:
                        v.scalar_tensor_tensor(w_rel[:, :, r, :], bas[:, b, :, :], c, w_rel[:, :, r, :],
                                               ALU.mult, ALU.add)
                dve.drain()
            dve.drain().then_inc(w_ready, 1)

            dve.wait_ge(edges_loaded, 128)
            v.scalar_tensor_tensor(meta[:, :, 0], src_i[:, :], float(RELS), et_i[:, :], ALU.mult, ALU.add)
            v.tensor_copy(meta_f[:, :, 1], dst_i[:, :])
            dve.drain().then_inc(meta_built, 1)

            def dve_x(t, i):
                dve.wait_ge(x_loaded[i], (t // 2 + 1) * 16)
                v.bn_stats(st[i][:, :], xin[i][:, :])
                dve.drain()
                v.bn_aggr(mv[i][:, :], st[i][:, :]).then_inc(var_ready, 1)

            def dve_xn(t, i):
                dve.wait_ge(std_ready, t + 1)
                v.reciprocal(rs[i][:, :], sd[i][:, :])
                dve.drain()
                v.tensor_scalar(xn[i][:, :], xin[i][:, :], mv[i][:, 0:1], rs[i][:, :], ALU.subtract, ALU.mult
                                ).then_inc(xn_ready, 1)

            def dve_out(t, i, warm):
                if warm:
                    dve.wait_ge(h_stored[i], (t // 2) * 16)
                for j in (1, 3):
                    dve.wait_ge(h_done, 4 * t + j + 1)
                    v.tensor_copy(hr[i][:, j * 512:(j + 1) * 512], bank[j][0:TILE, :]).then_inc(h_out_dve, 1)

            def edge_ranges():
                v.tensor_reduce(bmin[:, :], meta_f[:, :, 1].rearrange("p (b e) -> p b e", e=BLOCK), AX.X, ALU.min)
                v.tensor_reduce(bmax[:, :], meta_f[:, :, 1].rearrange("p (b e) -> p b e", e=BLOCK), AX.X, ALU.max)
                dve.wait_ge(pool_const, 1)
                dve.drain()
                t_b = tlo[:, :].unsqueeze(2).to_broadcast([P, TILES, BLOCKS])
                v.tensor_tensor(candA[:, :, :], bmax[:, :].unsqueeze(1).to_broadcast([P, TILES, BLOCKS]), t_b,
                                ALU.is_ge)
                v.tensor_tensor(candB[:, :, :], bmin[:, :].unsqueeze(1).to_broadcast([P, TILES, BLOCKS]), t_b,
                                ALU.subtract)
                dve.drain()
                v.scalar_tensor_tensor(candA[:, :, :], candB[:, :, :], TILE - 0.5, candA[:, :, :], ALU.is_lt, ALU.mult)
                dve.drain()
                v.tensor_tensor(candB[:, :, :], candA[:, :, :],
                                bidr[:, :].unsqueeze(1).to_broadcast([P, TILES, BLOCKS]), ALU.mult)
                dve.drain()
                v.tensor_reduce(ends[:, 0:TILES], candB[:, :, :], AX.X, ALU.max)
                dve.drain()
                v.tensor_tensor(candB[:, :, :], candA[:, :, :],
                                bid[:, :].unsqueeze(1).to_broadcast([P, TILES, BLOCKS]), ALU.mult)
                dve.drain()
                v.tensor_reduce(ends[:, TILES:2 * TILES], candB[:, :, :], AX.X, ALU.max).then_inc(ends_ready, 1)
                dve.wait_ge(ends_turned, 1)
                v.tensor_reduce(ends1[:, :], bank[6][0:2 * TILES, 0:P], AX.X, ALU.max).then_inc(ends_max, 1)
                dve.wait_ge(ends_back, 1)
                v.tensor_copy(er[:, :], bank[7][0:1, 0:2 * TILES])
                dve.drain()
                v.tensor_scalar(has[:, :], er[:, 0:TILES], 0.5, None, ALU.is_ge)
                v.tensor_scalar(fst[:, :], er[:, 0:TILES], -1.0, BIG, ALU.mult, ALU.add)
                dve.drain()
                v.tensor_tensor(fst[:, :], fst[:, :], has[:, :], ALU.mult)
                dve.drain()
                v.tensor_scalar(start_t[:, :], fst[:, :], float(BLOCK), None, ALU.mult)
                v.tensor_tensor(rnf[:, :], er[:, TILES:2 * TILES], fst[:, :], ALU.subtract)
                dve.drain()
                v.tensor_scalar(rni[:, :], rnf[:, :], float(ROUND // BLOCK - 1), None, ALU.add)
                dve.drain()
                v.tensor_scalar(rni[:, :], rni[:, :], (ROUND // BLOCK).bit_length() - 1, None,
                                ALU.arith_shift_right)
                dve.drain()
                v.tensor_scalar(rounds_t[:, :], rni[:, :], float(MIN_ROUNDS), None, ALU.max)
                dve.drain().then_inc(ranges_ready, 1)

            dve_x(0, 0)
            dve_xn(0, 0)
            dve_x(1, 1)
            dve_xn(1, 1)
            edge_ranges()
            dve_out(0, 0, False)
            dve_x(2, 0)
            dve_xn(2, 0)
            dve_out(1, 1, False)
            with dve.Fori(1, TILES // 2 - 1) as m:
                for i in range(2):
                    t = 2 * m + i
                    dve_x(t + 1, 1 - i)
                    dve_xn(t + 1, 1 - i)
                    dve_out(t, i, True)
            dve_x(TILES - 1, 1)
            dve_xn(TILES - 1, 1)
            dve_out(TILES - 2, 0, True)
            dve_out(TILES - 1, 1, True)

            rnd = dve.alloc_register("rnd_dve")
            dve.reg_mov(rnd, 0)

            def one_hots(q, u1):
                dve.wait_ge(meta_loaded[q], u1 * 16)
                for c in range(CHUNKS):
                    last = v.tensor_scalar(hot[q][:, c, :], iota_n[:, :], m_f[q][:, 3 * c + 1:3 * c + 2],
                                           m_f[q][:, 3 * c + 2:3 * c + 3], ALU.is_equal, ALU.mult)
                last.then_inc(hot_ready[q], 1)

            def residual(t, warm):
                dve.wait_ge(agg_done, t + 1)
                dve.wait_ge(xc_loaded, (t + 1) * 16)
                if warm:
                    dve.wait_ge(pair_stored, t * 16)
                v.scalar_tensor_tensor(pair[:, 0, :], agg[0:TILE, 0:D], 0.0, x_c[:, :], ALU.max, ALU.add
                                       ).then_inc(agg_read, 1)
                dve.drain()
                v.bn_stats(st_c[:, :], pair[:, 0, :])
                dve.drain()
                v.bn_aggr(mv_c[:, :], st_c[:, :]).then_inc(var2_ready, 1)

            def norm2(t):
                dve.wait_ge(std2_ready, t + 1)
                v.reciprocal(rs_c[:, :], sd_c[:, :])
                dve.drain()
                v.tensor_scalar(pair[:, 1, :], pair[:, 0, :], mv_c[:, 0:1], rs_c[:, :], ALU.subtract, ALU.mult
                                ).then_inc(xn2_ready, 1)

            def pick(t):
                dve.wait_ge(logits_done, t + 1)
                v.tensor_copy(lg[:, :], lg_p[0:TILE, 0:EXPERTS])
                dve.drain()
                v.max(top[:, :], lg[:, :])
                dve.drain()
                v.max_index(topi[:, :], top[:, :], lg[:, :])
                v.tensor_tensor(gap[:, bass.ds(t, 1)], top[:, 1:2], top[:, 0:1], ALU.subtract)
                dve.drain()
                v.tensor_copy(topf[:, :], topi[:, 0:2])
                dve.drain()
                v.tensor_tensor(oh[:, :, :], iota_e[0:TILE, :].unsqueeze(1).to_broadcast([TILE, 2, EXPERTS]),
                                topf[:, :].unsqueeze(2).to_broadcast([TILE, 2, EXPERTS]), ALU.is_equal)
                dve.drain()
                v.tensor_tensor(both[0:TILE, :], oh[:, 0, :], oh[:, 1, :], ALU.add).then_inc(both_ready, 1)

            def place(t, warm):
                dve.wait_ge(rank_done, t + 1)
                if warm:
                    for k in range(2):
                        dve.wait_ge(sent[k], t * 16)
                v.tensor_tensor(slf[:, :], rank_p[0:TILE, 32:32 + EXPERTS], region[0:TILE, :], ALU.add)
                v.tensor_tensor(seen[0:TILE, :], seen[0:TILE, :], both[0:TILE, :], ALU.add)
                dve.drain()
                v.tensor_tensor(slx[:, :, :], oh[:, :, :], slf[:, :].unsqueeze(1).to_broadcast([TILE, 2, EXPERTS]),
                                ALU.mult)
                dve.drain()
                v.tensor_reduce(slot_f[:, :], slx[:, :, :], AX.X, ALU.add)
                dve.drain()
                v.tensor_copy(slot_all[:, bass.ds(t * 2, 2)], slot_f[:, :])
                v.tensor_copy(expert_all[:, bass.ds(t * 2, 2)], topf[:, :])
                v.tensor_copy(slots[:, :], slot_f[:, :]).then_inc(slots_ready, 1)

            def dve_tile(t, finish, warm):
                dve.drain()
                v.tensor_scalar(iota_n[:, :], iota_n[:, :], float(TILE), None, ALU.add)
                dve.drain()

                def between(s):
                    if finish:
                        if s == 0:
                            residual(t - 1, warm)
                        if s == 1:
                            norm2(t - 1)
                        if s == 3:
                            pick(t - 1)

                tile_rounds(dve, rnd, t, one_hots, between)
                if finish:
                    place(t - 1, warm)

            dve_tile(0, False, False)
            dve_tile(1, True, False)
            with dve.Fori(2, TILES) as t:
                dve_tile(t, True, True)
            residual(TILES - 1, True)
            norm2(TILES - 1)
            pick(TILES - 1)
            place(TILES - 1, True)
            dve.drain().then_inc(gap_ready, 1)

            dve.wait_ge(count_done, 1)
            v.tensor_copy(cnt[:, :], rank_p[0:TILE, 64:64 + EXPERTS])
            dve.drain()
            v.tensor_tensor(padr_i[:, :], cnt[:, :], region[0:TILE, :], ALU.add)
            v.tensor_scalar(cnt_i[:, :], cnt[:, :], float(P - 1), None, ALU.add)
            dve.drain()
            v.tensor_scalar(nt_i[:, :], cnt_i[:, :], P.bit_length() - 1, None, ALU.arith_shift_right)
            dve.drain()
            v.tensor_copy(nt_f[:, :], nt_i[:, :])
            dve.drain()
            v.tensor_tensor_scan(cum[:, :], ones[0:TILE, 0:EXPERTS], nt_f[:, :], 0.0, ALU.mult, ALU.add)
            v.tensor_scalar(step[:, :], nt_f[:, :], -float(P), float(CAP), ALU.mult, ALU.add)
            dve.drain()
            shape = [1, MOE_TILES, EXPERTS]
            v.tensor_tensor(past[:, :, :], iota_m[:, :].unsqueeze(2).to_broadcast(shape),
                            cum[0:1, :].unsqueeze(1).to_broadcast(shape), ALU.is_ge)
            dve.drain()
            v.tensor_reduce(e_f[:, :], past[:, :, :], AX.X, ALU.add)
            v.tensor_tensor(past2[:, :, :], past[:, :, :], step[0:1, :].unsqueeze(1).to_broadcast(shape), ALU.mult)
            dve.drain()
            v.tensor_reduce(r_f[:, :], past2[:, :, :], AX.X, ALU.add)
            v.tensor_scalar(e_f[:, :], e_f[:, :], float(EXPERTS - 1), None, ALU.min)
            v.memset(new_f[:, 0:RING], 1.0)
            dve.drain()
            v.scalar_tensor_tensor(r_f[:, :], iota_m[:, :], float(P), r_f[:, :], ALU.mult, ALU.add)
            v.tensor_tensor(new_f[:, RING:MOE_TILES], e_f[:, RING:MOE_TILES], e_f[:, 0:MOE_TILES - RING], ALU.not_equal)
            v.tensor_copy(e_t[:, :], e_f[:, :])
            dve.drain()
            v.tensor_scalar(row_t[:, :], r_f[:, :], float(REGIONS), None, ALU.min)
            v.tensor_copy(new_t[:, :], new_f[:, :])
            dve.drain().then_inc(moe_table, 1)
            v.tensor_tensor(shift0[:, :], cum[:, :], nt_f[:, :], ALU.subtract)
            dve.drain()
            v.scalar_tensor_tensor(shift[:, :], shift0[:, :], float(P), region[0:TILE, :], ALU.mult, ALU.subtract)
            dve.drain()
            for e in range(EXPERTS):
                v.tensor_scalar(shifted[e % 2][:, :], expert_all[:, :], float(e), shift[:, e:e + 1],
                                ALU.is_equal, ALU.mult)
                dve.drain()
                v.tensor_tensor(slot_all[:, :], slot_all[:, :], shifted[e % 2][:, :], ALU.add)
            dve.drain()
            v.tensor_copy(moe_row[:, :], slot_all[:, :])

            def add_b2(i, k, warm):
                dve.wait_ge(mm2_done, i + 1)
                if warm:
                    dve.wait_ge(yo_stored[k], (i // RING) * 16)
                v.tensor_tensor(yo[k][:, :], y_p[:, 0:D], b2_s[k][:, :], ALU.add).then_inc(yo_ready, 1)

            for k in range(RING):
                add_b2(k, k, False)
            with dve.Fori(1, MOE_TILES // RING) as m:
                for k in range(RING):
                    dve.wait_ge(mm2_done, RING * m + k + 1)
                    dve.wait_ge(yo_stored[k], m * 16)
                    v.tensor_tensor(yo[k][:, :], y_p[:, 0:D], b2_s[k][:, :], ALU.add).then_inc(yo_ready, 1)

            dve.wait_ge(exp_done, 1)
            v.tensor_scalar(wden[:, :], wt[:, 1, :], 1.0, None, ALU.add)
            dve.drain()
            v.reciprocal(wt[:, 0, :], wden[:, :])
            dve.drain()
            v.tensor_tensor(wt[:, 1, :], wt[:, 1, :], wt[:, 0, :], ALU.mult)

            def ready_slots(t, i):
                dve.drain()
                v.tensor_copy(sl_e[i][:, :], moe_row[:, bass.ds(t * 2, 2)])
                dve.drain().then_inc(sl_ready, 1)

            def mix(m, t, i):
                for k in range(2):
                    dve.wait_ge(y_loaded[i][k], (m + 1) * 16)
                dve.wait_ge(pr_loaded[i], (m + 1) * 16)
                v.scalar_tensor_tensor(acc_e[i][:, :], y_e[i][0][:, :], wt[:, 0, bass.ds(t, 1)], pr_e[i][:, 1, :],
                                       ALU.mult, ALU.add)
                dve.drain()
                v.scalar_tensor_tensor(acc_e[i][:, :], y_e[i][1][:, :], wt[:, 1, bass.ds(t, 1)], acc_e[i][:, :],
                                       ALU.mult, ALU.add)
                dve.drain()
                v.bn_stats(st_e[i][:, :], acc_e[i][:, :])
                dve.drain()
                v.bn_aggr(mv_e[i][:, :], st_e[i][:, :]).then_inc(var3_ready, 1)

            def emit(m, t, i, warm):
                dve.wait_ge(std3_ready, t + 1)
                v.reciprocal(rs_e[i][:, :], sd_e[i][:, :])
                dve.drain()
                v.tensor_scalar(acc_e[i][:, :], acc_e[i][:, :], mv_e[i][:, 0:1], rs_e[i][:, :], ALU.subtract, ALU.mult)
                dve.drain()
                v.tensor_tensor(acc_e[i][:, :], acc_e[i][:, :], gam[0:TILE, :], ALU.mult)
                dve.drain()
                v.tensor_tensor(acc_e[i][:, :], acc_e[i][:, :], bet[0:TILE, :], ALU.add)
                dve.drain()
                if warm:
                    dve.wait_ge(o_stored[i], m * 16)
                v.tensor_tensor(o_e[i][:, :], acc_e[i][:, :], pr_e[i][:, 0, :], ALU.add).then_inc(o_ready, 1)

            dve.wait_ge(const_loaded, 96)
            ready_slots(0, 0)
            ready_slots(1, 1)
            for i in range(2):
                mix(0, i, i)
                emit(0, i, i, False)
                ready_slots(2 + i, i)
            with dve.Fori(1, TILES // 2 - 1) as m:
                for i in range(2):
                    t = 2 * m + i
                    mix(m, t, i)
                    emit(m, t, i, True)
                    ready_slots(t + 2, i)
            for i in range(2):
                mix(TILES // 2 - 1, TILES - 2 + i, i)
                emit(TILES // 2 - 1, TILES - 2 + i, i, True)

        @block.tensor
        def _(pe):
            mm = nc.tensor.matmul

            def turn(dst_p, rows_, n):
                for k in range(2):
                    last = nc.tensor.transpose(dst_p[:, k * n:(k + 1) * n], rows_[:, k * P:(k + 1) * P],
                                               ident[0:n, 0:n])
                return last

            pe.wait_ge(pool_const, 1)
            pe.wait_ge(zeros_set, 1)
            pe.wait_ge(const_loaded, 96)

            def pe_turn(t, i):
                pe.wait_ge(xn_ready, t + 1)
                turn(bank[4 + i], xn[i], TILE).then_inc(xnT_done, 1)

            def pe_h(t, i, warm):
                pe.wait_ge(xnT_ready, t + 1)
                for j in range(4):
                    if warm and j in (0, 2):
                        pe.wait_ge(h_out_act, 2 * t - 1 + j // 2)
                    if warm and j in (1, 3):
                        pe.wait_ge(h_out_dve, 2 * t - 1 + j // 2)
                    for k in range(2):
                        last = mm(bank[j][0:TILE, :], xnT[i][:, k, :],
                                  w_rel[:, k, 2 * j:2 * j + 2, :].rearrange("p r o -> p (r o)"),
                                  start=(k == 0), stop=(k == 1))
                    last.then_inc(h_done, 1)

            pe_turn(0, 0)
            pe.wait_ge(w_ready, 1)
            pe_turn(1, 1)
            pe_h(0, 0, False)
            pe.wait_ge(ends_ready, 1)
            nc.tensor.transpose(bank[6][0:2 * TILES, 0:P], ends[:, :], ident[:, :]).then_inc(ends_turned, 1)
            pe.wait_ge(ends_max, 1)
            nc.tensor.transpose(bank[7][0:1, 0:2 * TILES], ends1[:, :], ident[0:2 * TILES, 0:2 * TILES]
                                ).then_inc(ends_back, 1)
            pe_turn(2, 0)
            pe_h(1, 1, True)
            with pe.Fori(1, TILES // 2 - 1) as m:
                for i in range(2):
                    pe_turn(2 * m + i + 1, 1 - i)
                    pe_h(2 * m + i, i, True)
            pe_turn(TILES - 1, 1)
            pe_h(TILES - 2, 0, True)
            pe_h(TILES - 1, 1, True)

            for q in range(PHASES):
                pe.nop(nofuse=True).then_inc(phase_free[q], 1)
            pe.wait_ge(ranges_ready, 1)
            pe.wait_ge(h_out_act, 2 * TILES)
            pe.wait_ge(h_out_dve, 2 * TILES)
            rnd = pe.alloc_register("rnd_pe")
            pe.reg_mov(rnd, 0)

            def sum_round(q, u1):
                pe.wait_ge(hot_ready[q], u1)
                for c in range(CHUNKS):
                    pe.wait_ge(gathered[q][c], u1 * 16)
                    last = mm(agg[0:TILE, 0:D], hot[q][:, c, :], rows[q][c][:, :], start=False, stop=False)
                last.then_inc(phase_free[q], 1)

            def turn2(t):
                pe.wait_ge(xn2_ready, t + 1)
                turn(x2T_p, pair[:, 1, :], TILE).then_inc(x2T_done, 1)

            def logits(t):
                pe.wait_ge(x2T_ready, t + 1)
                for k in range(2):
                    mm(lg_p[0:TILE, 0:EXPERTS], xn2T[:, k, :], gw[:, k, :], start=(k == 0), stop=False)
                mm(lg_p[0:TILE, 0:EXPERTS], row0[:, 0:TILE], gb[:, :], start=False, stop=True).then_inc(logits_done, 1)

            def rank(t):
                pe.wait_ge(both_ready, t + 1)
                mm(rank_p[0:TILE, 32:32 + EXPERTS], ones[:, 0:TILE], seen[:, :], start=True, stop=False)
                mm(rank_p[0:TILE, 32:32 + EXPERTS], before[:, 0:TILE], both[:, :], start=False, stop=True
                   ).then_inc(rank_done, 1)

            def pe_tile(t, finish):
                pe.wait_ge(xTc_loaded, (t + 1) * 16)
                if finish and False:
                    pass
                if not (isinstance(t, int) and t == 0):
                    pe.wait_ge(agg_read, t)
                for k in range(2):
                    last = mm(agg[0:TILE, 0:D], xT_c[:, k * TILE:(k + 1) * TILE], lw[:, k, :],
                              start=(k == 0), stop=False)
                last.then_inc(agg_open, 1)

                def between(s):
                    if finish:
                        if s == 1:
                            turn2(t - 1)
                        if s == 2:
                            logits(t - 1)
                        if s == 4:
                            rank(t - 1)

                tile_rounds(pe, rnd, t, sum_round, between)
                mm(agg[0:TILE, 0:D], row0[:, 0:TILE], hb[:, :], start=False, stop=True).then_inc(agg_done, 1)

            pe_tile(0, False)
            with pe.Fori(1, TILES) as t:
                pe_tile(t, True)
            turn2(TILES - 1)
            logits(TILES - 1)
            rank(TILES - 1)
            pe.wait_ge(slots_ready, TILES)
            mm(rank_p[0:TILE, 64:64 + EXPERTS], ones[:, 0:TILE], seen[:, :], start=True, stop=True
               ).then_inc(count_done, 1)

            def turn_rows(i, k, m):
                pe.wait_ge(xd_loaded[k], (m + 1) * 16)
                if not (isinstance(i, int) and i == 0):
                    pe.wait_ge(xdT_ready, i)
                turn(xdT_p, xd[k], P).then_inc(xdT_done, 1)

            def up(i, k, m):
                pe.wait_ge(xdT_ready, i + 1)
                pe.wait_ge(w_loaded[k], (m + 1) * 32)
                for f in range(4):
                    for kk in range(2):
                        last = mm(h_p[k][:, f * P:(f + 1) * P], w_s[k][:, kk * FF + f * P:kk * FF + (f + 1) * P],
                                  xdT[k][:, kk, :], start=(kk == 0), stop=(kk == 1))
                last.then_inc(mm1_done, 1)

            def down(i, k):
                pe.wait_ge(hT_ready, i + 1)
                if not (isinstance(i, int) and i == 0):
                    pe.wait_ge(yo_ready, i)
                for f in range(4):
                    last = mm(y_p[:, 0:D], hT[k][:, f, :], w_s[k][:, 2 * FF + f * D:2 * FF + (f + 1) * D],
                              start=(f == 0), stop=(f == 3))
                last.then_inc(mm2_done, 1)

            for s in range(RING):
                turn_rows(s, s, 0)
                if s >= 1:
                    up(s - 1, s - 1, 0)
                if s >= 2:
                    down(s - 2, s - 2)
            with pe.Fori(1, MOE_TILES // RING) as m:
                for k in range(RING):
                    s = RING * m + k
                    turn_rows(s, k, m)
                    up(s - 1, (k - 1) % RING, m if k else m - 1)
                    down(s - 2, (k - 2) % RING)
            up(MOE_TILES - 1, RING - 1, MOE_TILES // RING - 1)
            down(MOE_TILES - 2, RING - 2)
            down(MOE_TILES - 1, RING - 1)


def kernel(x, src, dst, edge_type_8, edge_weight1, L0_gnn_weight, L0_gnn_w_comp, L0_gnn_loop_weight, L0_gnn_h_bias,
           L0_ffn_gate_w, L0_ffn_gate_b, L0_ffn_w1, L0_ffn_b1, L0_ffn_w2, L0_ffn_b2, L0_ffn_gamma, L0_ffn_beta):
    import numpy as np
    import concourse.bacc as bacc
    from concourse.bass_utils import run_bass_kernel_spmd

    def rows(a, parts):
        a = np.asarray(a)
        return a.reshape(EXPERTS, parts, P, -1).transpose(0, 2, 1, 3).reshape(EXPERTS, P, -1)

    w_cat = np.concatenate([rows(L0_ffn_w1, 2), rows(L0_ffn_w2, 4), rows(L0_ffn_b1, 4)], axis=2)
    arrays = {
        "x_in": x, "src_in": src, "dst_in": dst, "etype_in": edge_type_8,
        "eweight_in": np.asarray(edge_weight1).reshape(N_EDGES), "basis_in": L0_gnn_weight, "comp_in": L0_gnn_w_comp,
        "loop_in": L0_gnn_loop_weight, "hbias_in": L0_gnn_h_bias, "gatew_in": L0_ffn_gate_w, "gateb_in": L0_ffn_gate_b,
        "wcat_in": w_cat.reshape(EXPERTS * P, W_COLS), "b2_in": L0_ffn_b2, "gamma_in": L0_ffn_gamma,
        "beta_in": L0_ffn_beta,
    }
    arrays = {k: np.ascontiguousarray(np.asarray(a)) for k, a in arrays.items()}
    nc = bacc.Bacc("TRN2", target_bir_lowering=False, num_devices=1)
    args = [nc.dram_tensor(k, a.shape, mybir.dt.from_np(a.dtype), kind="ExternalInput").ap() for k, a in arrays.items()]
    out = nc.dram_tensor("out_x", (N_NODES, D), F32, kind="ExternalOutput").ap()
    build(nc, *args, out)
    r = run_bass_kernel_spmd(nc, [arrays], core_ids=[0])
    return r.results[0]["out_x"]
```

```python
from contextlib import ExitStack

import concourse.bass as bass
from concourse import mybir

F32 = mybir.dt.float32
I32 = mybir.dt.int32
U32 = mybir.dt.uint32
ALU = mybir.AluOpType
ACT = mybir.ActivationFunctionType
AX = mybir.AxisListType

N_NODES = 6250
N_EDGES = 106250
D = 256
RELS = 8
BASES = 4
EXPERTS = 16
FF = 512
EPS = 1e-5
P = 128

TILE = 125
TILES = N_NODES // TILE
assert TILE * TILES == N_NODES

EDGE_COLS = 832
EDGES_PAD = P * EDGE_COLS
LAST_COLS = N_EDGES - (P - 1) * EDGE_COLS
BLOCK = 32
BLOCKS = EDGE_COLS // BLOCK
CHUNKS = 2
ROUND = CHUNKS * P
META_ROWS = EDGES_PAD + ROUND * 8
NO_NODE = N_NODES + TILE - 1
BIG = float(P * BLOCKS)
PHASES = 8
SINGLE = 7
MIN_ROUNDS = SINGLE + 1
MAX_ROUNDS = EDGES_PAD // ROUND + MIN_ROUNDS

WAVES = 2
WAVE_TILES = [23, 27]
WAVE_START = [0, 23]
assert sum(WAVE_TILES) == TILES
CAP = (-(-max(WAVE_TILES) * TILE // P) + 1) * P
REGIONS = EXPERTS * CAP
RING = 3
MIX_FROM = 29
GAP_TILES = 4
MOE = [RING * (TILES - MIX_FROM),
       -(-((2 * WAVE_TILES[1] * TILE + EXPERTS * (P - 1)) // P) // RING) * RING]
assert MOE[0] >= (2 * WAVE_TILES[0] * TILE + EXPERTS * (P - 1)) // P
MOE_ALL = sum(MOE)
ITERS_A = MOE[0] // RING
ITERS_B = MOE[1] // RING
assert WAVE_TILES[0] <= ITERS_B
E_USES = [WAVE_TILES[0] + (WAVE_TILES[1] + 1) // 2, WAVE_TILES[1] // 2]
assert WAVE_TILES[1] % 2 == 1
W_B1 = 2 * FF + 4 * D
W_B2 = W_B1 + 4
W_COLS = W_B2 + D


def build(nc, x, src, dst, etype, eweight, basis, comp, loop_w, h_bias, gate_w, gate_b, w_cat,
          gamma, beta, out):
    ctx = ExitStack()
    with ctx:
        def sb(name, shape, dt=F32):
            return ctx.enter_context(nc.sbuf_tensor(name, shape, dt))

        def sem(name):
            return ctx.enter_context(nc.semaphore(name))

        def dram(name, shape, dt=F32):
            return nc.dram_tensor(name, shape, dt).ap()

        meta_d = dram("meta_d", (META_ROWS, 3), I32)
        h_d = dram("h_d", (N_NODES * RELS, D))
        xnT_d = dram("xnT_d", (TILES * P, 2 * TILE))
        pair_d = dram("pair_d", (N_NODES, 2 * D))
        disp_d = [dram(f"disp{w}_d", (REGIONS + P + 1, D)) for w in range(WAVES)]
        moe_d = [dram(f"moe{w}_d", (MOE[w] * P, D)) for w in range(WAVES)]

        ident = sb("ident", [P, P])
        ones = sb("ones", [P, P])
        row0 = sb("row0", [P, P])
        before = sb("before", [P, P])
        zeros = sb("zeros", [P, D])
        iota_n = sb("iota_n", [P, TILE])
        iota_e = sb("iota_e", [P, EXPERTS])
        region = sb("region", [P, EXPERTS])
        hb = sb("hb", [P, D])
        gb = sb("gb", [P, EXPERTS])
        gw = sb("gw", [P, 2, EXPERTS])
        lw = sb("lw", [P, 2, D])
        eps = sb("eps", [P, 1])
        gam = sb("gam", [P, D])
        bet = sb("bet", [P, D])

        src_i = sb("src_i", [P, EDGE_COLS], I32)
        dst_i = sb("dst_i", [P, EDGE_COLS], I32)
        et_i = sb("et_i", [P, EDGE_COLS], I32)
        nrm = sb("nrm", [P, EDGE_COLS])
        meta = sb("meta", [P, EDGE_COLS, 3], I32)
        tail_meta = sb("tail_meta", [P, (META_ROWS - EDGES_PAD) // P, 3], I32)
        meta_f = meta[:, :, :].bitcast(F32)
        bmin = sb("bmin", [P, BLOCKS])
        bmax = sb("bmax", [P, BLOCKS])
        bid = sb("bid", [P, BLOCKS])
        bidr = sb("bidr", [P, BLOCKS])
        tlo = sb("tlo", [P, TILES])
        candA = sb("candA", [P, TILES, BLOCKS])
        candB = sb("candB", [P, TILES, BLOCKS])
        ends = sb("ends", [P, 2 * TILES])
        ends1 = sb("ends1", [2 * TILES, 1])
        er = sb("er", [1, 2 * TILES])
        has = sb("has", [1, TILES])
        fst = sb("fst", [1, TILES])
        rnf = sb("rnf", [1, TILES])
        rni = sb("rni", [1, TILES], I32)
        start_t = sb("start_t", [1, TILES], I32)
        rounds_t = sb("rounds_t", [1, TILES], I32)

        comp_s = sb("comp_s", [P, RELS * BASES])
        bas = sb("bas", [P, BASES, 2, D])
        w_rel = sb("w_rel", [P, 2, RELS, D])
        xin = [sb(f"xin{i}", [TILE, D]) for i in range(2)]
        st = [sb(f"st{i}", [TILE, 6]) for i in range(2)]
        mv = [sb(f"mv{i}", [TILE, 2]) for i in range(2)]
        sd = [sb(f"sd{i}", [TILE, 1]) for i in range(2)]
        rs = [sb(f"rs{i}", [TILE, 1]) for i in range(2)]
        xn = [sb(f"xn{i}", [TILE, D]) for i in range(2)]
        xnT = [sb(f"xnT{i}", [P, 2, TILE]) for i in range(2)]
        hr = [sb(f"hr{i}", [TILE, RELS * D]) for i in range(2)]

        m_s = [sb(f"m_s{q}", [P, CHUNKS * 3], I32) for q in range(PHASES)]
        m_f = [t[:, :].bitcast(F32) for t in m_s]
        rows = [[sb(f"rows{q}_{c}", [P, D]) for c in range(CHUNKS)] for q in range(PHASES)]
        hot = [sb(f"hot{q}", [P, CHUNKS, TILE]) for q in range(PHASES)]
        x_c = sb("x_c", [TILE, D])
        xT_c = sb("xT_c", [P, 2 * TILE])
        pair = sb("pair", [TILE, 2, D])
        st_c = sb("st_c", [TILE, 6])
        mv_c = sb("mv_c", [TILE, 2])
        sd_c = sb("sd_c", [TILE, 1])
        rs_c = sb("rs_c", [TILE, 1])
        send = sb("send", [TILE, D])
        xn2T = sb("xn2T", [P, 2, TILE])
        lg = sb("lg", [TILE, EXPERTS])
        top = sb("top", [TILE, 8])
        topi = sb("topi", [TILE, 8], U32)
        topf = sb("topf", [TILE, 2])
        oh = sb("oh", [TILE, 2, EXPERTS])
        both = sb("both", [P, EXPERTS])
        seen = [sb(f"seen{w}", [P, EXPERTS]) for w in range(WAVES)]
        slf = sb("slf", [TILE, EXPERTS])
        slx = sb("slx", [TILE, 2, EXPERTS])
        slot_f = sb("slot_f", [TILE, 2])
        slots = sb("slots", [TILE, 2], I32)
        slot_all = sb("slot_all", [TILE, 2 * TILES])
        expert_all = sb("expert_all", [TILE, 2 * TILES])
        moe_row = sb("moe_row", [TILE, 2 * TILES], I32)
        shifted = [sb(f"shifted{i}", [TILE, 2 * TILES]) for i in range(2)]
        shift = sb("shift", [TILE, EXPERTS])
        shift0 = sb("shift0", [TILE, EXPERTS])
        gap = sb("gap", [TILE, TILES])

        cnt = sb("cnt", [TILE, EXPERTS])
        cnt_i = sb("cnt_i", [TILE, EXPERTS], I32)
        padr_i = [sb(f"padr_i{w}", [TILE, EXPERTS], I32) for w in range(WAVES)]
        nt_i = sb("nt_i", [TILE, EXPERTS], I32)
        nt_f = sb("nt_f", [TILE, EXPERTS])
        cum = sb("cum", [TILE, EXPERTS])
        step = sb("step", [TILE, EXPERTS])
        iota_m = sb("iota_m", [1, max(MOE)])
        past = sb("past", [1, max(MOE), EXPERTS])
        past2 = sb("past2", [1, max(MOE), EXPERTS])
        e_f = sb("e_f", [1, max(MOE)])
        r_f = sb("r_f", [1, max(MOE)])
        new_f = sb("new_f", [1, max(MOE)])
        moe_t = sb("moe_t", [1, MOE_ALL], I32)
        xd = [sb(f"xd{i}", [P, D]) for i in range(RING)]
        xdT = [sb(f"xdT{i}", [P, 2, P]) for i in range(RING)]
        w_s = [sb(f"w_s{i}", [P, W_COLS]) for i in range(RING)]
        hT = [sb(f"hT{i}", [P, 4, P]) for i in range(RING)]
        yo = [sb(f"yo{i}", [P, D]) for i in range(RING)]

        wt = sb("wt", [TILE, 2, TILES])
        wden = sb("wden", [TILE, TILES])
        sl_e = [sb(f"sl_e{i}", [TILE, 2], I32) for i in range(2)]
        y_e = [[sb(f"y_e{i}_{k}", [TILE, D]) for k in range(2)] for i in range(2)]
        pr_e = [sb(f"pr_e{i}", [TILE, 2, D]) for i in range(2)]
        acc_e = [sb(f"acc_e{i}", [TILE, D]) for i in range(2)]
        o_e = [sb(f"o_e{i}", [TILE, D]) for i in range(2)]
        st_e = [sb(f"st_e{i}", [TILE, 6]) for i in range(2)]
        mv_e = [sb(f"mv_e{i}", [TILE, 2]) for i in range(2)]
        sd_e = [sb(f"sd_e{i}", [TILE, 1]) for i in range(2)]
        rs_e = [sb(f"rs_e{i}", [TILE, 1]) for i in range(2)]
        nm_e = [sb(f"nm_e{i}", [TILE, 1]) for i in range(2)]
        z_e = [sb(f"z_e{i}", [TILE, D]) for i in range(2)]

        bank = [ctx.enter_context(nc.psum_tensor(f"bank{i}", [P, 512], F32)) for i in range(8)]
        agg = bank[0]
        x2T_p, lg_p, rank_p, y_p, xdT_p = bank[1], bank[2], bank[2], bank[3], bank[4]
        h_p = bank[5:8]

        const_loaded = sem("const_loaded")
        edges_loaded = sem("edges_loaded")
        basis_loaded = sem("basis_loaded")
        pool_const = sem("pool_const")
        pads_set = sem("pads_set")
        zeros_set = sem("zeros_set")
        meta_built = sem("meta_built")
        nrm_copied = sem("nrm_copied")
        meta_stored = sem("meta_stored")
        zero_rows = sem("zero_rows")
        ends_ready = sem("ends_ready")
        ends_turned = sem("ends_turned")
        ends_max = sem("ends_max")
        ends_back = sem("ends_back")
        ranges_ready = sem("ranges_ready")
        w_ready = sem("w_ready")
        x_loaded = [sem(f"x_loaded{i}") for i in range(2)]
        var_ready = sem("var_ready")
        std_ready = sem("std_ready")
        xn_ready = sem("xn_ready")
        xnT_done = sem("xnT_done")
        xnT_ready = sem("xnT_ready")
        h_done = sem("h_done")
        h_out_act = sem("h_out_act")
        h_out_dve = sem("h_out_dve")
        h_stored = [sem(f"h_stored{i}") for i in range(2)]
        xnT_stored = [sem(f"xnT_stored{i}") for i in range(2)]
        table_ready = sem("table_ready")

        meta_loaded = [sem(f"meta_loaded{q}") for q in range(PHASES)]
        gathered = [[sem(f"gathered{q}_{c}") for c in range(CHUNKS)] for q in range(PHASES)]
        hot_ready = [sem(f"hot_ready{q}") for q in range(PHASES)]
        phase_free = [sem(f"phase_free{q}") for q in range(PHASES)]
        xc_loaded = sem("xc_loaded")
        xTc_loaded = sem("xTc_loaded")
        agg_open = sem("agg_open")
        agg_done = sem("agg_done")
        agg_read = sem("agg_read")
        var2_ready = sem("var2_ready")
        std2_ready = sem("std2_ready")
        xn2_ready = sem("xn2_ready")
        x2T_done = sem("x2T_done")
        send_ready = sem("send_ready")
        x2T_ready = sem("x2T_ready")
        pair_ready = sem("pair_ready")
        pair_stored = sem("pair_stored")
        logits_done = sem("logits_done")
        both_ready = sem("both_ready")
        rank_done = sem("rank_done")
        slots_ready = sem("slots_ready")
        sent = [sem(f"sent{k}") for k in range(2)]

        count_done = sem("count_done")
        moe_table = sem("moe_table")
        gaps_zeroed = sem("gaps_zeroed")
        xd_loaded = [sem(f"xd_loaded{i}") for i in range(RING)]
        w_loaded = [sem(f"w_loaded{i}") for i in range(RING)]
        xdT_done = sem("xdT_done")
        xdT_ready = sem("xdT_ready")
        mm1_done = sem("mm1_done")
        hT_ready = sem("hT_ready")
        mm2_done = sem("mm2_done")
        yo_ready = sem("yo_ready")
        yo_stored = [sem(f"yo_stored{i}") for i in range(RING)]
        moe_stored = [sem(f"moe_stored{w}") for w in range(WAVES)]

        exp_done = sem("exp_done")
        gap_ready = sem("gap_ready")
        sl_ready = sem("sl_ready")
        y_loaded = [[sem(f"y_loaded{i}_{k}") for k in range(2)] for i in range(2)]
        pr_loaded = [sem(f"pr_loaded{i}") for i in range(2)]
        mixed = sem("mixed")
        std3_ready = sem("std3_ready")
        scale_ready = sem("scale_ready")
        z_ready = sem("z_ready")
        o_ready = sem("o_ready")
        o_stored = [sem(f"o_stored{i}") for i in range(2)]

        block = ctx.enter_context(nc.Block())

        def by_phase(eng, counter, body):
            r = eng.snap(counter, min_val=0, max_val=TILES * MAX_ROUNDS)
            u1 = eng.snap((r >> (PHASES.bit_length() - 1)) + 1, min_val=1, max_val=TILES * MAX_ROUNDS)
            q = eng.snap(r & (PHASES - 1), min_val=0, max_val=PHASES - 1)

            def branch(lo, n):
                if n == 1:
                    body(lo, u1)
                    return
                with eng.If(q < lo + n // 2):
                    branch(lo, n // 2)
                with eng.Else():
                    branch(lo + n // 2, n // 2)
                if n < PHASES:
                    eng.nop()

            branch(0, PHASES)
            eng.reg_add(counter, counter, 1)

        def tile_rounds(eng, counter, t, body, between=None):
            n = eng.value_load(rounds_t[0:1, bass.ds(t, 1)], min_val=MIN_ROUNDS, max_val=MAX_ROUNDS)
            if between is None:
                with eng.Fori(0, n):
                    by_phase(eng, counter, body)
                return
            for p in range(SINGLE):
                by_phase(eng, counter, body)
                between(p)
            with eng.Fori(SINGLE, n):
                by_phase(eng, counter, body)

        def all_tiles(eng, one, peel=False):
            w1 = WAVE_START[1]
            one(0, None, None, None, False)
            one(1, 0, None, None, False)
            with eng.Fori(2, w1 + 1) as t:
                one(t, 0, 0, None, True)
            one(w1 + 1, 1, 0, None, True)
            with eng.Fori(w1 + 2, w1 + 2 + GAP_TILES) as t:
                one(t, 1, 1, None, True)
            assert w1 + 2 + GAP_TILES == MIX_FROM
            one(MIX_FROM, 1, 1, 0, True)
            if peel:
                one(MIX_FROM + 1, 1, 1, 1, True)
            with eng.Fori(MIX_FROM + 1 + peel, TILES) as t:
                one(t, 1, 1, t - MIX_FROM, True)

        @block.sync
        def _(sp):
            sp.dma_start(bas[:, :, :, :].rearrange("p b k o -> p (b k) o"),
                         basis.rearrange("b (k p) o -> p (b k) o", p=P)).then_inc(basis_loaded, 16)
            sp.dma_start(comp_s[:, :], comp.rearrange("(a r) b -> a (r b)", a=1).to_broadcast([P, RELS * BASES])
                         ).then_inc(basis_loaded, 16)
            for i in range(2):
                sp.dma_start(xin[i][:, :], x[i * TILE:(i + 1) * TILE, :]).then_inc(x_loaded[i], 16)
            sp.wait_ge(pads_set, 4)
            for dst_t, src_t in ((src_i, src), (dst_i, dst), (et_i, etype), (nrm, eweight)):
                sp.dma_start(dst_t[0:P - 1, :], src_t[0:(P - 1) * EDGE_COLS].rearrange("(p c) -> p c", p=P - 1)
                             ).then_inc(edges_loaded, 16)
                sp.dma_start(dst_t[P - 1:P, 0:LAST_COLS],
                             src_t[(P - 1) * EDGE_COLS:N_EDGES].rearrange("(p c) -> p c", p=1)
                             ).then_inc(edges_loaded, 16)
            sp.wait_ge(zeros_set, 1)
            sp.dma_start(hb[0:1, :], h_bias.rearrange("(a o) -> a o", a=1)).then_inc(const_loaded, 16)
            sp.dma_start(gb[0:1, :], gate_b.rearrange("(a o) -> a o", a=1)).then_inc(const_loaded, 16)
            sp.dma_start(gw[:, :, :], gate_w.rearrange("(k p) e -> p k e", p=P)).then_inc(const_loaded, 16)
            sp.dma_start(lw[:, :, :], loop_w.rearrange("(k p) o -> p k o", p=P)).then_inc(const_loaded, 16)
            sp.dma_start(gam[:, :], gamma.rearrange("(a o) -> a o", a=1).to_broadcast([P, D])).then_inc(const_loaded, 16)
            sp.dma_start(bet[:, :], beta.rearrange("(a o) -> a o", a=1).to_broadcast([P, D])).then_inc(const_loaded, 16)

            def load_x(t, i):
                sp.dma_start(xin[i][:, :], x[bass.ds(t * TILE, TILE), :]).then_inc(x_loaded[i], 16)

            def store_h(t, i):
                sp.wait_ge(xnT_ready, t + 1)
                sp.dma_start(xnT_d[bass.ds(t * P, P), :], xnT[i][:, :, :].rearrange("p k n -> p (k n)")
                             ).then_inc(xnT_stored[i], 16)
                sp.wait_ge(h_out_act, 2 * t + 2)
                sp.wait_ge(h_out_dve, 2 * t + 2)
                sp.dma_start(h_d[bass.ds(t * TILE * RELS, TILE * RELS), :].rearrange("(n r) o -> n (r o)", r=RELS),
                             hr[i][:, :]).then_inc(h_stored[i], 16)

            def store_edges():
                sp.wait_ge(meta_built, 1)
                sp.wait_ge(nrm_copied, 1)
                sp.dma_start(meta_d[0:EDGES_PAD, :].rearrange("(p c) f -> p (c f)", p=P),
                             meta[:, :, :].rearrange("p c f -> p (c f)")).then_inc(meta_stored, 16)
                sp.dma_start(meta_d[EDGES_PAD:META_ROWS, :].rearrange("(p c) f -> p (c f)", p=P),
                             tail_meta[:, :, :].rearrange("p c f -> p (c f)")).then_inc(meta_stored, 16)
                for w in range(WAVES):
                    sp.dma_start(disp_d[w][REGIONS:REGIONS + P, :], zeros[:, :]).then_inc(zero_rows, 16)

            def b_tile(t, i):
                sp.wait_ge(xn_ready, t + 1)
                load_x(t + 2, i)
                store_h(t, i)

            b_tile(0, 0)
            b_tile(1, 1)
            store_edges()
            with sp.Fori(1, TILES // 2 - 1) as m:
                for i in range(2):
                    b_tile(2 * m + i, i)
            for i in range(2):
                store_h(TILES - 2 + i, i)

            for i in range(2):
                sp.wait_ge(xnT_stored[i], 16 * (TILES // 2))
                sp.wait_ge(h_stored[i], 16 * (TILES // 2))
            sp.wait_ge(meta_stored, 32)
            sp.wait_ge(zero_rows, 16 * WAVES)
            sp.nop(nofuse=True).then_inc(table_ready, 1)
            sp.wait_ge(ranges_ready, 1)
            rnd = sp.alloc_register("rnd_sp")
            edge = sp.alloc_register("edge_sp")
            sp.reg_mov(rnd, 0)

            def load_meta(q, u1):
                e0 = sp.snap(edge, min_val=0, max_val=META_ROWS - ROUND)
                sp.wait_ge(phase_free[q], u1)
                sp.dma_start(m_s[q][:, :], meta_d[bass.ds(e0, ROUND), :].rearrange("(p c) f -> p (c f)", p=P)
                             ).then_inc(meta_loaded[q], 16)
                sp.reg_add(edge, edge, ROUND)

            with sp.Fori(0, TILES) as t:
                sp.reg_mov(edge, sp.value_load(start_t[0:1, bass.ds(t, 1)], min_val=0, max_val=EDGES_PAD))
                tile_rounds(sp, rnd, t, load_meta)

            def load_pair(t, i):
                sp.dma_start(pr_e[i][:, :, :].rearrange("n a o -> n (a o)"), pair_d[bass.ds(t * TILE, TILE), :]
                             ).then_inc(pr_loaded[i], 16)

            def store_out(t, i):
                sp.wait_ge(o_ready, t + 1)
                sp.dma_start(out[bass.ds(t * TILE, TILE), :], o_e[i][:, :]).then_inc(o_stored[i], 16)

            sp.wait_ge(pair_stored, 16 * TILES)
            load_pair(0, 0)
            with sp.Fori(0, WAVE_TILES[0]) as t:
                store_out(t, 0)
                load_pair(t + 1, 0)
            first = WAVE_START[1]
            load_pair(first + 1, 1)
            with sp.Fori(0, (WAVE_TILES[1] - 3) // 2) as m:
                for i in range(2):
                    store_out(2 * m + first + i, i)
                    load_pair(2 * m + first + 2 + i, i)
            store_out(TILES - 3, 0)
            load_pair(TILES - 1, 0)
            store_out(TILES - 2, 1)
            store_out(TILES - 1, 0)
            sp.wait_ge(o_stored[0], 16 * E_USES[0])
            sp.wait_ge(o_stored[1], 16 * E_USES[1])

        @block.gpsimd
        def _(pool):
            nc.gpsimd.memset(ident[:, :], 0.0)
            nc.gpsimd.memset(row0[:, :], 0.0)
            nc.gpsimd.memset(before[:, :], 0.0)
            nc.gpsimd.iota(iota_n[:, :], pattern=[[1, TILE]], base=-TILE, channel_multiplier=0,
                           allow_small_or_imprecise_dtypes=True)
            nc.gpsimd.iota(iota_e[:, :], pattern=[[1, EXPERTS]], base=0, channel_multiplier=0,
                           allow_small_or_imprecise_dtypes=True)
            nc.gpsimd.iota(region[:, :], pattern=[[CAP, EXPERTS]], base=0, channel_multiplier=0,
                           allow_small_or_imprecise_dtypes=True)
            nc.gpsimd.iota(tlo[:, :], pattern=[[TILE, TILES]], base=0, channel_multiplier=0,
                           allow_small_or_imprecise_dtypes=True)
            nc.gpsimd.iota(bid[:, :], pattern=[[1, BLOCKS]], base=1, channel_multiplier=BLOCKS,
                           allow_small_or_imprecise_dtypes=True)
            nc.gpsimd.iota(bidr[:, :], pattern=[[-1, BLOCKS]], base=int(BIG), channel_multiplier=-BLOCKS,
                           allow_small_or_imprecise_dtypes=True)
            nc.gpsimd.iota(iota_m[:, :], pattern=[[1, max(MOE)]], base=0, channel_multiplier=0,
                           allow_small_or_imprecise_dtypes=True)
            pool.drain()
            nc.gpsimd.affine_select(out=ident[:, :], in_=ident[:, :], compare_op=ALU.not_equal, fill=1.0, base=0,
                                    pattern=[[-1, P]], channel_multiplier=1)
            nc.gpsimd.affine_select(out=before[:, :], in_=before[:, :], compare_op=ALU.is_ge, fill=1.0, base=0,
                                    pattern=[[-1, P]], channel_multiplier=1)
            nc.gpsimd.affine_select(out=row0[:, :], in_=row0[:, :], compare_op=ALU.not_equal, fill=1.0, base=0,
                                    pattern=[[0, P]], channel_multiplier=1)
            pool.drain().then_inc(pool_const, 1)

            pool.wait_ge(table_ready, 1)
            pool.wait_ge(ranges_ready, 1)
            rnd = pool.alloc_register("rnd_pool")
            pool.reg_mov(rnd, 0)

            def gather(q, u1):
                pool.wait_ge(meta_loaded[q], u1 * 16)
                pool.nop(nofuse=True)
                for c in range(CHUNKS):
                    nc.gpsimd.indirect_dma_start(
                        out=rows[q][c][:, :], out_offset=None, in_=h_d,
                        in_offset=bass.IndirectOffsetOnAxis(ap=m_s[q][:, 3 * c:3 * c + 1], axis=0),
                    ).then_inc(gathered[q][c], 16)

            def scatter(t, w):
                pool.wait_ge(slots_ready, t + 1)
                pool.wait_ge(send_ready, t + 1)
                pool.nop(nofuse=True)
                for k in range(2):
                    nc.gpsimd.indirect_dma_start(
                        out=disp_d[w], out_offset=bass.IndirectOffsetOnAxis(ap=slots[:, k:k + 1], axis=0),
                        in_=send[:, :], in_offset=None).then_inc(sent[k], 16)

            def pool_tile(t, w1, w2, m, warm):
                def between(p):
                    if p == 1 and w2 is not None:
                        scatter(t - 2, w2)

                tile_rounds(pool, rnd, t, gather, between)

            all_tiles(pool, pool_tile)
            scatter(TILES - 2, 1)
            scatter(TILES - 1, 1)

            def gather_y(t, i, w):
                pool.wait_ge(sl_ready, t + 1)
                pool.nop(nofuse=True)
                for k in range(2):
                    nc.gpsimd.indirect_dma_start(
                        out=y_e[i][k][:, :], out_offset=None, in_=moe_d[w],
                        in_offset=bass.IndirectOffsetOnAxis(ap=sl_e[i][:, k:k + 1], axis=0),
                    ).then_inc(y_loaded[i][k], 16)

            pool.wait_ge(moe_stored[0], 1)
            with pool.Fori(0, WAVE_TILES[0]) as t:
                gather_y(t, 0, 0)
            pool.wait_ge(moe_stored[1], 1)
            with pool.Fori(0, WAVE_TILES[1] // 2) as m:
                for i in range(2):
                    gather_y(2 * m + WAVE_START[1] + i, i, 1)
            gather_y(TILES - 1, 0, 1)

        @block.scalar
        def _(act):
            act.wait_ge(edges_loaded, 128)
            nc.scalar.copy(meta_f[:, :, 2], nrm[:, :])
            act.drain().then_inc(nrm_copied, 1)
            act.wait_ge(zeros_set, 1)

            def act_std(t, i):
                act.wait_ge(var_ready, t + 1)
                nc.scalar.activation(sd[i][:, :], mv[i][:, 1:2], ACT.Sqrt, bias=eps[0:TILE, :]).then_inc(std_ready, 1)

            def act_h(t, i, warm):
                act.wait_ge(xnT_done, t + 1)
                if warm:
                    act.wait_ge(xnT_stored[i], (t // 2) * 16)
                nc.scalar.copy(xnT[i][:, :, :].rearrange("p k n -> p (k n)"), bank[4 + i][:, 0:2 * TILE]
                               ).then_inc(xnT_ready, 1)

            def act_out(t, i, warm):
                if warm:
                    act.wait_ge(h_stored[i], (t // 2) * 16)
                for j in (0, 2):
                    act.wait_ge(h_done, 4 * t + j + 1)
                    nc.scalar.copy(hr[i][:, j * 512:(j + 1) * 512], bank[j][0:TILE, :]).then_inc(h_out_act, 1)

            act_std(0, 0)
            act_h(0, 0, False)
            act_std(1, 1)
            act_h(1, 1, False)
            act_out(0, 0, False)
            act_std(2, 0)
            act_h(2, 0, True)
            act_out(1, 1, False)
            with act.Fori(1, TILES // 2 - 1) as m:
                for i in range(2):
                    t = 2 * m + i
                    act_std(t + 1, 1 - i)
                    act_h(t + 1, 1 - i, True)
                    act_out(t, i, True)
            act_std(TILES - 1, 1)
            act_h(TILES - 1, 1, True)
            act_out(TILES - 2, 0, True)
            act_out(TILES - 1, 1, True)

            def load_rows(i, k, w):
                word = act.value_load(moe_t[0:1, bass.ds(i, 1)], min_val=0, max_val=REGIONS * 32 + 31)
                row = act.snap(word >> 5, min_val=0, max_val=REGIONS + 1)
                act.dma_start(xd[k][:, :], disp_d[w][bass.ds(row, P), :]).then_inc(xd_loaded[k], 16)

            def load_weights(i, k):
                word = act.value_load(moe_t[0:1, bass.ds(i, 1)], min_val=0, max_val=REGIONS * 32 + 31)
                expert = act.snap((word >> 1) & (EXPERTS - 1), min_val=0, max_val=EXPERTS - 1)
                act.dma_start(w_s[k][:, :], w_cat[bass.ds(expert * P, P), :], cond=(word & 1) == 1
                              ).then_inc(w_loaded[k], 16)

            def act_turn(i, k):
                act.wait_ge(xdT_done, i + 1)
                nc.scalar.copy(xdT[k][:, :, :].rearrange("p k n -> p (k n)"), xdT_p[:, 0:2 * P]).then_inc(xdT_ready, 1)

            def act_relu(i, k):
                act.wait_ge(mm1_done, i + 1)
                for f in range(4):
                    last = nc.scalar.activation(hT[k][:, f, :], h_p[k][:, f * P:(f + 1) * P], ACT.Relu,
                                                bias=w_s[k][:, W_B1 + f:W_B1 + f + 1])
                last.then_inc(hT_ready, 1)

            def store_rows(i, k, w, j):
                act.wait_ge(yo_ready, i + 1)
                act.dma_start(moe_d[w][bass.ds(j * P, P), :], yo[k][:, :]).then_inc(yo_stored[k], 16)

            def finish_std(t):
                act.wait_ge(var2_ready, t + 1)
                nc.scalar.activation(sd_c[:, :], mv_c[:, 1:2], ACT.Sqrt, bias=eps[0:TILE, :]).then_inc(std2_ready, 1)

            def finish_send(t, warm):
                act.wait_ge(xn2_ready, t + 1)
                if warm:
                    for k in range(2):
                        act.wait_ge(sent[k], t * 16)
                nc.scalar.copy(send[:, :], pair[:, 1, :]).then_inc(send_ready, 1)
                act.wait_ge(pair_ready, t + 1)
                act.dma_start(pair_d[bass.ds(t * TILE, TILE), :], pair[:, :, :].rearrange("n a o -> n (a o)")
                              ).then_inc(pair_stored, 16)

            def finish_turn(t):
                act.wait_ge(x2T_done, t + 1)
                nc.scalar.copy(xn2T[:, :, :].rearrange("p k n -> p (k n)"), x2T_p[:, 0:2 * TILE]).then_inc(x2T_ready, 1)

            def act_tile(t, w1, w2, m, warm, last=False):
                def front(k):
                    s = RING * m + k
                    act_turn(s, k)
                    if not last:
                        load_rows(s + RING, k, 0)
                    if not (isinstance(s, int) and s < 1):
                        act_relu(s - 1, (k - 1) % RING)

                def back(k):
                    s = RING * m + k
                    if not (isinstance(s, int) and s < 2):
                        store_rows(s - 2, (k - 2) % RING, 0, s - 2)
                    if not (last and k == RING - 1):
                        load_weights(s + 1, (k + 1) % RING)

                if not last:
                    act.wait_ge(agg_open, t + 1)
                    act.dma_start(xT_c[:, :], xnT_d[bass.ds(t * P + P, P), :]).then_inc(xTc_loaded, 16)
                if w1 is None:
                    return
                if m is not None:
                    front(0)
                finish_std(t - 1)
                act.dma_start(x_c[:, :], x[bass.ds(t * TILE, TILE), :]).then_inc(xc_loaded, 16)
                finish_send(t - 1, warm)
                if m is not None:
                    back(0)
                    front(1)
                finish_turn(t - 1)
                if m is not None:
                    back(1)
                    front(2)
                    back(2)

            w1 = WAVE_START[1]
            act.wait_ge(table_ready, 1)
            act.dma_start(xT_c[:, :], xnT_d[0:P, :]).then_inc(xTc_loaded, 16)
            act.dma_start(x_c[:, :], x[0:TILE, :]).then_inc(xc_loaded, 16)
            act_tile(0, None, None, None, False)
            act_tile(1, 0, None, None, False)
            with act.Fori(2, w1 + 1) as t:
                act_tile(t, 0, 0, None, True)
            act_tile(w1 + 1, 1, 0, None, True)
            act.wait_ge(moe_table, 1)
            for k in range(2):
                act.wait_ge(sent[k], 16 * w1)
            with act.Fori(w1 + 2, MIX_FROM) as t:
                act_tile(t, 1, 1, None, True)
                for j in range(EXPERTS // GAP_TILES):
                    e = (t - (w1 + 2)) * (EXPERTS // GAP_TILES) + j
                    r = act.value_load(padr_i[0][0:1, bass.ds(e, 1)], min_val=0, max_val=REGIONS - P)
                    act.dma_start(disp_d[0][bass.ds(r, P), :], zeros[:, :]).then_inc(gaps_zeroed, 16)
            act.wait_ge(gaps_zeroed, 16 * EXPERTS)
            for k in range(RING):
                load_rows(k, k, 0)
            load_weights(0, 0)
            act_tile(MIX_FROM, 1, 1, 0, True)
            with act.Fori(MIX_FROM + 1, TILES - 1) as t:
                act_tile(t, 1, 1, t - MIX_FROM, True)
            act_tile(TILES - 1, 1, 1, ITERS_A - 1, True, last=True)
            finish_std(TILES - 1)
            finish_send(TILES - 1, True)
            finish_turn(TILES - 1)

            act.wait_ge(moe_table, 2)
            for k in range(2):
                act.wait_ge(sent[k], 16 * TILES)
            with act.Fori(0, EXPERTS) as e:
                r = act.value_load(padr_i[1][0:1, bass.ds(e, 1)], min_val=0, max_val=REGIONS - P)
                act.dma_start(disp_d[1][bass.ds(r, P), :], zeros[:, :]).then_inc(gaps_zeroed, 16)
            act.wait_ge(gap_ready, 1)
            nc.scalar.activation(wt[:, 1, :], gap[:, :], ACT.Exp).then_inc(exp_done, 1)
            nc.scalar.activation(sd_e[0][:, :], eps[0:TILE, :], ACT.Sqrt)
            act.wait_ge(gaps_zeroed, 16 * EXPERTS * WAVES)
            for k in range(RING):
                load_rows(MOE[0] + k, k, 1)
            load_weights(MOE[0], 0)

            def e_std(t, i):
                act.wait_ge(mixed, t + 1)
                nc.scalar.activation(sd_e[i][:, :], mv_e[i][:, 1:2], ACT.Sqrt, bias=eps[0:TILE, :]
                                     ).then_inc(std3_ready, 1)

            def e_scale(t, i):
                act.wait_ge(scale_ready, t + 1)
                nc.scalar.activation(z_e[i][:, :], acc_e[i][:, :], ACT.Identity, bias=nm_e[i][:, :],
                                     scale=rs_e[i][:, :]).then_inc(z_ready, 1)

            def b_iteration(m, ahead):
                for k in range(RING):
                    s = RING * m + MOE[0] + k
                    seam = isinstance(m, int) and m == 0
                    act_turn(s, k)
                    if ahead:
                        load_rows(s + RING, k, 1)
                    act_relu(s - 1, (k - 1) % RING)
                    if seam and k < 2:
                        store_rows(s - 2, (k - 2) % RING, 0, s - 2)
                    else:
                        store_rows(s - 2, (k - 2) % RING, 1, RING * m + k - 2)
                    if ahead or k < RING - 1:
                        load_weights(s + 1, (k + 1) % RING)
                    if k == 0 and not seam:
                        e_std(m - 1, 0)
                    if k == 1 and not seam:
                        e_scale(m - 1, 0)

            b_iteration(0, True)
            for k in range(RING):
                act.wait_ge(yo_stored[k], 16 * (ITERS_A + (1 if k == 0 else 0)))
            act.nop(nofuse=True).then_inc(moe_stored[0], 1)
            with act.Fori(1, ITERS_B - 1) as m:
                b_iteration(m, True)
            b_iteration(ITERS_B - 1, False)
            act_relu(MOE_ALL - 1, RING - 1)
            store_rows(MOE_ALL - 2, RING - 2, 1, MOE[1] - 2)
            store_rows(MOE_ALL - 1, RING - 1, 1, MOE[1] - 1)
            for k in range(RING):
                act.wait_ge(yo_stored[k], 16 * (ITERS_A + ITERS_B))
            act.nop(nofuse=True).then_inc(moe_stored[1], 1)
            e_std(WAVE_TILES[0] - 1, 0)
            e_scale(WAVE_TILES[0] - 1, 0)
            with act.Fori(0, WAVE_TILES[1] // 2) as m:
                for i in range(2):
                    e_std(2 * m + WAVE_START[1] + i, i)
                    e_scale(2 * m + WAVE_START[1] + i, i)
            e_std(TILES - 1, 0)
            e_scale(TILES - 1, 0)

        @block.vector
        def _(dve):
            v = nc.vector
            v.memset(src_i[96:P, :], 0).then_inc(pads_set, 1)
            v.memset(dst_i[96:P, :], NO_NODE).then_inc(pads_set, 1)
            v.memset(et_i[96:P, :], 0).then_inc(pads_set, 1)
            v.memset(nrm[96:P, :], 0.0).then_inc(pads_set, 1)
            v.memset(ones[:, :], 1.0)
            v.memset(zeros[:, :], 0.0)
            v.memset(hb[:, :], 0.0)
            v.memset(gb[:, :], 0.0)
            v.memset(eps[:, :], EPS)
            v.memset(both[:, :], 0.0)
            for w in range(WAVES):
                v.memset(seen[w][:, :], 0.0)
            v.memset(tail_meta[:, :, :], 0)
            dve.drain().then_inc(zeros_set, 1)
            v.memset(tail_meta[:, :, :].bitcast(F32)[:, :, 1], float(NO_NODE))

            dve.wait_ge(basis_loaded, 32)
            for b in range(BASES):
                for r in range(RELS):
                    c = comp_s[:, r * BASES + b:r * BASES + b + 1]
                    if b == 0:
                        v.tensor_scalar(w_rel[:, :, r, :], bas[:, b, :, :], c, None, ALU.mult)
                    else:
                        v.scalar_tensor_tensor(w_rel[:, :, r, :], bas[:, b, :, :], c, w_rel[:, :, r, :],
                                               ALU.mult, ALU.add)
                dve.drain()
            dve.drain().then_inc(w_ready, 1)

            dve.wait_ge(edges_loaded, 128)
            v.scalar_tensor_tensor(meta[:, :, 0], src_i[:, :], float(RELS), et_i[:, :], ALU.mult, ALU.add)
            v.tensor_copy(meta_f[:, :, 1], dst_i[:, :])
            dve.drain().then_inc(meta_built, 1)

            def dve_x(t, i):
                dve.wait_ge(x_loaded[i], (t // 2 + 1) * 16)
                v.bn_stats(st[i][:, :], xin[i][:, :])
                dve.drain()
                v.bn_aggr(mv[i][:, :], st[i][:, :]).then_inc(var_ready, 1)

            def dve_xn(t, i):
                dve.wait_ge(std_ready, t + 1)
                v.reciprocal(rs[i][:, :], sd[i][:, :])
                dve.drain()
                v.tensor_scalar(xn[i][:, :], xin[i][:, :], mv[i][:, 0:1], rs[i][:, :], ALU.subtract, ALU.mult
                                ).then_inc(xn_ready, 1)

            def dve_out(t, i, warm):
                if warm:
                    dve.wait_ge(h_stored[i], (t // 2) * 16)
                for j in (1, 3):
                    dve.wait_ge(h_done, 4 * t + j + 1)
                    v.tensor_copy(hr[i][:, j * 512:(j + 1) * 512], bank[j][0:TILE, :]).then_inc(h_out_dve, 1)

            def edge_ranges():
                v.tensor_reduce(bmin[:, :], meta_f[:, :, 1].rearrange("p (b e) -> p b e", e=BLOCK), AX.X, ALU.min)
                v.tensor_reduce(bmax[:, :], meta_f[:, :, 1].rearrange("p (b e) -> p b e", e=BLOCK), AX.X, ALU.max)
                dve.wait_ge(pool_const, 1)
                dve.drain()
                t_b = tlo[:, :].unsqueeze(2).to_broadcast([P, TILES, BLOCKS])
                v.tensor_tensor(candA[:, :, :], bmax[:, :].unsqueeze(1).to_broadcast([P, TILES, BLOCKS]), t_b,
                                ALU.is_ge)
                v.tensor_tensor(candB[:, :, :], bmin[:, :].unsqueeze(1).to_broadcast([P, TILES, BLOCKS]), t_b,
                                ALU.subtract)
                dve.drain()
                v.scalar_tensor_tensor(candA[:, :, :], candB[:, :, :], TILE - 0.5, candA[:, :, :], ALU.is_lt, ALU.mult)
                dve.drain()
                v.tensor_tensor(candB[:, :, :], candA[:, :, :],
                                bidr[:, :].unsqueeze(1).to_broadcast([P, TILES, BLOCKS]), ALU.mult)
                dve.drain()
                v.tensor_reduce(ends[:, 0:TILES], candB[:, :, :], AX.X, ALU.max)
                dve.drain()
                v.tensor_tensor(candB[:, :, :], candA[:, :, :],
                                bid[:, :].unsqueeze(1).to_broadcast([P, TILES, BLOCKS]), ALU.mult)
                dve.drain()
                v.tensor_reduce(ends[:, TILES:2 * TILES], candB[:, :, :], AX.X, ALU.max).then_inc(ends_ready, 1)
                dve.wait_ge(ends_turned, 1)
                v.tensor_reduce(ends1[:, :], bank[6][0:2 * TILES, 0:P], AX.X, ALU.max).then_inc(ends_max, 1)
                dve.wait_ge(ends_back, 1)
                v.tensor_copy(er[:, :], bank[7][0:1, 0:2 * TILES])
                dve.drain()
                v.tensor_scalar(has[:, :], er[:, 0:TILES], 0.5, None, ALU.is_ge)
                v.tensor_scalar(fst[:, :], er[:, 0:TILES], -1.0, BIG, ALU.mult, ALU.add)
                dve.drain()
                v.tensor_tensor(fst[:, :], fst[:, :], has[:, :], ALU.mult)
                dve.drain()
                v.tensor_scalar(start_t[:, :], fst[:, :], float(BLOCK), None, ALU.mult)
                v.tensor_tensor(rnf[:, :], er[:, TILES:2 * TILES], fst[:, :], ALU.subtract)
                dve.drain()
                v.tensor_scalar(rni[:, :], rnf[:, :], float(ROUND // BLOCK - 1), None, ALU.add)
                dve.drain()
                v.tensor_scalar(rni[:, :], rni[:, :], (ROUND // BLOCK).bit_length() - 1, None,
                                ALU.arith_shift_right)
                dve.drain()
                v.tensor_scalar(rounds_t[:, :], rni[:, :], float(MIN_ROUNDS), None, ALU.max)
                dve.drain().then_inc(ranges_ready, 1)

            dve_x(0, 0)
            dve_xn(0, 0)
            dve_x(1, 1)
            dve_xn(1, 1)
            edge_ranges()
            dve_out(0, 0, False)
            dve_x(2, 0)
            dve_xn(2, 0)
            dve_out(1, 1, False)
            with dve.Fori(1, TILES // 2 - 1) as m:
                for i in range(2):
                    t = 2 * m + i
                    dve_x(t + 1, 1 - i)
                    dve_xn(t + 1, 1 - i)
                    dve_out(t, i, True)
            dve_x(TILES - 1, 1)
            dve_xn(TILES - 1, 1)
            dve_out(TILES - 2, 0, True)
            dve_out(TILES - 1, 1, True)

            rnd = dve.alloc_register("rnd_dve")
            dve.reg_mov(rnd, 0)

            def one_hots(q, u1):
                dve.wait_ge(meta_loaded[q], u1 * 16)
                for c in range(CHUNKS):
                    last = v.tensor_scalar(hot[q][:, c, :], iota_n[:, :], m_f[q][:, 3 * c + 1:3 * c + 2],
                                           m_f[q][:, 3 * c + 2:3 * c + 3], ALU.is_equal, ALU.mult)
                last.then_inc(hot_ready[q], 1)

            def residual(t, warm):
                dve.wait_ge(agg_done, t + 1)
                dve.wait_ge(xc_loaded, (t + 1) * 16)
                if warm:
                    dve.wait_ge(pair_stored, t * 16)
                v.scalar_tensor_tensor(pair[:, 0, :], agg[0:TILE, 0:D], 0.0, x_c[:, :], ALU.max, ALU.add
                                       ).then_inc(agg_read, 1)
                dve.drain()
                v.bn_stats(st_c[:, :], pair[:, 0, :])
                dve.drain()
                v.bn_aggr(mv_c[:, :], st_c[:, :]).then_inc(var2_ready, 1)

            def norm2(t):
                dve.wait_ge(std2_ready, t + 1)
                v.reciprocal(rs_c[:, :], sd_c[:, :])
                dve.drain()
                v.tensor_scalar(pair[:, 1, :], pair[:, 0, :], mv_c[:, 0:1], rs_c[:, :], ALU.subtract, ALU.mult
                                ).then_inc(xn2_ready, 1)
                dve.drain()
                v.tensor_tensor(pair[:, 0, :], pair[:, 0, :], bet[0:TILE, :], ALU.add).then_inc(pair_ready, 1)

            def pick(t):
                dve.wait_ge(logits_done, t + 1)
                v.tensor_copy(lg[:, :], lg_p[0:TILE, 0:EXPERTS])
                dve.drain()
                v.max(top[:, :], lg[:, :])
                dve.drain()
                v.max_index(topi[:, :], top[:, :], lg[:, :])
                v.tensor_tensor(gap[:, bass.ds(t, 1)], top[:, 1:2], top[:, 0:1], ALU.subtract)
                dve.drain()
                v.tensor_copy(topf[:, :], topi[:, 0:2])
                dve.drain()
                v.tensor_tensor(oh[:, :, :], iota_e[0:TILE, :].unsqueeze(1).to_broadcast([TILE, 2, EXPERTS]),
                                topf[:, :].unsqueeze(2).to_broadcast([TILE, 2, EXPERTS]), ALU.is_equal)
                dve.drain()
                v.tensor_tensor(both[0:TILE, :], oh[:, 0, :], oh[:, 1, :], ALU.add).then_inc(both_ready, 1)

            def place(t, w, warm):
                dve.wait_ge(rank_done, t + 1)
                if warm:
                    for k in range(2):
                        dve.wait_ge(sent[k], t * 16)
                v.tensor_tensor(slf[:, :], rank_p[0:TILE, 32:32 + EXPERTS], region[0:TILE, :], ALU.add)
                v.tensor_tensor(seen[w][0:TILE, :], seen[w][0:TILE, :], both[0:TILE, :], ALU.add)
                dve.drain()
                v.tensor_tensor(slx[:, :, :], oh[:, :, :], slf[:, :].unsqueeze(1).to_broadcast([TILE, 2, EXPERTS]),
                                ALU.mult)
                dve.drain()
                v.tensor_reduce(slot_f[:, :], slx[:, :, :], AX.X, ALU.add)
                dve.drain()
                v.tensor_copy(slot_all[:, bass.ds(t * 2, 2)], slot_f[:, :])
                v.tensor_copy(expert_all[:, bass.ds(t * 2, 2)], topf[:, :])
                v.tensor_copy(slots[:, :], slot_f[:, :]).then_inc(slots_ready, 1)

            def add_b2(i, k, warm, uses=0):
                dve.wait_ge(mm2_done, i + 1)
                if warm:
                    dve.wait_ge(yo_stored[k], uses * 16)
                v.tensor_tensor(yo[k][:, :], y_p[:, 0:D], w_s[k][:, W_B2:W_B2 + D], ALU.add).then_inc(yo_ready, 1)

            def expert_table(w):
                n, at = MOE[w], w * MOE[0]
                dve.wait_ge(count_done, w + 1)
                v.tensor_copy(cnt[:, :], rank_p[0:TILE, 64 + 32 * w:64 + 32 * w + EXPERTS])
                dve.drain()
                v.tensor_tensor(padr_i[w][:, :], cnt[:, :], region[0:TILE, :], ALU.add)
                v.tensor_scalar(cnt_i[:, :], cnt[:, :], float(P - 1), None, ALU.add)
                dve.drain()
                v.tensor_scalar(nt_i[:, :], cnt_i[:, :], P.bit_length() - 1, None, ALU.arith_shift_right)
                dve.drain()
                v.tensor_copy(nt_f[:, :], nt_i[:, :])
                dve.drain()
                v.tensor_tensor_scan(cum[:, :], ones[0:TILE, 0:EXPERTS], nt_f[:, :], 0.0, ALU.mult, ALU.add)
                v.tensor_scalar(step[:, :], nt_f[:, :], -float(P), float(CAP), ALU.mult, ALU.add)
                dve.drain()
                shape = [1, n, EXPERTS]
                v.tensor_tensor(past[:, 0:n, :], iota_m[:, 0:n].unsqueeze(2).to_broadcast(shape),
                                cum[0:1, :].unsqueeze(1).to_broadcast(shape), ALU.is_ge)
                dve.drain()
                v.tensor_reduce(e_f[:, 0:n], past[:, 0:n, :], AX.X, ALU.add)
                v.tensor_tensor(past2[:, 0:n, :], past[:, 0:n, :], step[0:1, :].unsqueeze(1).to_broadcast(shape),
                                ALU.mult)
                dve.drain()
                v.tensor_reduce(r_f[:, 0:n], past2[:, 0:n, :], AX.X, ALU.add)
                v.tensor_scalar(e_f[:, 0:n], e_f[:, 0:n], float(EXPERTS - 1), None, ALU.min)
                v.memset(new_f[:, 0:RING], 1.0)
                dve.drain()
                v.scalar_tensor_tensor(r_f[:, 0:n], iota_m[:, 0:n], float(P), r_f[:, 0:n], ALU.mult, ALU.add)
                v.tensor_tensor(new_f[:, RING:n], e_f[:, RING:n], e_f[:, 0:n - RING], ALU.not_equal)
                dve.drain()
                v.tensor_scalar(r_f[:, 0:n], r_f[:, 0:n], float(REGIONS), 16.0, ALU.min, ALU.mult)
                dve.drain()
                v.tensor_tensor(r_f[:, 0:n], r_f[:, 0:n], e_f[:, 0:n], ALU.add)
                dve.drain()
                v.scalar_tensor_tensor(moe_t[:, at:at + n], r_f[:, 0:n], 2.0, new_f[:, 0:n], ALU.mult, ALU.add)
                dve.drain().then_inc(moe_table, 1)

            def expert_rows(w):
                a, b = 2 * WAVE_START[w], 2 * (WAVE_START[w] + WAVE_TILES[w])
                v.tensor_tensor(shift0[:, :], cum[:, :], nt_f[:, :], ALU.subtract)
                dve.drain()
                v.scalar_tensor_tensor(shift[:, :], shift0[:, :], float(P), region[0:TILE, :], ALU.mult, ALU.subtract)
                dve.drain()
                for e in range(EXPERTS):
                    v.tensor_scalar(shifted[e % 2][:, a:b], expert_all[:, a:b], float(e), shift[:, e:e + 1],
                                    ALU.is_equal, ALU.mult)
                    dve.drain()
                    v.tensor_tensor(slot_all[:, a:b], slot_all[:, a:b], shifted[e % 2][:, a:b], ALU.add)
                dve.drain()
                v.tensor_copy(moe_row[:, a:b], slot_all[:, a:b])

            def dve_tile(t, w1, w2, m, warm):
                dve.drain()
                v.tensor_scalar(iota_n[:, :], iota_n[:, :], float(TILE), None, ALU.add)
                dve.drain()
                tables = isinstance(t, int) and t == WAVE_START[1] + 1
                warm_yo = not (isinstance(m, int) and m == 0)

                def between(p):
                    if w1 is not None:
                        if p == 1:
                            residual(t - 1, warm)
                        if p == 2:
                            norm2(t - 1)
                        if p == 6:
                            pick(t - 1)
                    if m is not None and warm_yo:
                        if p == 3:
                            add_b2(RING * m - 2, 1, not first_uses(m), m - 1)
                        if p == 5:
                            add_b2(RING * m - 1, 2, not first_uses(m), m - 1)
                    if tables and p == 3:
                        expert_table(0)
                    if tables and p == 5:
                        expert_rows(0)

                tile_rounds(dve, rnd, t, one_hots, between)
                if w1 is not None:
                    place(t - 1, w1, warm)
                if m is not None:
                    add_b2(RING * m, 0, warm_yo, m)

            def first_uses(m):
                return isinstance(m, int) and m <= 1

            dve.wait_ge(const_loaded, 96)
            all_tiles(dve, dve_tile, peel=True)
            residual(TILES - 1, True)
            norm2(TILES - 1)
            pick(TILES - 1)
            place(TILES - 1, 1, True)
            dve.drain().then_inc(gap_ready, 1)
            expert_table(1)
            expert_rows(1)

            dve.wait_ge(exp_done, 1)
            v.tensor_scalar(wden[:, :], wt[:, 1, :], 1.0, None, ALU.add)
            dve.drain()
            v.reciprocal(wt[:, 0, :], wden[:, :])
            dve.drain()
            v.tensor_tensor(wt[:, 1, :], wt[:, 1, :], wt[:, 0, :], ALU.mult)

            def ready_slots(t, i):
                dve.drain()
                v.tensor_copy(sl_e[i][:, :], moe_row[:, bass.ds(t * 2, 2)]).then_inc(sl_ready, 1)

            def mix(t, i, use):
                for k in range(2):
                    dve.wait_ge(y_loaded[i][k], (use + 1) * 16)
                dve.wait_ge(pr_loaded[i], (use + 1) * 16)
                v.scalar_tensor_tensor(acc_e[i][:, :], y_e[i][0][:, :], wt[:, 0, bass.ds(t, 1)], pr_e[i][:, 1, :],
                                       ALU.mult, ALU.add)
                dve.drain()
                v.scalar_tensor_tensor(acc_e[i][:, :], y_e[i][1][:, :], wt[:, 1, bass.ds(t, 1)], acc_e[i][:, :],
                                       ALU.mult, ALU.add)
                dve.drain()
                v.bn_stats(st_e[i][:, :], acc_e[i][:, :])
                dve.drain()
                v.bn_aggr(mv_e[i][:, :], st_e[i][:, :]).then_inc(mixed, 1)

            def scales(t, i):
                dve.wait_ge(std3_ready, t + 1)
                v.reciprocal(rs_e[i][:, :], sd_e[i][:, :])
                dve.drain()
                v.scalar_tensor_tensor(nm_e[i][:, :], mv_e[i][:, 0:1], -1.0, rs_e[i][:, :], ALU.mult, ALU.mult
                                       ).then_inc(scale_ready, 1)

            def emit(t, i, use):
                dve.wait_ge(z_ready, t + 1)
                v.tensor_tensor(z_e[i][:, :], z_e[i][:, :], gam[0:TILE, :], ALU.mult)
                dve.drain()
                if not (isinstance(use, int) and use == 0):
                    dve.wait_ge(o_stored[i], use * 16)
                v.tensor_tensor(o_e[i][:, :], z_e[i][:, :], pr_e[i][:, 0, :], ALU.add).then_inc(o_ready, 1)

            def b_iteration(m):
                seam = isinstance(m, int) and m == 0
                for k in range(RING):
                    buf = (k - 2) % RING
                    add_b2(RING * m + MOE[0] + k - 2, buf, True, m + ITERS_A + (0 if k == 2 else -1))
                    if not seam:
                        if k == 0:
                            mix(m - 1, 0, m - 1)
                            ready_slots(m, 0)
                        if k == 1:
                            scales(m - 1, 0)
                        if k == 2:
                            emit(m - 1, 0, m - 1)

            ready_slots(0, 0)
            b_iteration(0)
            b_iteration(1)
            with dve.Fori(2, ITERS_B) as m:
                b_iteration(m)
            assert WAVE_TILES[0] == ITERS_B
            add_b2(MOE_ALL - 2, RING - 2, True, ITERS_A + ITERS_B - 1)
            add_b2(MOE_ALL - 1, RING - 1, True, ITERS_A + ITERS_B - 1)
            t0, u0 = WAVE_START[1], WAVE_TILES[0]
            mix(t0 - 1, 0, u0 - 1)
            ready_slots(t0, 0)
            ready_slots(t0 + 1, 1)
            scales(t0 - 1, 0)
            emit(t0 - 1, 0, u0 - 1)

            def two_tiles(m, ahead):
                mix(t0 + 1 + 2 * m, 1, m)
                if ahead:
                    ready_slots(t0 + 3 + 2 * m, 1)
                emit(t0 + 2 * m, 0, u0 + m)
                scales(t0 + 1 + 2 * m, 1)
                mix(t0 + 2 + 2 * m, 0, u0 + m + 1)
                if ahead:
                    ready_slots(t0 + 4 + 2 * m, 0)
                emit(t0 + 1 + 2 * m, 1, m)
                scales(t0 + 2 + 2 * m, 0)

            mix(t0, 0, u0)
            ready_slots(t0 + 2, 0)
            scales(t0, 0)
            two_tiles(0, True)
            with dve.Fori(1, WAVE_TILES[1] // 2 - 1) as m:
                two_tiles(m, True)
            two_tiles(WAVE_TILES[1] // 2 - 1, False)
            emit(TILES - 1, 0, E_USES[0] - 1)

        @block.tensor
        def _(pe):
            mm = nc.tensor.matmul

            def turn(dst_p, rows_, n):
                for k in range(2):
                    last = nc.tensor.transpose(dst_p[:, k * n:(k + 1) * n], rows_[:, k * P:(k + 1) * P],
                                               ident[0:n, 0:n])
                return last

            pe.wait_ge(pool_const, 1)

            def pe_turn(t, i):
                pe.wait_ge(xn_ready, t + 1)
                turn(bank[4 + i], xn[i], TILE).then_inc(xnT_done, 1)

            def pe_h(t, i, warm):
                pe.wait_ge(xnT_ready, t + 1)
                for j in range(4):
                    if warm and j in (0, 2):
                        pe.wait_ge(h_out_act, 2 * t - 1 + j // 2)
                    if warm and j in (1, 3):
                        pe.wait_ge(h_out_dve, 2 * t - 1 + j // 2)
                    for k in range(2):
                        last = mm(bank[j][0:TILE, :], xnT[i][:, k, :],
                                  w_rel[:, k, 2 * j:2 * j + 2, :].rearrange("p r o -> p (r o)"),
                                  start=(k == 0), stop=(k == 1))
                    last.then_inc(h_done, 1)

            pe_turn(0, 0)
            pe.wait_ge(w_ready, 1)
            pe_turn(1, 1)
            pe_h(0, 0, False)
            pe.wait_ge(ends_ready, 1)
            nc.tensor.transpose(bank[6][0:2 * TILES, 0:P], ends[:, :], ident[:, :]).then_inc(ends_turned, 1)
            pe.wait_ge(ends_max, 1)
            nc.tensor.transpose(bank[7][0:1, 0:2 * TILES], ends1[:, :], ident[0:2 * TILES, 0:2 * TILES]
                                ).then_inc(ends_back, 1)
            pe_turn(2, 0)
            pe_h(1, 1, True)
            with pe.Fori(1, TILES // 2 - 1) as m:
                for i in range(2):
                    pe_turn(2 * m + i + 1, 1 - i)
                    pe_h(2 * m + i, i, True)
            pe_turn(TILES - 1, 1)
            pe_h(TILES - 2, 0, True)
            pe_h(TILES - 1, 1, True)

            for q in range(PHASES):
                pe.nop(nofuse=True).then_inc(phase_free[q], 1)
            pe.wait_ge(zeros_set, 1)
            pe.wait_ge(const_loaded, 96)
            pe.wait_ge(ranges_ready, 1)
            pe.wait_ge(h_out_act, 2 * TILES)
            pe.wait_ge(h_out_dve, 2 * TILES)
            rnd = pe.alloc_register("rnd_pe")
            pe.reg_mov(rnd, 0)

            def sum_round(q, u1):
                pe.wait_ge(hot_ready[q], u1)
                for c in range(CHUNKS):
                    pe.wait_ge(gathered[q][c], u1 * 16)
                    last = mm(agg[0:TILE, 0:D], hot[q][:, c, :], rows[q][c][:, :], start=False, stop=False)
                last.then_inc(phase_free[q], 1)

            def turn2(t):
                pe.wait_ge(xn2_ready, t + 1)
                turn(x2T_p, pair[:, 1, :], TILE).then_inc(x2T_done, 1)

            def logits(t):
                pe.wait_ge(x2T_ready, t + 1)
                for k in range(2):
                    mm(lg_p[0:TILE, 0:EXPERTS], xn2T[:, k, :], gw[:, k, :], start=(k == 0), stop=False)
                mm(lg_p[0:TILE, 0:EXPERTS], row0[:, 0:TILE], gb[:, :], start=False, stop=True).then_inc(logits_done, 1)

            def rank(t, w):
                pe.wait_ge(both_ready, t + 1)
                mm(rank_p[0:TILE, 32:32 + EXPERTS], ones[:, 0:TILE], seen[w][:, :], start=True, stop=False)
                mm(rank_p[0:TILE, 32:32 + EXPERTS], before[:, 0:TILE], both[:, :], start=False, stop=True
                   ).then_inc(rank_done, 1)

            def count(w):
                pe.wait_ge(slots_ready, WAVE_START[w] + WAVE_TILES[w])
                mm(rank_p[0:TILE, 64 + 32 * w:64 + 32 * w + EXPERTS], ones[:, 0:TILE], seen[w][:, :],
                   start=True, stop=True).then_inc(count_done, 1)

            def turn_rows(i, k, use):
                pe.wait_ge(xd_loaded[k], (use + 1) * 16)
                if not (isinstance(i, int) and i == 0):
                    pe.wait_ge(xdT_ready, i)
                turn(xdT_p, xd[k], P).then_inc(xdT_done, 1)

            def up(i, k, use):
                pe.wait_ge(xdT_ready, i + 1)
                pe.wait_ge(w_loaded[k], (use + 1) * 16)
                for f in range(4):
                    for kk in range(2):
                        last = mm(h_p[k][:, f * P:(f + 1) * P], w_s[k][:, kk * FF + f * P:kk * FF + (f + 1) * P],
                                  xdT[k][:, kk, :], start=(kk == 0), stop=(kk == 1))
                last.then_inc(mm1_done, 1)

            def down(i, k):
                pe.wait_ge(hT_ready, i + 1)
                if not (isinstance(i, int) and i == 0):
                    pe.wait_ge(yo_ready, i)
                for f in range(4):
                    last = mm(y_p[:, 0:D], hT[k][:, f, :], w_s[k][:, 2 * FF + f * D:2 * FF + (f + 1) * D],
                              start=(f == 0), stop=(f == 3))
                last.then_inc(mm2_done, 1)

            def step_front(m, k):
                s = RING * m + k
                turn_rows(s, k, m)
                if not (isinstance(s, int) and s < 1):
                    up(s - 1, (k - 1) % RING, m if k else m - 1)

            def step_back(m, k):
                s = RING * m + k
                if not (isinstance(s, int) and s < 2):
                    down(s - 2, (k - 2) % RING)

            def pe_tile(t, w1, w2, m, warm):
                pe.wait_ge(xTc_loaded, (t + 1) * 16)
                if w1 is not None:
                    pe.wait_ge(agg_read, t)
                for k in range(2):
                    last = mm(agg[0:TILE, 0:D], xT_c[:, k * TILE:(k + 1) * TILE], lw[:, k, :],
                              start=(k == 0), stop=False)
                last.then_inc(agg_open, 1)

                def between(p):
                    if m is not None:
                        if p in (0, 2, 4):
                            step_front(m, p // 2)
                        if p in (1, 3, 5):
                            step_back(m, p // 2)
                    if w1 is not None:
                        if p == 3:
                            turn2(t - 1)
                        if p == 4:
                            logits(t - 1)
                        if p == 6:
                            rank(t - 1, w1)
                    if p == 0 and isinstance(t, int) and t == WAVE_START[1] + 1:
                        count(0)

                tile_rounds(pe, rnd, t, sum_round, between)
                mm(agg[0:TILE, 0:D], row0[:, 0:TILE], hb[:, :], start=False, stop=True).then_inc(agg_done, 1)

            all_tiles(pe, pe_tile)
            turn2(TILES - 1)
            logits(TILES - 1)
            rank(TILES - 1, 1)
            count(1)
            with pe.Fori(ITERS_A, ITERS_A + ITERS_B) as m:
                for k in range(RING):
                    step_front(m, k)
                    step_back(m, k)
            up(MOE_ALL - 1, RING - 1, ITERS_A + ITERS_B - 1)
            down(MOE_ALL - 2, RING - 2)
            down(MOE_ALL - 1, RING - 1)


def kernel(x, src, dst, edge_type_8, edge_weight1, L0_gnn_weight, L0_gnn_w_comp, L0_gnn_loop_weight, L0_gnn_h_bias,
           L0_ffn_gate_w, L0_ffn_gate_b, L0_ffn_w1, L0_ffn_b1, L0_ffn_w2, L0_ffn_b2, L0_ffn_gamma, L0_ffn_beta):
    import numpy as np
    import concourse.bacc as bacc
    from concourse.bass_utils import run_bass_kernel_spmd

    def rows(a, parts):
        a = np.asarray(a)
        return a.reshape(EXPERTS, parts, P, -1).transpose(0, 2, 1, 3).reshape(EXPERTS, P, -1)

    b2_rows = np.broadcast_to(np.asarray(L0_ffn_b2)[:, None, :], (EXPERTS, P, D))
    w_cat = np.concatenate([rows(L0_ffn_w1, 2), rows(L0_ffn_w2, 4), rows(L0_ffn_b1, 4), b2_rows], axis=2)
    arrays = {
        "x_in": x, "src_in": src, "dst_in": dst, "etype_in": edge_type_8,
        "eweight_in": np.asarray(edge_weight1).reshape(N_EDGES), "basis_in": L0_gnn_weight, "comp_in": L0_gnn_w_comp,
        "loop_in": L0_gnn_loop_weight, "hbias_in": L0_gnn_h_bias, "gatew_in": L0_ffn_gate_w, "gateb_in": L0_ffn_gate_b,
        "wcat_in": w_cat.reshape(EXPERTS * P, W_COLS), "gamma_in": L0_ffn_gamma,
        "beta_in": L0_ffn_beta,
    }
    arrays = {k: np.ascontiguousarray(np.asarray(a)) for k, a in arrays.items()}
    nc = bacc.Bacc("TRN2", target_bir_lowering=False, num_devices=1)
    args = [nc.dram_tensor(k, a.shape, mybir.dt.from_np(a.dtype), kind="ExternalInput").ap() for k, a in arrays.items()]
    out = nc.dram_tensor("out_x", (N_NODES, D), F32, kind="ExternalOutput").ap()
    build(nc, *args, out)
    r = run_bass_kernel_spmd(nc, [arrays], core_ids=[0])
    return r.results[0]["out_x"]
```

```python
from contextlib import ExitStack

import concourse.bass as bass
from concourse import mybir

F32 = mybir.dt.float32
I32 = mybir.dt.int32
U32 = mybir.dt.uint32
ALU = mybir.AluOpType
ACT = mybir.ActivationFunctionType
AX = mybir.AxisListType

N_NODES = 6250
N_EDGES = 106250
D = 256
RELS = 8
BASES = 4
EXPERTS = 16
FF = 512
EPS = 1e-5
P = 128

TILE = 125
TILES = N_NODES // TILE
assert TILE * TILES == N_NODES

GROUPS = -(-N_EDGES // (P * P))
CHUNKS_PAD = GROUPS * P
FULL_CHUNKS = N_EDGES // P
NO_NODE = N_NODES + TILE - 1
BIG = float(CHUNKS_PAD)
TURNED = 4
B_FROM = 10
TURN_FROM = 2
ENDS_AT = TURN_FROM + 6
ROUNDS = 8
CHUNKS = [2] * (ROUNDS - 1) + [1]
HEAD = sum(CHUNKS)
HALF = 8
PAD_CHUNK = CHUNKS_PAD - 1
MAX_REST = CHUNKS_PAD
assert FULL_CHUNKS + 1 + 2 * HALF <= PAD_CHUNK and sum(CHUNKS[:ROUNDS // 2]) == HALF

WAVES = 2
WAVE_TILES = [23, 27]
WAVE_START = [0, 23]
assert sum(WAVE_TILES) == TILES
CAP = (-(-max(WAVE_TILES) * TILE // P) + 1) * P
REGIONS = EXPERTS * CAP
RING = 3
MIX_FROM = 29
GAP_TILES = 4
MOE = [RING * (TILES - MIX_FROM),
       -(-((2 * WAVE_TILES[1] * TILE + EXPERTS * (P - 1)) // P) // RING) * RING]
assert MOE[0] >= (2 * WAVE_TILES[0] * TILE + EXPERTS * (P - 1)) // P
MOE_ALL = sum(MOE)
ITERS_A = MOE[0] // RING
ITERS_B = MOE[1] // RING
assert WAVE_TILES[0] <= ITERS_B
E_BUFS = 4
E_FIRST = WAVE_TILES[0] - 1
E_PAIRS = (TILES - E_FIRST) // 2
assert E_FIRST + 2 * E_PAIRS == TILES and E_PAIRS % 2 == 0
W1_COLS = 2 * FF + 4
W2_COLS = 4 * D + D
LOGITS_AT, RANK_AT, COUNT_AT = 256, 288, 320
BANK = 512


def build(nc, x, src, dst, etype, eweight, basis, comp, loop_w, h_bias, gate_w, gate_b, w1_cat, w2_cat,
          gamma, beta, out):
    ctx = ExitStack()
    with ctx:
        def sb(name, shape, dt=F32):
            return ctx.enter_context(nc.sbuf_tensor(name, shape, dt))

        def sem(name):
            return ctx.enter_context(nc.semaphore(name))

        def dram(name, shape, dt=F32):
            return nc.dram_tensor(name, shape, dt).ap()

        idx_d = dram("idx_d", (P, CHUNKS_PAD), I32)
        h_d = dram("h_d", (N_NODES * RELS, D))
        xnT_d = dram("xnT_d", (TILES * P, 2 * TILE))
        pair_d = dram("pair_d", (N_NODES, 2 * D))
        disp_d = [dram(f"disp{w}_d", (REGIONS + P + 1, D)) for w in range(WAVES)]
        moe_d = [dram(f"moe{w}_d", (MOE[w] * P, D)) for w in range(WAVES)]

        ident = sb("ident", [P, P])
        ones = sb("ones", [P, P])
        row0 = sb("row0", [P, P])
        before = sb("before", [P, P])
        zeros = sb("zeros", [P, D])
        iota_n = sb("iota_n", [P, TILE])
        iota_e = sb("iota_e", [P, EXPERTS])
        region = sb("region", [P, EXPERTS])
        hb = sb("hb", [P, D])
        gb = sb("gb", [P, EXPERTS])
        gw = sb("gw", [P, 2, EXPERTS])
        lw = sb("lw", [P, 2, D])
        eps = sb("eps", [P, 1])
        gam = sb("gam", [P, D])
        bet = sb("bet", [P, D])

        src_i, dst_i, et_i = [sb(n, [P, GROUPS, P], I32) for n in ("src_i", "dst_i", "et_i")]
        nrm = sb("nrm", [P, GROUPS, P])
        idx_f = sb("idx_f", [P, GROUPS, P])
        dst_f = sb("dst_f", [P, GROUPS, P])
        idx_all = sb("idx_all", [P, CHUNKS_PAD], I32)
        dw_all = sb("dw_all", [P, CHUNKS_PAD, 2])
        cmin = sb("cmin", [P, GROUPS])
        cmax = sb("cmax", [P, GROUPS])
        cid = sb("cid", [P, GROUPS])
        cidr = sb("cidr", [P, GROUPS])
        tlo = sb("tlo", [P, TILES])
        candA = sb("candA", [P, TILES, GROUPS])
        candB = sb("candB", [P, TILES, GROUPS])
        ends = sb("ends", [P, 2 * TILES])
        ends1 = sb("ends1", [2 * TILES, 1])
        er = sb("er", [1, 2 * TILES])
        has = sb("has", [1, TILES])
        fst = sb("fst", [1, TILES])
        rnf = sb("rnf", [1, TILES])
        start_t = sb("start_t", [1, TILES], I32)
        rest_t = sb("rest_t", [1, TILES], I32)
        seam_t = sb("seam_t", [1, TILES - 1], I32)
        nxt = sb("nxt", [1, TILES - 1])
        seam = sb("seam", [1, TILES])

        comp_s = sb("comp_s", [P, RELS * BASES])
        bas = sb("bas", [P, BASES, 2, D])
        w_rel = sb("w_rel", [P, 2, RELS, D])
        xin = [sb(f"xin{i}", [TILE, D]) for i in range(2)]
        st = [sb(f"st{i}", [TILE, 6]) for i in range(2)]
        mv = [sb(f"mv{i}", [TILE, 2]) for i in range(2)]
        sd = [sb(f"sd{i}", [TILE, 1]) for i in range(2)]
        rs = [sb(f"rs{i}", [TILE, 1]) for i in range(2)]
        xn = [sb(f"xn{i}", [TILE, D]) for i in range(2)]
        xnT = [sb(f"xnT{i}", [P, 2, TILE]) for i in range(2)]
        hr = [sb(f"hr{i}", [TILE, RELS * D]) for i in range(2)]

        idx_h = [sb(f"idx_h{h}", [P, HALF], I32) for h in range(2)]
        idx_r = [sb(f"idx_r{b}", [P, 2], I32) for b in range(2)]
        dw_h = sb("dw_h", [P, HEAD, 2])
        dw_r = sb("dw_r", [P, 2])
        rows = [[sb(f"rows{p}_{c}", [P, D]) for c in range(CHUNKS[p])] for p in range(ROUNDS)]
        hot = [sb(f"hot{p}", [P, CHUNKS[p], TILE]) for p in range(ROUNDS)]
        rows_r = [sb(f"rows_r{b}", [P, D]) for b in range(2)]
        hot_r = [sb(f"hot_r{b}", [P, TILE]) for b in range(2)]
        dw_m = sb("dw_m", [P, 2])
        hot_m = sb("hot_m", [P, TILE])
        x_c = sb("x_c", [TILE, D])
        xT_c = sb("xT_c", [P, 2 * TILE])
        pair = sb("pair", [TILE, 2, D])
        st_c = sb("st_c", [TILE, 6])
        mv_c = sb("mv_c", [TILE, 2])
        sd_c = sb("sd_c", [TILE, 1])
        rs_c = sb("rs_c", [TILE, 1])
        send = sb("send", [TILE, D])
        xn2T = sb("xn2T", [P, 2, TILE])
        lg = sb("lg", [TILE, EXPERTS])
        top = sb("top", [TILE, 8])
        topi = sb("topi", [TILE, 8], U32)
        topf = sb("topf", [TILE, 2])
        oh = sb("oh", [TILE, 2, EXPERTS])
        both = sb("both", [P, EXPERTS])
        seen = [sb(f"seen{w}", [P, EXPERTS]) for w in range(WAVES)]
        slf = sb("slf", [TILE, EXPERTS])
        slx = sb("slx", [TILE, 2, EXPERTS])
        slot_f = sb("slot_f", [TILE, 2])
        slots = sb("slots", [TILE, 2], I32)
        slot_all = sb("slot_all", [TILE, 2 * TILES])
        expert_all = sb("expert_all", [TILE, 2 * TILES])
        moe_row = sb("moe_row", [TILE, 2 * TILES], I32)
        shifted = [sb(f"shifted{i}", [TILE, 2 * TILES]) for i in range(2)]
        shift = sb("shift", [TILE, EXPERTS])
        shift0 = sb("shift0", [TILE, EXPERTS])
        gap = sb("gap", [TILE, TILES])

        cnt = sb("cnt", [TILE, EXPERTS])
        cnt_i = sb("cnt_i", [TILE, EXPERTS], I32)
        padr_i = [sb(f"padr_i{w}", [TILE, EXPERTS], I32) for w in range(WAVES)]
        nt_i = sb("nt_i", [TILE, EXPERTS], I32)
        nt_f = sb("nt_f", [TILE, EXPERTS])
        cum = sb("cum", [TILE, EXPERTS])
        step = sb("step", [TILE, EXPERTS])
        iota_m = sb("iota_m", [1, max(MOE)])
        past = sb("past", [1, max(MOE), EXPERTS])
        past2 = sb("past2", [1, max(MOE), EXPERTS])
        e_f = sb("e_f", [1, max(MOE)])
        r_f = sb("r_f", [1, max(MOE)])
        new_f = sb("new_f", [1, max(MOE)])
        moe_t = sb("moe_t", [1, MOE_ALL], I32)
        xd = [sb(f"xd{i}", [P, D]) for i in range(RING)]
        xdT = [sb(f"xdT{i}", [P, 2, P]) for i in range(RING)]
        w1_s = [sb(f"w1_s{i}", [P, W1_COLS]) for i in range(RING)]
        w2_s = [sb(f"w2_s{i}", [P, W2_COLS]) for i in range(RING)]
        hT = [sb(f"hT{i}", [P, 4, P]) for i in range(RING)]
        yo = [sb(f"yo{i}", [P, D]) for i in range(RING)]

        wt = sb("wt", [TILE, 2, TILES])
        wden = sb("wden", [TILE, TILES])
        sl_e = [sb(f"sl_e{i}", [TILE, 2], I32) for i in range(E_BUFS)]
        y_e = [[w_rel[0:TILE, k, i, :] for k in range(2)] for i in range(E_BUFS)]
        acc_e = [w_rel[0:TILE, 0, E_BUFS + i, :] for i in range(E_BUFS)]
        o_e = [w_rel[0:TILE, 1, E_BUFS + i, :] for i in range(E_BUFS)]
        xb_e = [hr[0][:, i * D:(i + 1) * D] for i in range(E_BUFS)]
        ln_e = [hr[0][:, (E_BUFS + i) * D:(E_BUFS + i + 1) * D] for i in range(E_BUFS)]
        st_e = [sb(f"st_e{i}", [TILE, 6]) for i in range(E_BUFS)]
        mv_e = [sb(f"mv_e{i}", [TILE, 2]) for i in range(E_BUFS)]
        sd_e = [sb(f"sd_e{i}", [TILE, 1]) for i in range(E_BUFS)]
        rs_e = [sb(f"rs_e{i}", [TILE, 1]) for i in range(E_BUFS)]

        agg = ctx.enter_context(nc.psum_tensor("agg", [P, 2 * BANK], F32))
        bank = [agg[:, 0:BANK], agg[:, BANK:2 * BANK]]
        bank += [ctx.enter_context(nc.psum_tensor(f"bank{i}", [P, BANK], F32)) for i in range(2, 8)]
        finish_p, y_p, xdT_p = bank[2:5]
        h_p = bank[5:8]

        const_loaded = sem("const_loaded")
        edges_loaded = sem("edges_loaded")
        basis_loaded = sem("basis_loaded")
        pool_const = sem("pool_const")
        pads_set = sem("pads_set")
        zeros_set = sem("zeros_set")
        edges_built = sem("edges_built")
        edges_turned = sem("edges_turned")
        edges_copied = sem("edges_copied")
        idx_stored = sem("idx_stored")
        zero_rows = sem("zero_rows")
        ends_ready = sem("ends_ready")
        ends_turned = sem("ends_turned")
        ends_max = sem("ends_max")
        ends_back = sem("ends_back")
        ranges_ready = sem("ranges_ready")
        w_begun = sem("w_begun")
        w_ready = sem("w_ready")
        x_loaded = [sem(f"x_loaded{i}") for i in range(2)]
        var_ready = sem("var_ready")
        std_ready = sem("std_ready")
        xn_ready = sem("xn_ready")
        xnT_done = sem("xnT_done")
        xnT_ready = sem("xnT_ready")
        h_done = sem("h_done")
        h_out_act = sem("h_out_act")
        h_out_dve = sem("h_out_dve")
        h_stored = [sem(f"h_stored{i}") for i in range(2)]
        xnT_stored = [sem(f"xnT_stored{i}") for i in range(2)]
        table_ready = sem("table_ready")

        idx_loaded = [sem(f"idx_loaded{h}") for h in range(2)]
        gathered = [[sem(f"gathered{p}_{c}") for c in range(CHUNKS[p])] for p in range(ROUNDS)]
        hot_ready = [sem(f"hot_ready{p}") for p in range(ROUNDS)]
        round_free = [sem(f"round_free{p}") for p in range(ROUNDS)]
        rest_loaded = [sem(f"rest_loaded{b}") for b in range(2)]
        rest_gathered = [sem(f"rest_gathered{b}") for b in range(2)]
        rest_hot = [sem(f"rest_hot{b}") for b in range(2)]
        seam_hot = sem("seam_hot")
        seam_free = sem("seam_free")
        rest_free = [sem(f"rest_free{b}") for b in range(2)]
        xc_loaded = sem("xc_loaded")
        xTc_loaded = sem("xTc_loaded")
        agg_open = sem("agg_open")
        agg_done = sem("agg_done")
        agg_read = sem("agg_read")
        var2_ready = sem("var2_ready")
        std2_ready = sem("std2_ready")
        xn2_ready = sem("xn2_ready")
        x2T_done = sem("x2T_done")
        send_ready = sem("send_ready")
        x2T_ready = sem("x2T_ready")
        pair_ready = sem("pair_ready")
        pair_stored = sem("pair_stored")
        logits_done = sem("logits_done")
        both_ready = sem("both_ready")
        rank_done = sem("rank_done")
        slots_ready = sem("slots_ready")
        sent = [sem(f"sent{k}") for k in range(2)]

        count_done = sem("count_done")
        region_ends = sem("region_ends")
        moe_table = sem("moe_table")
        gaps_zeroed = sem("gaps_zeroed")
        xd_loaded = [sem(f"xd_loaded{i}") for i in range(RING)]
        w1_loaded = [sem(f"w1_loaded{i}") for i in range(RING)]
        w2_loaded = [sem(f"w2_loaded{i}") for i in range(RING)]
        xdT_done = sem("xdT_done")
        xdT_ready = sem("xdT_ready")
        mm1_done = sem("mm1_done")
        hT_ready = sem("hT_ready")
        mm2_done = sem("mm2_done")
        yo_ready = sem("yo_ready")
        yo_stored = [sem(f"yo_stored{i}") for i in range(RING)]
        moe_stored = [sem(f"moe_stored{w}") for w in range(WAVES)]

        exp_done = sem("exp_done")
        gap_ready = sem("gap_ready")
        sl_ready = sem("sl_ready")
        y_loaded = [[sem(f"y_loaded{i}_{k}") for k in range(2)] for i in range(E_BUFS)]
        ln_loaded = [sem(f"ln_loaded{i}") for i in range(E_BUFS)]
        xb_loaded = [sem(f"xb_loaded{i}") for i in range(E_BUFS)]
        mixed = sem("mixed")
        std3_ready = sem("std3_ready")
        o_ready = sem("o_ready")
        o_stored = [sem(f"o_stored{i}") for i in range(E_BUFS)]

        block = ctx.enter_context(nc.Block())

        def rest_chunks(eng, counter, t, body):
            n = eng.value_load(rest_t[0:1, bass.ds(t, 1)], min_val=1, max_val=MAX_REST)
            with eng.Fori(0, n):
                r = eng.snap(counter, min_val=0, max_val=TILES * MAX_REST)
                u1 = eng.snap((r >> 1) + 1, min_val=1, max_val=TILES * MAX_REST)
                b = eng.snap(r & 1, min_val=0, max_val=1)
                with eng.If(b < 1):
                    body(0, u1)
                with eng.Else():
                    body(1, u1)
                eng.reg_add(counter, counter, 1)

        def sums_of(eng, t):
            at = t % 2 * BANK if isinstance(t, int) else eng.snap((t & 1) * BANK, min_val=0, max_val=BANK)
            return agg[0:TILE, bass.ds(at, D)]

        def last_tile(t):
            return isinstance(t, int) and t == TILES - 1

        def first_chunk(eng, t):
            return eng.value_load(start_t[0:1, bass.ds(t, 1)], min_val=0, max_val=FULL_CHUNKS)

        def all_tiles(eng, one, peel=False):
            w1 = WAVE_START[1]
            one(0, None, None, None, False)
            one(1, 0, None, None, False)
            one(2, 0, 0, None, True)
            with eng.Fori(3, w1 + 1) as t:
                one(t, 0, 0, None, True)
            one(w1 + 1, 1, 0, None, True)
            one(w1 + 2, 1, 1, None, True)
            with eng.Fori(w1 + 3, w1 + 2 + GAP_TILES) as t:
                one(t, 1, 1, None, True)
            assert w1 + 2 + GAP_TILES == MIX_FROM
            one(MIX_FROM, 1, 1, 0, True)
            if peel:
                one(MIX_FROM + 1, 1, 1, 1, True)
            with eng.Fori(MIX_FROM + 1 + peel, TILES - 1) as t:
                one(t, 1, 1, t - MIX_FROM, True)
            one(TILES - 1, 1, 1, ITERS_A - 1, True)

        @block.sync
        def _(sp):
            for i in range(2):
                sp.dma_start(xin[i][:, :], x[i * TILE:(i + 1) * TILE, :]).then_inc(x_loaded[i], 16)
            sp.dma_start(bas[:, :, :, :].rearrange("p b k o -> p (b k) o"),
                         basis.rearrange("b (k p) o -> p (b k) o", p=P)).then_inc(basis_loaded, 16)
            sp.dma_start(comp_s[:, :], comp.rearrange("(a r) b -> a (r b)", a=1).to_broadcast([P, RELS * BASES])
                         ).then_inc(basis_loaded, 16)
            sp.wait_ge(pads_set, 4)
            full = (GROUPS - 1) * P * P
            for to, fr in ((src_i, src), (et_i, etype), (dst_i, dst), (nrm, eweight)):
                sp.dma_start(to[:, 0:GROUPS - 1, :], fr[0:full].rearrange("(g p c) -> p g c", p=P, c=P)
                             ).then_inc(edges_loaded, 16)
                sp.dma_start(to[0:FULL_CHUNKS % P, GROUPS - 1, :], fr[full:FULL_CHUNKS * P].rearrange("(p c) -> p c", c=P)
                             ).then_inc(edges_loaded, 16)
                sp.dma_start(to[FULL_CHUNKS % P:FULL_CHUNKS % P + 1, GROUPS - 1, 0:N_EDGES % P],
                             fr[FULL_CHUNKS * P:N_EDGES].rearrange("(p c) -> p c", p=1)).then_inc(edges_loaded, 16)
            sp.wait_ge(zeros_set, 1)
            sp.dma_start(hb[0:1, :], h_bias.rearrange("(a o) -> a o", a=1)).then_inc(const_loaded, 16)
            sp.dma_start(gb[0:1, :], gate_b.rearrange("(a o) -> a o", a=1)).then_inc(const_loaded, 16)
            sp.dma_start(gw[:, :, :], gate_w.rearrange("(k p) e -> p k e", p=P)).then_inc(const_loaded, 16)
            sp.dma_start(lw[:, :, :], loop_w.rearrange("(k p) o -> p k o", p=P)).then_inc(const_loaded, 16)
            sp.dma_start(gam[:, :], gamma.rearrange("(a o) -> a o", a=1).to_broadcast([P, D])).then_inc(const_loaded, 16)
            sp.dma_start(bet[:, :], beta.rearrange("(a o) -> a o", a=1).to_broadcast([P, D])).then_inc(const_loaded, 16)

            def load_x(t, i):
                sp.dma_start(xin[i][:, :], x[bass.ds(t * TILE, TILE), :]).then_inc(x_loaded[i], 16)

            def store_h(t, i):
                sp.wait_ge(xnT_ready, t + 1)
                sp.dma_start(xnT_d[bass.ds(t * P, P), :], xnT[i][:, :, :].rearrange("p k n -> p (k n)")
                             ).then_inc(xnT_stored[i], 16)
                sp.wait_ge(h_out_act, 2 * t + 2)
                sp.wait_ge(h_out_dve, 2 * t + 2)
                sp.dma_start(h_d[bass.ds(t * TILE * RELS, TILE * RELS), :].rearrange("(n r) o -> n (r o)", r=RELS),
                             hr[i][:, :]).then_inc(h_stored[i], 16)

            def store_idx():
                sp.wait_ge(edges_copied, 2)
                sp.dma_start(idx_d, idx_all[:, :]).then_inc(idx_stored, 16)
                for w in range(WAVES):
                    sp.dma_start(disp_d[w][REGIONS:REGIONS + P, :], zeros[:, :]).then_inc(zero_rows, 16)

            def b_tile(t, i):
                sp.wait_ge(xn_ready, t + 2)
                load_x(t + 3, 1 - i)
                store_h(t, i)

            sp.wait_ge(xn_ready, 1)
            load_x(2, 0)
            for t in range(TURN_FROM + 4):
                b_tile(t, t % 2)
            store_idx()
            with sp.Fori(TURN_FROM // 2 + 2, TILES // 2 - 2) as m:
                for i in range(2):
                    b_tile(2 * m + i, i)
            b_tile(TILES - 4, 0)
            for i in range(3):
                store_h(TILES - 3 + i, 1 - i % 2)

            rest = sp.alloc_register("rest_sp")
            chunk = sp.alloc_register("chunk_sp")
            sp.reg_mov(rest, 0)

            def load_rest(b, u1):
                j = sp.snap(chunk, min_val=0, max_val=CHUNKS_PAD - 2)
                sp.wait_ge(rest_free[b], u1)
                sp.nop(nofuse=True)
                sp.dma_start(idx_r[b][:, :], idx_d[:, bass.ds(j, 2)]).then_inc(rest_loaded[b], 16)
                sp.reg_add(chunk, chunk, 1)

            def sp_rounds(t, warm):
                j = first_chunk(sp, t)
                at = [j, sp.snap(j + HALF, min_val=0, max_val=CHUNKS_PAD - HALF)]
                before_t = sp.snap(t * 16) if warm else None
                for h in range(2):
                    if warm:
                        for p in range(h * ROUNDS // 2, (h + 1) * ROUNDS // 2):
                            for c in range(CHUNKS[p]):
                                sp.wait_ge(gathered[p][c], before_t)
                        sp.nop(nofuse=True)
                    sp.dma_start(idx_h[h][:, :], idx_d[:, bass.ds(at[h], HALF)]).then_inc(idx_loaded[h], 16)
                sp.reg_mov(chunk, j + HEAD)

            def sp_rest(t):
                rest_chunks(sp, rest, t, load_rest)

            word = sp.alloc_register("word_sp")

            def expert_of(word_):
                return sp.snap((word_ >> 1) & (EXPERTS - 1), min_val=0, max_val=EXPERTS - 1)

            def next_word(i):
                sp.reg_mov(word, sp.value_load(moe_t[0:1, bass.ds(i, 1)], min_val=0, max_val=REGIONS * 32 + 31))

            def load_w1(k):
                w = sp.snap(word, min_val=0, max_val=REGIONS * 32 + 31)
                sp.dma_start(w1_s[k][:, :], w1_cat[bass.ds(expert_of(w) * P, P), :], cond=(w & 1) == 1
                             ).then_inc(w1_loaded[k], 16)

            def load_w2(k):
                w = sp.snap(word, min_val=0, max_val=REGIONS * 32 + 31)
                sp.dma_start(w2_s[k][:, :], w2_cat[bass.ds(expert_of(w) * P, P), :], cond=(w & 1) == 1
                             ).then_inc(w2_loaded[k], 16)

            def first_weights(s):
                next_word(s)
                load_w1(s % RING)
                load_w2(s % RING)
                next_word(s + 1)
                load_w1((s + 1) % RING)

            def sp_step(m, k, w, first=False, last=False):
                s = RING * m + k + MOE[0] * w
                if not (first and k < 2 and w == 0):
                    sp.wait_ge(yo_ready, s - 1)
                    v, j = (0, s - 2) if w == 0 or first and k < 2 else (1, RING * m + k - 2)
                    sp.dma_start(moe_d[v][bass.ds(j * P, P), :], yo[(k - 2) % RING][:, :]
                                 ).then_inc(yo_stored[(k - 2) % RING], 16)
                if not (last and k == RING - 1):
                    load_w2((k + 1) % RING)
                if not (last and k >= RING - 2):
                    next_word(s + 2)
                    if not (first and k == 0 and w == 0):
                        sp.wait_ge(hT_ready, s)
                    load_w1((k + 2) % RING)

            sp.wait_ge(idx_stored, 16)
            sp.wait_ge(ranges_ready, 1)
            sp_rounds(0, False)
            for i in range(2):
                sp.wait_ge(xnT_stored[i], 16 * (TILES // 2))
                sp.wait_ge(h_stored[i], 16 * (TILES // 2))
            sp.wait_ge(zero_rows, 16 * WAVES)
            sp.nop(nofuse=True).then_inc(table_ready, 1)
            sp_rest(0)
            with sp.Fori(1, MIX_FROM - 1) as t:
                sp_rounds(t, True)
                sp_rest(t)
            sp.wait_ge(moe_table, 1)
            first_weights(0)
            with sp.Fori(MIX_FROM - 1, MIX_FROM + 1) as t:
                sp_rounds(t, True)
                sp_rest(t)
            sp_rounds(MIX_FROM + 1, True)
            for k in range(RING):
                sp_step(0, k, 0, first=True)
            sp_rest(MIX_FROM + 1)
            with sp.Fori(MIX_FROM + 2, TILES) as t:
                sp_rounds(t, True)
                for k in range(RING):
                    sp_step(t - (MIX_FROM + 1), k, 0)
                sp_rest(t)
            for k in range(RING):
                sp_step(ITERS_A - 1, k, 0, last=True)

            sp.wait_ge(region_ends, 2)
            for k in range(2):
                sp.wait_ge(sent[k], 16 * TILES)
            for e in range(0, EXPERTS // 2):
                r = sp.value_load(padr_i[1][0:1, e:e + 1], min_val=0, max_val=REGIONS - P)
                sp.dma_start(disp_d[1][bass.ds(r, P), :], zeros[:, :]).then_inc(gaps_zeroed, 16)

            def load_ln(t, i):
                sp.dma_start(ln_e[i], pair_d[bass.ds(t * TILE, TILE), D:2 * D]).then_inc(ln_loaded[i], 16)

            def load_xb(t, i):
                sp.dma_start(xb_e[i], pair_d[bass.ds(t * TILE, TILE), 0:D]).then_inc(xb_loaded[i], 16)

            def store_out(t, i):
                sp.wait_ge(o_ready, t + 1)
                sp.dma_start(out[bass.ds(t * TILE, TILE), :], o_e[i]).then_inc(o_stored[i], 16)

            sp.wait_ge(pair_stored, 16 * TILES)
            for i in range(1, E_BUFS):
                load_ln(E_FIRST + i, i)
                load_xb(E_FIRST + i, i)
            load_ln(0, 0)
            load_xb(0, 0)
            sp.wait_ge(moe_table, 2)
            sp.wait_ge(hT_ready, MOE[0] - 1)
            first_weights(MOE[0])

            def b_iteration(m, last=False):
                for k in range(RING):
                    sp_step(m, k, 1, first=isinstance(m, int) and m == 0, last=last)
                    if isinstance(m, int) and m == 0:
                        continue
                    if k == 0 and not (isinstance(m, int) and m == 1):
                        store_out(m - 2, 0)
                        load_xb(m - 1, 0)
                    if k == 1:
                        sp.wait_ge(mixed, m)
                        load_ln(m, 0)

            b_iteration(0)
            for k in range(RING):
                sp.wait_ge(yo_stored[k], 16 * (ITERS_A + (1 if k == 0 else 0)))
            sp.nop(nofuse=True).then_inc(moe_stored[0], 1)
            b_iteration(1)
            with sp.Fori(2, ITERS_B - 1) as m:
                b_iteration(m)
            b_iteration(ITERS_B - 1, last=True)
            store_out(ITERS_B - 2, 0)
            load_xb(ITERS_B - 1, 0)
            for j in (MOE[1] - 2, MOE[1] - 1):
                sp.wait_ge(yo_ready, MOE[0] + j + 1)
                sp.dma_start(moe_d[1][j * P:(j + 1) * P, :], yo[j % RING][:, :]).then_inc(yo_stored[j % RING], 16)
            for k in range(RING):
                sp.wait_ge(yo_stored[k], 16 * (ITERS_A + ITERS_B))
            sp.nop(nofuse=True).then_inc(moe_stored[1], 1)

            def out_pair(m, q, ahead):
                t = E_FIRST + 2 * m
                if ahead:
                    sp.wait_ge(mixed, t + 2)
                    for b in range(2):
                        load_ln(t + 4 + b, 2 * q + b)
                for b in range(2):
                    store_out(t + b, 2 * q + b)
                    if ahead:
                        load_xb(t + 4 + b, 2 * q + b)

            with sp.Fori(0, E_PAIRS // 2 - 1) as j:
                for q in range(2):
                    out_pair(2 * j + q, q, True)
            for q in range(2):
                out_pair(E_PAIRS - 2 + q, q, False)
            for i in range(E_BUFS):
                sp.wait_ge(o_stored[i], 16 * (E_PAIRS // 2 + (E_FIRST if i == 0 else 0)))

        @block.gpsimd
        def _(pool):
            nc.gpsimd.memset(ident[:, :], 0.0)
            nc.gpsimd.memset(row0[:, :], 0.0)
            nc.gpsimd.memset(before[:, :], 0.0)
            nc.gpsimd.iota(iota_n[:, :], pattern=[[1, TILE]], base=-TILE, channel_multiplier=0,
                           allow_small_or_imprecise_dtypes=True)
            nc.gpsimd.iota(iota_e[:, :], pattern=[[1, EXPERTS]], base=0, channel_multiplier=0,
                           allow_small_or_imprecise_dtypes=True)
            nc.gpsimd.iota(region[:, :], pattern=[[CAP, EXPERTS]], base=0, channel_multiplier=0,
                           allow_small_or_imprecise_dtypes=True)
            nc.gpsimd.iota(tlo[:, :], pattern=[[TILE, TILES]], base=0, channel_multiplier=0,
                           allow_small_or_imprecise_dtypes=True)
            nc.gpsimd.iota(cid[:, :], pattern=[[P, GROUPS]], base=1, channel_multiplier=1,
                           allow_small_or_imprecise_dtypes=True)
            nc.gpsimd.iota(cidr[:, :], pattern=[[-P, GROUPS]], base=CHUNKS_PAD, channel_multiplier=-1,
                           allow_small_or_imprecise_dtypes=True)
            nc.gpsimd.iota(iota_m[:, :], pattern=[[1, max(MOE)]], base=0, channel_multiplier=0,
                           allow_small_or_imprecise_dtypes=True)
            pool.drain()
            nc.gpsimd.affine_select(out=ident[:, :], in_=ident[:, :], compare_op=ALU.not_equal, fill=1.0, base=0,
                                    pattern=[[-1, P]], channel_multiplier=1)
            nc.gpsimd.affine_select(out=before[:, :], in_=before[:, :], compare_op=ALU.is_ge, fill=1.0, base=0,
                                    pattern=[[-1, P]], channel_multiplier=1)
            nc.gpsimd.affine_select(out=row0[:, :], in_=row0[:, :], compare_op=ALU.not_equal, fill=1.0, base=0,
                                    pattern=[[0, P]], channel_multiplier=1)
            pool.drain().then_inc(pool_const, 1)

            pool.wait_ge(table_ready, 1)
            pool.wait_ge(ranges_ready, 1)
            rest = pool.alloc_register("rest_pool")
            pool.reg_mov(rest, 0)

            def gather(t, p):
                if p % (ROUNDS // 2) == 0:
                    pool.wait_ge(idx_loaded[p // (ROUNDS // 2)], (t + 1) * 16)
                pool.wait_ge(round_free[p], t + 1)
                pool.nop(nofuse=True)
                for c in range(CHUNKS[p]):
                    k = (2 * p + c) % HALF
                    nc.gpsimd.indirect_dma_start(
                        out=rows[p][c][:, :], out_offset=None, in_=h_d,
                        in_offset=bass.IndirectOffsetOnAxis(ap=idx_h[p // (ROUNDS // 2)][:, k:k + 1], axis=0),
                    ).then_inc(gathered[p][c], 16)

            def gather_rest(b, u1):
                pool.wait_ge(rest_loaded[b], u1 * 16)
                pool.nop(nofuse=True)
                nc.gpsimd.indirect_dma_start(
                    out=rows_r[b][:, :], out_offset=None, in_=h_d,
                    in_offset=bass.IndirectOffsetOnAxis(ap=idx_r[b][:, 0:1], axis=0),
                ).then_inc(rest_gathered[b], 16)

            def scatter(t, w):
                pool.wait_ge(slots_ready, t + 1)
                pool.wait_ge(send_ready, t + 1)
                pool.nop(nofuse=True)
                for k in range(2):
                    nc.gpsimd.indirect_dma_start(
                        out=disp_d[w], out_offset=bass.IndirectOffsetOnAxis(ap=slots[:, k:k + 1], axis=0),
                        in_=send[:, :], in_offset=None).then_inc(sent[k], 16)

            def pool_tile(t, w1, w2, m, warm):
                for p in range(ROUNDS):
                    gather(t, p)
                    if p == ROUNDS - 2 and w2 is not None:
                        scatter(t - 2, w2)
                rest_chunks(pool, rest, t, gather_rest)

            all_tiles(pool, pool_tile)
            scatter(TILES - 2, 1)
            scatter(TILES - 1, 1)

            def gather_y(t, i, w):
                pool.wait_ge(sl_ready, t + 1)
                pool.nop(nofuse=True)
                for k in range(2):
                    nc.gpsimd.indirect_dma_start(
                        out=y_e[i][k], out_offset=None, in_=moe_d[w],
                        in_offset=bass.IndirectOffsetOnAxis(ap=sl_e[i][:, k:k + 1], axis=0),
                    ).then_inc(y_loaded[i][k], 16)

            pool.wait_ge(moe_stored[0], 1)
            with pool.Fori(0, E_FIRST + 1) as t:
                gather_y(t, 0, 0)
            pool.wait_ge(moe_stored[1], 1)
            for i in range(1, E_BUFS):
                gather_y(E_FIRST + i, i, 1)
            with pool.Fori(0, E_PAIRS // 2 - 1) as j:
                for i in range(E_BUFS):
                    gather_y(E_BUFS * j + E_FIRST + E_BUFS + i, i, 1)

        @block.scalar
        def _(act):
            act.wait_ge(zeros_set, 1)

            def act_std(t, i):
                act.wait_ge(var_ready, t + 1)
                nc.scalar.activation(sd[i][:, :], mv[i][:, 1:2], ACT.Sqrt, bias=eps[0:TILE, :]).then_inc(std_ready, 1)

            def act_h(t, i, warm):
                act.wait_ge(xnT_done, t + 1)
                if warm:
                    act.wait_ge(xnT_stored[i], (t // 2) * 16)
                nc.scalar.copy(xnT[i][:, :, :].rearrange("p k n -> p (k n)"), bank[4 + i][:, 0:2 * TILE]
                               ).then_inc(xnT_ready, 1)

            def act_out(t, i, warm):
                if warm:
                    act.wait_ge(h_stored[i], (t // 2) * 16)
                for j in (0, 2):
                    act.wait_ge(h_done, 4 * t + j + 1)
                    nc.scalar.copy(hr[i][:, j * 512:(j + 1) * 512], bank[j][0:TILE, :]).then_inc(h_out_act, 1)

            act_std(0, 0)
            act_std(1, 1)
            act.wait_ge(basis_loaded, 32)
            for r in range(RELS):
                nc.scalar.activation(w_rel[:, :, r, :], bas[:, 0, :, :], ACT.Identity,
                                     scale=comp_s[:, r * BASES:r * BASES + 1]).then_inc(w_begun, 1)
            act_h(0, 0, False)
            for t in range(TILES):
                if t == B_FROM:
                    with act.Fori(B_FROM // 2, TILES // 2 - 1) as m:
                        for i in range(2):
                            act_std(2 * m + i + 2, i)
                            act_h(2 * m + i + 1, 1 - i, True)
                            act_out(2 * m + i, i, True)
                if t < B_FROM or t >= TILES - 2:
                    if t + 2 < TILES:
                        act_std(t + 2, t % 2)
                    if t + 1 < TILES:
                        act_h(t + 1, (t + 1) % 2, t >= 1)
                    act_out(t, t % 2, t >= 2)

            def load_rows(i, k, w):
                word = act.value_load(moe_t[0:1, bass.ds(i, 1)], min_val=0, max_val=REGIONS * 32 + 31)
                row = act.snap(word >> 5, min_val=0, max_val=REGIONS + 1)
                act.dma_start(xd[k][:, :], disp_d[w][bass.ds(row, P), :]).then_inc(xd_loaded[k], 16)

            def act_turn(i, k):
                act.wait_ge(xdT_done, i + 1)
                nc.scalar.copy(xdT[k][:, :, :].rearrange("p k n -> p (k n)"), xdT_p[:, 0:2 * P]).then_inc(xdT_ready, 1)

            def act_relu(i, k):
                act.wait_ge(mm1_done, i + 1)
                for f in range(4):
                    last = nc.scalar.activation(hT[k][:, f, :], h_p[k][:, f * P:(f + 1) * P], ACT.Relu,
                                                bias=w1_s[k][:, 2 * FF + f:2 * FF + f + 1])
                last.then_inc(hT_ready, 1)

            def finish_std(t):
                act.wait_ge(var2_ready, t + 1)
                nc.scalar.activation(sd_c[:, :], mv_c[:, 1:2], ACT.Sqrt, bias=eps[0:TILE, :]).then_inc(std2_ready, 1)

            def finish_send(t, warm):
                act.wait_ge(xn2_ready, t + 1)
                if warm:
                    for k in range(2):
                        act.wait_ge(sent[k], t * 16)
                nc.scalar.copy(send[:, :], pair[:, 1, :]).then_inc(send_ready, 1)
                act.wait_ge(pair_ready, t + 1)
                act.dma_start(pair_d[bass.ds(t * TILE, TILE), :], pair[:, :, :].rearrange("n a o -> n (a o)")
                              ).then_inc(pair_stored, 16)

            def finish_turn(t):
                act.wait_ge(x2T_done, t + 1)
                nc.scalar.copy(xn2T[:, :, :].rearrange("p k n -> p (k n)"), finish_p[:, 0:2 * TILE]).then_inc(x2T_ready, 1)

            def act_tile(t, w1, w2, m, warm, last=False):
                def front(k):
                    s = RING * m + k
                    act_turn(s, k)
                    if not last:
                        load_rows(s + RING, k, 0)
                    if not (isinstance(s, int) and s < 1):
                        act_relu(s - 1, (k - 1) % RING)

                if not last:
                    act.wait_ge(agg_open, t + 1)
                    act.dma_start(xT_c[:, :], xnT_d[bass.ds(t * P + P, P), :]).then_inc(xTc_loaded, 16)
                if w1 is None:
                    return
                if m is not None:
                    front(0)
                finish_std(t - 1)
                act.dma_start(x_c[:, :], x[bass.ds(t * TILE, TILE), :]).then_inc(xc_loaded, 16)
                finish_send(t - 1, warm)
                if m is not None:
                    front(1)
                finish_turn(t - 1)
                if m is not None:
                    front(2)

            w1 = WAVE_START[1]
            act.wait_ge(table_ready, 1)
            act.dma_start(xT_c[:, :], xnT_d[0:P, :]).then_inc(xTc_loaded, 16)
            act.dma_start(x_c[:, :], x[0:TILE, :]).then_inc(xc_loaded, 16)
            act_tile(0, None, None, None, False)
            act_tile(1, 0, None, None, False)
            with act.Fori(2, w1 + 1) as t:
                act_tile(t, 0, 0, None, True)
            act_tile(w1 + 1, 1, 0, None, True)
            act.wait_ge(moe_table, 1)
            for k in range(2):
                act.wait_ge(sent[k], 16 * w1)
            with act.Fori(w1 + 2, MIX_FROM) as t:
                act_tile(t, 1, 1, None, True)
                for j in range(EXPERTS // GAP_TILES):
                    e = (t - (w1 + 2)) * (EXPERTS // GAP_TILES) + j
                    r = act.value_load(padr_i[0][0:1, bass.ds(e, 1)], min_val=0, max_val=REGIONS - P)
                    act.dma_start(disp_d[0][bass.ds(r, P), :], zeros[:, :]).then_inc(gaps_zeroed, 16)
            act.wait_ge(gaps_zeroed, 16 * EXPERTS)
            for k in range(RING):
                load_rows(k, k, 0)
            act_tile(MIX_FROM, 1, 1, 0, True)
            with act.Fori(MIX_FROM + 1, TILES - 1) as t:
                act_tile(t, 1, 1, t - MIX_FROM, True)
            act_tile(TILES - 1, 1, 1, ITERS_A - 1, True, last=True)
            finish_std(TILES - 1)
            finish_send(TILES - 1, True)
            finish_turn(TILES - 1)

            act.wait_ge(gap_ready, 1)
            nc.scalar.activation(wt[:, 1, :], gap[:, :], ACT.Exp).then_inc(exp_done, 1)
            nc.scalar.activation(sd_e[0][:, :], eps[0:TILE, :], ACT.Sqrt)
            act.wait_ge(region_ends, 2)
            for k in range(2):
                act.wait_ge(sent[k], 16 * TILES)
            for e in range(EXPERTS // 2, EXPERTS):
                r = act.value_load(padr_i[1][0:1, e:e + 1], min_val=0, max_val=REGIONS - P)
                act.dma_start(disp_d[1][bass.ds(r, P), :], zeros[:, :]).then_inc(gaps_zeroed, 16)
            act.wait_ge(moe_table, 2)
            act.wait_ge(gaps_zeroed, 16 * EXPERTS * WAVES)
            for k in range(RING):
                load_rows(MOE[0] + k, k, 1)

            def e_std(t, i):
                act.wait_ge(mixed, t + 1)
                nc.scalar.activation(sd_e[i][:, :], mv_e[i][:, 1:2], ACT.Sqrt, bias=eps[0:TILE, :]
                                     ).then_inc(std3_ready, 1)

            def b_iteration(m, ahead):
                for k in range(RING):
                    s = RING * m + MOE[0] + k
                    seam = isinstance(m, int) and m == 0
                    act_turn(s, k)
                    if ahead:
                        load_rows(s + RING, k, 1)
                    act_relu(s - 1, (k - 1) % RING)
                    if k == 0 and not seam:
                        e_std(m - 1, 0)

            b_iteration(0, True)
            with act.Fori(1, ITERS_B - 1) as m:
                b_iteration(m, True)
            b_iteration(ITERS_B - 1, False)
            act_relu(MOE_ALL - 1, RING - 1)
            with act.Fori(0, E_PAIRS // 2) as j:
                for i in range(E_BUFS):
                    e_std(E_BUFS * j + E_FIRST + i, i)

        @block.vector
        def _(dve):
            v = nc.vector
            v.memset(src_i[:, GROUPS - 1, :], 0).then_inc(pads_set, 1)
            v.memset(et_i[:, GROUPS - 1, :], 0).then_inc(pads_set, 1)
            v.memset(dst_i[:, GROUPS - 1, :], NO_NODE).then_inc(pads_set, 1)
            v.memset(nrm[:, GROUPS - 1, :], 0.0).then_inc(pads_set, 1)
            v.memset(ones[:, :], 1.0)
            v.memset(zeros[:, :], 0.0)
            v.memset(hb[:, :], 0.0)
            v.memset(gb[:, :], 0.0)
            v.memset(eps[:, :], EPS)
            v.memset(both[:, :], 0.0)
            for w in range(WAVES):
                v.memset(seen[w][:, :], 0.0)
            dve.drain().then_inc(zeros_set, 1)

            dve.wait_ge(pool_const, 1)

            def dve_x(t, i):
                dve.wait_ge(x_loaded[i], (t // 2 + 1) * 16)
                v.bn_stats(st[i][:, :], xin[i][:, :])
                dve.drain()
                v.bn_aggr(mv[i][:, :], st[i][:, :]).then_inc(var_ready, 1)

            def dve_xn(t, i):
                dve.wait_ge(std_ready, t + 1)
                v.reciprocal(rs[i][:, :], sd[i][:, :])
                dve.drain()
                v.tensor_scalar(xn[i][:, :], xin[i][:, :], mv[i][:, 0:1], rs[i][:, :], ALU.subtract, ALU.mult
                                ).then_inc(xn_ready, 1)

            def dve_out(t, i, warm):
                if warm:
                    dve.wait_ge(h_stored[i], (t // 2) * 16)
                for j in (1, 3):
                    dve.wait_ge(h_done, 4 * t + j + 1)
                    v.tensor_copy(hr[i][:, j * 512:(j + 1) * 512], bank[j][0:TILE, :]).then_inc(h_out_dve, 1)

            def relation_weights(j):
                for b in range(1, BASES):
                    for r in (2 * j, 2 * j + 1):
                        if b == 1:
                            dve.wait_ge(w_begun, r + 1)
                        v.scalar_tensor_tensor(w_rel[:, :, r, :], bas[:, b, :, :],
                                               comp_s[:, r * BASES + b:r * BASES + b + 1], w_rel[:, :, r, :],
                                               ALU.mult, ALU.add)
                    if b < BASES - 1:
                        dve.drain()
                dve.drain().then_inc(w_ready, 1)

            t_b = tlo[:, :].unsqueeze(2).to_broadcast([P, TILES, GROUPS])

            def over_tiles(a):
                return a[:, :].unsqueeze(1).to_broadcast([P, TILES, GROUPS])

            def edge_numbers():
                dve.wait_ge(edges_loaded, 12 * 16)
                v.scalar_tensor_tensor(idx_f[:, :, :], src_i[:, :, :], float(RELS), et_i[:, :, :], ALU.mult, ALU.add)
                v.tensor_copy(dst_f[:, :, :], dst_i[:, :, :])
                dve.drain().then_inc(edges_built, 1)
                v.tensor_reduce(cmin[:, :], dst_f[:, :, :], AX.X, ALU.min)
                v.tensor_reduce(cmax[:, :], dst_f[:, :, :], AX.X, ALU.max)
                dve.drain()

            def chunk_ranges():
                v.tensor_tensor(candA[:, :, :], over_tiles(cmax), t_b, ALU.is_ge)
                v.tensor_tensor(candB[:, :, :], over_tiles(cmin), t_b, ALU.subtract)
                dve.drain()
                v.scalar_tensor_tensor(candA[:, :, :], candB[:, :, :], TILE - 0.5, candA[:, :, :], ALU.is_lt, ALU.mult)
                dve.drain()
                v.tensor_tensor(candB[:, :, :], candA[:, :, :], over_tiles(cidr), ALU.mult)
                dve.drain()
                v.tensor_reduce(ends[:, 0:TILES], candB[:, :, :], AX.X, ALU.max)
                dve.drain()
                v.tensor_tensor(candB[:, :, :], candA[:, :, :], over_tiles(cid), ALU.mult)
                dve.drain()
                v.tensor_reduce(ends[:, TILES:2 * TILES], candB[:, :, :], AX.X, ALU.max).then_inc(ends_ready, 1)

            def copy_turned(k):
                field, at = divmod(k, 2)
                n = (TURNED if at == 0 else GROUPS - TURNED) * P
                at *= TURNED * P
                to = idx_all[:, at:at + n] if field == 0 else dw_all[:, at:at + n, field - 1]
                dve.wait_ge(edges_turned, k + 1)
                v.tensor_copy(to, bank[6 + k % 2][:, 0:n]).then_inc(edges_copied, 1)

            def over_partitions():
                dve.wait_ge(ends_turned, 1)
                v.tensor_reduce(ends1[:, :], bank[6][0:2 * TILES, 0:P], AX.X, ALU.max).then_inc(ends_max, 1)

            def tile_ranges():
                dve.wait_ge(ends_back, 1)
                v.tensor_copy(er[:, :], bank[7][0:1, 0:2 * TILES])
                dve.drain()
                v.tensor_scalar(has[:, :], er[:, 0:TILES], 0.5, None, ALU.is_ge)
                v.tensor_scalar(fst[:, :], er[:, 0:TILES], -1.0, BIG, ALU.mult, ALU.add)
                dve.drain()
                v.tensor_tensor(fst[:, :], fst[:, :], has[:, :], ALU.mult)
                dve.drain()
                v.tensor_copy(start_t[:, :], fst[:, :])
                v.tensor_tensor(rnf[:, :], er[:, TILES:2 * TILES], fst[:, :], ALU.subtract)
                v.tensor_tensor(nxt[:, :], fst[:, 1:TILES], er[:, TILES:2 * TILES - 1], ALU.subtract)
                v.memset(seam[:, :], 0.0)
                dve.drain()
                v.tensor_scalar(nxt[:, :], nxt[:, :], -1.0, None, ALU.is_equal)
                dve.drain()
                v.scalar_tensor_tensor(seam[:, 0:TILES - 1], rnf[:, 0:TILES - 1], HEAD + 1.5, nxt[:, :], ALU.is_ge, ALU.mult)
                dve.drain()
                v.tensor_tensor(rnf[:, :], rnf[:, :], seam[:, :], ALU.subtract)
                v.scalar_tensor_tensor(nxt[:, :], fst[:, 1:TILES], float(-PAD_CHUNK), seam[:, 0:TILES - 1],
                                       ALU.add, ALU.mult)
                dve.drain()
                v.tensor_scalar(rest_t[:, :], rnf[:, :], float(-HEAD), 1.0, ALU.add, ALU.max)
                v.tensor_scalar(seam_t[:, :], nxt[:, :], float(PAD_CHUNK), None, ALU.add)
                dve.drain().then_inc(ranges_ready, 1)

            parts = [[edge_numbers], [chunk_ranges]] + [[lambda k=k: copy_turned(k)] for k in range(6)] + [[tile_ranges]]
            parts[ENDS_AT - 1].append(over_partitions)
            assert len(parts) <= B_FROM and ENDS_AT == len(parts) - 1
            for t in range(2):
                dve_x(t, t)
                dve_xn(t, t)
            dve.wait_ge(basis_loaded, 32)
            for j in range(RELS // 2):
                relation_weights(j)
            for t in range(TILES):
                if t == B_FROM:
                    with dve.Fori(B_FROM // 2, TILES // 2 - 1) as m:
                        for i in range(2):
                            dve_x(2 * m + i + 2, i)
                            dve_xn(2 * m + i + 2, i)
                            dve_out(2 * m + i, i, True)
                if t < B_FROM or t >= TILES - 2:
                    if t + 2 < TILES:
                        dve_x(t + 2, t % 2)
                        dve_xn(t + 2, t % 2)
                    dve_out(t, t % 2, t >= 2)
                    if t < len(parts):
                        for part in parts[t]:
                            part()

            rest = dve.alloc_register("rest_dve")
            chunk = dve.alloc_register("chunk_dve")
            dve.reg_mov(rest, 0)

            def one_hots(t, p):
                dve.wait_ge(round_free[p], t + 1)
                for c in range(CHUNKS[p]):
                    k = 2 * p + c
                    last = v.tensor_scalar(hot[p][:, c, :], iota_n[:, :], dw_h[:, k, 0:1], dw_h[:, k, 1:2],
                                           ALU.is_equal, ALU.mult)
                last.then_inc(hot_ready[p], 1)

            def one_hot_rest(b, u1):
                j = dve.snap(chunk, min_val=0, max_val=CHUNKS_PAD - 1)
                dve.drain()
                v.tensor_copy(dw_r[:, :], dw_all[:, bass.ds(j, 1), :].rearrange("p c f -> p (c f)"))
                dve.drain()
                dve.wait_ge(rest_free[b], u1)
                v.tensor_scalar(hot_r[b][:, :], iota_n[:, :], dw_r[:, 0:1], dw_r[:, 1:2], ALU.is_equal, ALU.mult
                                ).then_inc(rest_hot[b], 1)
                dve.reg_add(chunk, chunk, 1)

            def seam_hots(t):
                j = dve.value_load(seam_t[0:1, bass.ds(t, 1)], min_val=0, max_val=PAD_CHUNK)
                dve.drain()
                v.tensor_copy(dw_m[:, :], dw_all[:, bass.ds(j, 1), :].rearrange("p c f -> p (c f)"))
                dve.drain()
                dve.wait_ge(seam_free, t + 1)
                v.tensor_scalar(hot_m[:, :], iota_n[:, :], dw_m[:, 0:1], dw_m[:, 1:2], ALU.is_equal, ALU.mult
                                ).then_inc(seam_hot, 1)

            def residual(t, warm):
                dve.wait_ge(agg_done, t + 1)
                dve.wait_ge(xc_loaded, (t + 1) * 16)
                if warm:
                    dve.wait_ge(pair_stored, t * 16)
                v.scalar_tensor_tensor(pair[:, 0, :], sums_of(dve, t), 0.0, x_c[:, :], ALU.max, ALU.add
                                       ).then_inc(agg_read, 1)
                dve.drain()
                v.bn_stats(st_c[:, :], pair[:, 0, :])
                dve.drain()
                v.bn_aggr(mv_c[:, :], st_c[:, :]).then_inc(var2_ready, 1)

            def norm2(t):
                dve.wait_ge(std2_ready, t + 1)
                v.reciprocal(rs_c[:, :], sd_c[:, :])
                dve.drain()
                v.tensor_scalar(pair[:, 1, :], pair[:, 0, :], mv_c[:, 0:1], rs_c[:, :], ALU.subtract, ALU.mult
                                ).then_inc(xn2_ready, 1)
                dve.drain()
                v.tensor_tensor(pair[:, 0, :], pair[:, 0, :], bet[0:TILE, :], ALU.add).then_inc(pair_ready, 1)

            def pick(t):
                dve.wait_ge(logits_done, t + 1)
                v.tensor_copy(lg[:, :], finish_p[0:TILE, LOGITS_AT:LOGITS_AT + EXPERTS])
                dve.drain()
                v.max(top[:, :], lg[:, :])
                dve.drain()
                v.max_index(topi[:, :], top[:, :], lg[:, :])
                v.tensor_tensor(gap[:, bass.ds(t, 1)], top[:, 1:2], top[:, 0:1], ALU.subtract)
                dve.drain()
                v.tensor_copy(topf[:, :], topi[:, 0:2])
                dve.drain()
                v.tensor_tensor(oh[:, :, :], iota_e[0:TILE, :].unsqueeze(1).to_broadcast([TILE, 2, EXPERTS]),
                                topf[:, :].unsqueeze(2).to_broadcast([TILE, 2, EXPERTS]), ALU.is_equal)
                dve.drain()
                v.tensor_tensor(both[0:TILE, :], oh[:, 0, :], oh[:, 1, :], ALU.add).then_inc(both_ready, 1)

            def place(t, w, warm):
                dve.wait_ge(rank_done, t + 1)
                if warm:
                    for k in range(2):
                        dve.wait_ge(sent[k], t * 16)
                v.tensor_tensor(slf[:, :], finish_p[0:TILE, RANK_AT:RANK_AT + EXPERTS], region[0:TILE, :], ALU.add)
                v.tensor_tensor(seen[w][0:TILE, :], seen[w][0:TILE, :], both[0:TILE, :], ALU.add)
                dve.drain()
                v.tensor_tensor(slx[:, :, :], oh[:, :, :], slf[:, :].unsqueeze(1).to_broadcast([TILE, 2, EXPERTS]),
                                ALU.mult)
                dve.drain()
                v.tensor_reduce(slot_f[:, :], slx[:, :, :], AX.X, ALU.add)
                dve.drain()
                v.tensor_copy(slot_all[:, bass.ds(t * 2, 2)], slot_f[:, :])
                v.tensor_copy(expert_all[:, bass.ds(t * 2, 2)], topf[:, :])
                v.tensor_copy(slots[:, :], slot_f[:, :]).then_inc(slots_ready, 1)

            def add_b2(i, k, warm, uses=0):
                dve.wait_ge(mm2_done, i + 1)
                if warm:
                    dve.wait_ge(yo_stored[k], uses * 16)
                v.tensor_tensor(yo[k][:, :], y_p[:, 0:D], w2_s[k][:, 4 * D:5 * D], ALU.add).then_inc(yo_ready, 1)

            def read_counts(w):
                dve.wait_ge(count_done, w + 1)
                v.tensor_copy(cnt[:, :], finish_p[0:TILE, COUNT_AT:COUNT_AT + EXPERTS])
                dve.drain()
                v.tensor_tensor(padr_i[w][:, :], cnt[:, :], region[0:TILE, :], ALU.add)
                v.tensor_scalar(cnt_i[:, :], cnt[:, :], float(P - 1), None, ALU.add)
                dve.drain().then_inc(region_ends, 1)

            def expert_table(w):
                n, at = MOE[w], w * MOE[0]
                v.tensor_scalar(nt_i[:, :], cnt_i[:, :], P.bit_length() - 1, None, ALU.arith_shift_right)
                dve.drain()
                v.tensor_copy(nt_f[:, :], nt_i[:, :])
                dve.drain()
                v.tensor_tensor_scan(cum[:, :], ones[0:TILE, 0:EXPERTS], nt_f[:, :], 0.0, ALU.mult, ALU.add)
                v.tensor_scalar(step[:, :], nt_f[:, :], -float(P), float(CAP), ALU.mult, ALU.add)
                dve.drain()
                shape = [1, n, EXPERTS]
                v.tensor_tensor(past[:, 0:n, :], iota_m[:, 0:n].unsqueeze(2).to_broadcast(shape),
                                cum[0:1, :].unsqueeze(1).to_broadcast(shape), ALU.is_ge)
                dve.drain()
                v.tensor_reduce(e_f[:, 0:n], past[:, 0:n, :], AX.X, ALU.add)
                v.tensor_tensor(past2[:, 0:n, :], past[:, 0:n, :], step[0:1, :].unsqueeze(1).to_broadcast(shape),
                                ALU.mult)
                dve.drain()
                v.tensor_reduce(r_f[:, 0:n], past2[:, 0:n, :], AX.X, ALU.add)
                v.tensor_scalar(e_f[:, 0:n], e_f[:, 0:n], float(EXPERTS - 1), None, ALU.min)
                v.memset(new_f[:, 0:RING], 1.0)
                dve.drain()
                v.scalar_tensor_tensor(r_f[:, 0:n], iota_m[:, 0:n], float(P), r_f[:, 0:n], ALU.mult, ALU.add)
                v.tensor_tensor(new_f[:, RING:n], e_f[:, RING:n], e_f[:, 0:n - RING], ALU.not_equal)
                dve.drain()
                v.tensor_scalar(r_f[:, 0:n], r_f[:, 0:n], float(REGIONS), 16.0, ALU.min, ALU.mult)
                dve.drain()
                v.tensor_tensor(r_f[:, 0:n], r_f[:, 0:n], e_f[:, 0:n], ALU.add)
                dve.drain()
                v.scalar_tensor_tensor(moe_t[:, at:at + n], r_f[:, 0:n], 2.0, new_f[:, 0:n], ALU.mult, ALU.add)
                dve.drain().then_inc(moe_table, 1)

            def expert_rows(w):
                a, b = 2 * WAVE_START[w], 2 * (WAVE_START[w] + WAVE_TILES[w])
                v.tensor_tensor(shift0[:, :], cum[:, :], nt_f[:, :], ALU.subtract)
                dve.drain()
                v.scalar_tensor_tensor(shift[:, :], shift0[:, :], float(P), region[0:TILE, :], ALU.mult, ALU.subtract)
                dve.drain()
                for e in range(EXPERTS):
                    v.tensor_scalar(shifted[e % 2][:, a:b], expert_all[:, a:b], float(e), shift[:, e:e + 1],
                                    ALU.is_equal, ALU.mult)
                    dve.drain()
                    v.tensor_tensor(slot_all[:, a:b], slot_all[:, a:b], shifted[e % 2][:, a:b], ALU.add)
                dve.drain()
                v.tensor_copy(moe_row[:, a:b], slot_all[:, a:b])

            def dve_tile(t, w1, w2, m, warm):
                j = first_chunk(dve, t)
                dve.drain()
                v.tensor_scalar(iota_n[:, :], iota_n[:, :], float(TILE), None, ALU.add)
                v.tensor_copy(dw_h[:, :, :], dw_all[:, bass.ds(j, HEAD), :])
                dve.reg_mov(chunk, j + HEAD)
                dve.drain()
                tables = isinstance(t, int) and t == WAVE_START[1] + 1
                warm_yo = not (isinstance(m, int) and m == 0)

                def between(p):
                    if p == 0 and w2 is not None:
                        place(t - 2, w2, not (isinstance(t, int) and t == 2))
                    if p == 0 and m is not None and warm_yo:
                        add_b2(RING * m - 3, 0, not first_uses(m), m - 1)
                    if w1 is not None:
                        if p == 1:
                            residual(t - 1, warm)
                        if p == 2:
                            norm2(t - 1)
                        if p == 6:
                            pick(t - 1)
                    if m is not None and warm_yo:
                        if p == 3:
                            add_b2(RING * m - 2, 1, not first_uses(m), m - 1)
                        if p == 5:
                            add_b2(RING * m - 1, 2, not first_uses(m), m - 1)
                    if tables and p == 1:
                        read_counts(0)
                    if tables and p == 3:
                        expert_table(0)
                    if isinstance(t, int) and t == WAVE_START[1] + 2 and p == 3:
                        expert_rows(0)

                for p in range(ROUNDS):
                    one_hots(t, p)
                    between(p)
                if not last_tile(t):
                    seam_hots(t)
                rest_chunks(dve, rest, t, one_hot_rest)

            def first_uses(m):
                return isinstance(m, int) and m <= 1

            dve.wait_ge(const_loaded, 96)
            all_tiles(dve, dve_tile, peel=True)
            place(TILES - 2, 1, True)
            add_b2(MOE[0] - RING, 0, True, ITERS_A - 1)
            residual(TILES - 1, True)
            norm2(TILES - 1)
            pick(TILES - 1)
            place(TILES - 1, 1, True)
            dve.drain().then_inc(gap_ready, 1)
            read_counts(1)
            expert_table(1)
            expert_rows(1)

            dve.wait_ge(exp_done, 1)
            v.tensor_scalar(wden[:, :], wt[:, 1, :], 1.0, None, ALU.add)
            dve.drain()
            v.reciprocal(wt[:, 0, :], wden[:, :])
            dve.drain()
            v.tensor_tensor(wt[:, 1, :], wt[:, 1, :], wt[:, 0, :], ALU.mult)

            def ready_slots(t, i):
                dve.drain()
                v.tensor_copy(sl_e[i][:, :], moe_row[:, bass.ds(t * 2, 2)]).then_inc(sl_ready, 1)

            def mix(tiles):
                dve.drain()
                for t, i, use in tiles:
                    dve.wait_ge(ln_loaded[i], (use + 1) * 16)
                    dve.wait_ge(y_loaded[i][0], (use + 1) * 16)
                    v.scalar_tensor_tensor(acc_e[i], y_e[i][0], wt[:, 0, bass.ds(t, 1)], ln_e[i], ALU.mult, ALU.add)
                dve.drain()
                for t, i, use in tiles:
                    dve.wait_ge(y_loaded[i][1], (use + 1) * 16)
                    v.scalar_tensor_tensor(acc_e[i], y_e[i][1], wt[:, 1, bass.ds(t, 1)], acc_e[i], ALU.mult, ALU.add)
                dve.drain()
                for t, i, use in tiles:
                    v.bn_stats(st_e[i][:, :], acc_e[i])
                dve.drain()
                for t, i, use in tiles:
                    v.bn_aggr(mv_e[i][:, :], st_e[i][:, :]).then_inc(mixed, 1)

            def emit(tiles):
                for t, i, use in tiles:
                    v.scalar_tensor_tensor(acc_e[i], acc_e[i], mv_e[i][:, 0:1], gam[0:TILE, :], ALU.subtract, ALU.mult)
                    dve.wait_ge(std3_ready, t + 1)
                    v.reciprocal(rs_e[i][:, :], sd_e[i][:, :])
                dve.drain()
                for t, i, use in tiles:
                    dve.wait_ge(xb_loaded[i], (use + 1) * 16)
                    if not (isinstance(use, int) and use == 0):
                        dve.wait_ge(o_stored[i], use * 16)
                    v.scalar_tensor_tensor(o_e[i], acc_e[i], rs_e[i][:, :], xb_e[i], ALU.mult, ALU.add
                                           ).then_inc(o_ready, 1)

            def b_iteration(m):
                seam = isinstance(m, int) and m == 0
                for k in range(RING):
                    buf = (k - 2) % RING
                    add_b2(RING * m + MOE[0] + k - 2, buf, True, m + ITERS_A + (0 if k == 2 else -1))
                    if not seam:
                        if k == 0:
                            mix([(m - 1, 0, m - 1)])
                            ready_slots(m, 0)
                        if k == 2:
                            emit([(m - 1, 0, m - 1)])

            ready_slots(0, 0)
            b_iteration(0)
            b_iteration(1)
            with dve.Fori(2, ITERS_B) as m:
                b_iteration(m)
            assert WAVE_TILES[0] == ITERS_B
            add_b2(MOE_ALL - 2, RING - 2, True, ITERS_A + ITERS_B - 1)
            add_b2(MOE_ALL - 1, RING - 1, True, ITERS_A + ITERS_B - 1)

            def pair_of(m, j, q):
                return [(E_FIRST + 2 * m + b, 2 * q + b, j + (E_FIRST if q == b == 0 else 0)) for b in range(2)]

            def e_pair(j, q, ahead):
                m = 2 * j + q
                mix(pair_of(m, j, q))
                if ahead:
                    for t, i, _ in pair_of(m + 2, j + 1, q):
                        ready_slots(t, i)
                if not (isinstance(m, int) and m == 0):
                    emit(pair_of(m - 1, j if q else j - 1, 1 - q))

            for i in range(1, E_BUFS):
                ready_slots(E_FIRST + i, i)
            for m in range(4):
                e_pair(m // 2, m % 2, True)
            with dve.Fori(2, E_PAIRS // 2 - 1) as j:
                for q in range(2):
                    e_pair(j, q, True)
            for q in range(2):
                e_pair(E_PAIRS // 2 - 1, q, False)
            emit(pair_of(E_PAIRS - 1, E_PAIRS // 2 - 1, 1))

        @block.tensor
        def _(pe):
            mm = nc.tensor.matmul

            def turn(dst_p, rows_, n):
                for k in range(2):
                    last = nc.tensor.transpose(dst_p[:, k * n:(k + 1) * n], rows_[:, k * P:(k + 1) * P],
                                               ident[0:n, 0:n])
                return last

            pe.wait_ge(pool_const, 1)

            def pe_turn(t, i):
                pe.wait_ge(xn_ready, t + 1)
                turn(bank[4 + i], xn[i], TILE).then_inc(xnT_done, 1)

            def pe_h(t, i, warm):
                pe.wait_ge(xnT_ready, t + 1)
                for j in range(4):
                    if isinstance(t, int) and t == 0:
                        pe.wait_ge(w_ready, j + 1)
                    if warm and j in (0, 2):
                        pe.wait_ge(h_out_act, 2 * t - 1 + j // 2)
                    if warm and j in (1, 3):
                        pe.wait_ge(h_out_dve, 2 * t - 1 + j // 2)
                    for k in range(2):
                        last = mm(bank[j][0:TILE, :], xnT[i][:, k, :],
                                  w_rel[:, k, 2 * j:2 * j + 2, :].rearrange("p r o -> p (r o)"),
                                  start=(k == 0), stop=(k == 1))
                    last.then_inc(h_done, 1)

            def turn_edges(k):
                field, at = divmod(k, 2)
                if k == 0:
                    pe.wait_ge(edges_built, 1)
                if k >= 2:
                    pe.wait_ge(edges_copied, k - 1)
                for g in range(at * TURNED, TURNED if at == 0 else GROUPS):
                    last = nc.tensor.transpose(bank[6 + k % 2][:, g % TURNED * P:(g % TURNED + 1) * P],
                                               (idx_f, dst_f, nrm)[field][:, g, :], ident[:, :])
                last.then_inc(edges_turned, 1)

            pe_turn(0, 0)
            for t in range(TILES):
                if t == B_FROM:
                    with pe.Fori(B_FROM // 2, TILES // 2 - 1) as m:
                        for i in range(2):
                            pe_turn(2 * m + i + 1, 1 - i)
                            pe_h(2 * m + i, i, True)
                if t < B_FROM or t >= TILES - 2:
                    if t + 1 < TILES:
                        pe_turn(t + 1, (t + 1) % 2)
                    if TURN_FROM <= t < TURN_FROM + 6:
                        turn_edges(t - TURN_FROM)
                    if t == ENDS_AT:
                        pe.wait_ge(ends_ready, 1)
                        pe.wait_ge(edges_copied, 5)
                        nc.tensor.transpose(bank[6][0:2 * TILES, 0:P], ends[:, :], ident[:, :]).then_inc(ends_turned, 1)
                    if t == ENDS_AT + 1:
                        pe.wait_ge(ends_max, 1)
                        nc.tensor.transpose(bank[7][0:1, 0:2 * TILES], ends1[:, :], ident[0:2 * TILES, 0:2 * TILES]
                                            ).then_inc(ends_back, 1)
                    pe_h(t, t % 2, t >= 1)

            for p in range(ROUNDS):
                pe.nop(nofuse=True).then_inc(round_free[p], 1)
            for b in range(2):
                pe.nop(nofuse=True).then_inc(rest_free[b], 1)
            pe.nop(nofuse=True).then_inc(seam_free, 1)
            pe.wait_ge(zeros_set, 1)
            pe.wait_ge(const_loaded, 96)
            pe.wait_ge(ranges_ready, 1)
            pe.wait_ge(h_out_act, 2 * TILES)
            pe.wait_ge(h_out_dve, 2 * TILES)
            rest = pe.alloc_register("rest_pe")
            pe.reg_mov(rest, 0)

            def sum_round(t, p, sums):
                pe.wait_ge(hot_ready[p], t + 1)
                for c in range(CHUNKS[p]):
                    pe.wait_ge(gathered[p][c], (t + 1) * 16)
                    last = mm(sums, hot[p][:, c, :], rows[p][c][:, :], start=False, stop=False)
                last.then_inc(round_free[p], 1)

            def sum_rest(b, u1, sums):
                pe.wait_ge(rest_hot[b], u1)
                pe.wait_ge(rest_gathered[b], u1 * 16)
                mm(sums, hot_r[b][:, :], rows_r[b][:, :], start=False, stop=False).then_inc(rest_free[b], 1)

            def turn2(t):
                pe.wait_ge(xn2_ready, t + 1)
                turn(finish_p, pair[:, 1, :], TILE).then_inc(x2T_done, 1)

            def logits(t):
                pe.wait_ge(x2T_ready, t + 1)
                for k in range(2):
                    mm(finish_p[0:TILE, LOGITS_AT:LOGITS_AT + EXPERTS], xn2T[:, k, :], gw[:, k, :], start=(k == 0), stop=False)
                mm(finish_p[0:TILE, LOGITS_AT:LOGITS_AT + EXPERTS], row0[:, 0:TILE], gb[:, :], start=False, stop=True).then_inc(logits_done, 1)

            def rank(t, w):
                pe.wait_ge(both_ready, t + 1)
                mm(finish_p[0:TILE, RANK_AT:RANK_AT + EXPERTS], ones[:, 0:TILE], seen[w][:, :], start=True, stop=False)
                mm(finish_p[0:TILE, RANK_AT:RANK_AT + EXPERTS], before[:, 0:TILE], both[:, :], start=False, stop=True
                   ).then_inc(rank_done, 1)

            def count(w):
                pe.wait_ge(slots_ready, WAVE_START[w] + WAVE_TILES[w])
                mm(finish_p[0:TILE, COUNT_AT:COUNT_AT + EXPERTS], ones[:, 0:TILE], seen[w][:, :],
                   start=True, stop=True).then_inc(count_done, 1)

            def turn_rows(i, k, use):
                pe.wait_ge(xd_loaded[k], (use + 1) * 16)
                if not (isinstance(i, int) and i == 0):
                    pe.wait_ge(xdT_ready, i)
                turn(xdT_p, xd[k], P).then_inc(xdT_done, 1)

            def up(i, k, use):
                pe.wait_ge(xdT_ready, i + 1)
                pe.wait_ge(w1_loaded[k], (use + 1) * 16)
                for f in range(4):
                    for kk in range(2):
                        last = mm(h_p[k][:, f * P:(f + 1) * P], w1_s[k][:, kk * FF + f * P:kk * FF + (f + 1) * P],
                                  xdT[k][:, kk, :], start=(kk == 0), stop=(kk == 1))
                last.then_inc(mm1_done, 1)

            def down(i, k, use):
                pe.wait_ge(hT_ready, i + 1)
                pe.wait_ge(w2_loaded[k], (use + 1) * 16)
                if not (isinstance(i, int) and i == 0):
                    pe.wait_ge(yo_ready, i)
                for f in range(4):
                    last = mm(y_p[:, 0:D], hT[k][:, f, :], w2_s[k][:, f * D:(f + 1) * D],
                              start=(f == 0), stop=(f == 3))
                last.then_inc(mm2_done, 1)

            def step_front(m, k):
                s = RING * m + k
                turn_rows(s, k, m)
                if not (isinstance(s, int) and s < 1):
                    up(s - 1, (k - 1) % RING, m if k else m - 1)

            def step_back(m, k):
                s = RING * m + k
                if not (isinstance(s, int) and s < 2):
                    down(s - 2, (k - 2) % RING, m if k == 2 else m - 1)

            def pe_tile(t, w1, w2, m, warm):
                sums = sums_of(pe, t)
                pe.wait_ge(xTc_loaded, (t + 1) * 16)
                if not (isinstance(t, int) and t < 2):
                    pe.wait_ge(agg_read, t - 1)
                for k in range(2):
                    last = mm(sums, xT_c[:, k * TILE:(k + 1) * TILE], lw[:, k, :],
                              start=(k == 0), stop=False)
                last.then_inc(agg_open, 1)

                def between(p):
                    if m is not None:
                        if p in (0, 2, 4):
                            step_front(m, p // 2)
                        if p in (1, 3, 5):
                            step_back(m, p // 2)
                    if w1 is not None:
                        if p == 3:
                            if isinstance(t, int) and t == WAVE_START[1] + 1:
                                pe.wait_ge(region_ends, 1)
                            turn2(t - 1)
                        if p == 4:
                            logits(t - 1)
                        if p == 6:
                            rank(t - 1, w1)
                    if p == 0 and isinstance(t, int) and t == WAVE_START[1] + 1:
                        count(0)

                for p in range(ROUNDS):
                    sum_round(t, p, sums)
                    between(p)
                rest_chunks(pe, rest, t, lambda b, u1: sum_rest(b, u1, sums))
                if not last_tile(t):
                    pe.wait_ge(seam_hot, t + 1)
                    pe.wait_ge(gathered[0][0], (t + 2) * 16)
                    mm(sums, hot_m[:, :], rows[0][0][:, :], start=False, stop=False).then_inc(seam_free, 1)
                mm(sums, row0[:, 0:TILE], hb[:, :], start=False, stop=True).then_inc(agg_done, 1)

            all_tiles(pe, pe_tile)
            turn2(TILES - 1)
            logits(TILES - 1)
            rank(TILES - 1, 1)
            count(1)
            with pe.Fori(ITERS_A, ITERS_A + ITERS_B) as m:
                for k in range(RING):
                    step_front(m, k)
                    step_back(m, k)
            up(MOE_ALL - 1, RING - 1, ITERS_A + ITERS_B - 1)
            down(MOE_ALL - 2, RING - 2, ITERS_A + ITERS_B - 1)
            down(MOE_ALL - 1, RING - 1, ITERS_A + ITERS_B - 1)


def kernel(x, src, dst, edge_type_8, edge_weight1, L0_gnn_weight, L0_gnn_w_comp, L0_gnn_loop_weight, L0_gnn_h_bias,
           L0_ffn_gate_w, L0_ffn_gate_b, L0_ffn_w1, L0_ffn_b1, L0_ffn_w2, L0_ffn_b2, L0_ffn_gamma, L0_ffn_beta):
    import numpy as np
    import concourse.bacc as bacc
    from concourse.bass_utils import run_bass_kernel_spmd

    def rows(a, parts):
        a = np.asarray(a)
        return a.reshape(EXPERTS, parts, P, -1).transpose(0, 2, 1, 3).reshape(EXPERTS, P, -1)

    b2_rows = np.broadcast_to(np.asarray(L0_ffn_b2)[:, None, :], (EXPERTS, P, D))
    w1_cat = np.concatenate([rows(L0_ffn_w1, 2), rows(L0_ffn_b1, 4)], axis=2).reshape(EXPERTS * P, W1_COLS)
    w2_cat = np.concatenate([rows(L0_ffn_w2, 4), b2_rows], axis=2).reshape(EXPERTS * P, W2_COLS)
    arrays = {
        "x_in": x, "src_in": src, "dst_in": dst, "etype_in": edge_type_8,
        "eweight_in": np.asarray(edge_weight1).reshape(N_EDGES), "basis_in": L0_gnn_weight, "comp_in": L0_gnn_w_comp,
        "loop_in": L0_gnn_loop_weight, "hbias_in": L0_gnn_h_bias, "gatew_in": L0_ffn_gate_w, "gateb_in": L0_ffn_gate_b,
        "w1_in": w1_cat, "w2_in": w2_cat, "gamma_in": L0_ffn_gamma,
        "beta_in": L0_ffn_beta,
    }
    arrays = {k: np.ascontiguousarray(np.asarray(a)) for k, a in arrays.items()}
    nc = bacc.Bacc("TRN2", target_bir_lowering=False, num_devices=1)
    args = [nc.dram_tensor(k, a.shape, mybir.dt.from_np(a.dtype), kind="ExternalInput").ap() for k, a in arrays.items()]
    out = nc.dram_tensor("out_x", (N_NODES, D), F32, kind="ExternalOutput").ap()
    build(nc, *args, out)
    r = run_bass_kernel_spmd(nc, [arrays], core_ids=[0])
    return r.results[0]["out_x"]
```
